# Optimizing a Trainium2 kernel written in Bass

```python
import numpy as np
import jax
import jax.numpy as jnp

def _softmax(x, axis=-1):
    return jax.nn.softmax(x, axis=axis)

def _gelu(x):
    return jax.nn.gelu(x, approximate=True)

def _silu(x):
    return jax.nn.silu(x)

def _sigmoid(x):
    return jax.nn.sigmoid(x)

def _layernorm(x, axis=-1, eps=1e-05):
    m = jnp.mean(x, axis=axis, keepdims=True)
    v = jnp.var(x, axis=axis, keepdims=True)
    return (x - m) / jnp.sqrt(v + eps)

def _scatter_add(tgt, idx, src, axis=0):
    return tgt.at[idx].add(src)

def _segment_sum(src, seg, n):
    return jax.ops.segment_sum(src, seg, n)
kernel_name = 'mk_xattn_seq_d2_seqx_r8_7bf2e2'

def setup_inputs(seed: int=0):
    np.random.seed(seed)
    _w = jnp.asarray

    def _rec_inputs():
        import jax
        import jax.numpy as jnp
        _rk = jax.random.key(seed)
        x = -0.0001548 + 1 * jax.random.normal(jax.random.fold_in(_rk, 1), (4, 512, 160), jnp.float32)
        _lenS = 512 - jax.random.randint(jax.random.fold_in(_rk, 7), (4,), 0, max(1, 512 // 4) + 1, jnp.int32)
        _lenS2 = 77 - jax.random.randint(jax.random.fold_in(_rk, 8), (4,), 0, max(1, 77 // 4) + 1, jnp.int32)
        _ctx_768P = jax.random.normal(jax.random.fold_in(_rk, 11), (4, 16, 96), jnp.float32)
        _ctx_768c = jax.random.dirichlet(jax.random.fold_in(_rk, 511), 0.3 * jnp.ones((16,), jnp.float32), (4, 77))
        _ctx_768t = jnp.einsum('bsk,bkd->bsd', _ctx_768c, _ctx_768P)
        _ctx_768t = _ctx_768t * jax.lax.rsqrt(jnp.mean(jnp.square(_ctx_768t)) + 1e-12) * 0.953939
        ctx_768 = 0.00141353 + 0.998943 * (_ctx_768t + 0.3 * jax.random.normal(jax.random.fold_in(_rk, 611), (4, 77, 96), jnp.float32))
        return (x, ctx_768)
    x, ctx_768 = _rec_inputs()

    def _L0_xattn_setup():
        import jax, jax.numpy as jnp
        import numpy as np
        HEADS = 8
        NUM_TOKENS = 4
        CROSS_ATTENTION_DIM = 96

        def _mha(q, k, v, heads=HEADS):
            B, Sq, H = q.shape
            Sk = k.shape[1]
            d = H // heads
            qh = q.reshape(B, Sq, heads, d).transpose(0, 2, 1, 3)
            kh = k.reshape(B, Sk, heads, d).transpose(0, 2, 1, 3)
            vh = v.reshape(B, Sk, heads, d).transpose(0, 2, 1, 3)
            scores = jnp.einsum('bhqd,bhkd->bhqk', qh, kh) * jnp.asarray(d, q.dtype) ** (-0.5)
            probs = jax.nn.softmax(scores, axis=-1)
            out = jnp.einsum('bhqk,bhkd->bhqd', probs, vh)
            return out.transpose(0, 2, 1, 3).reshape(B, Sq, H)
        key = jax.random.key(seed)
        ks = jax.random.split(key, 10)
        B, S, H, CAD, T = (4, 128, 160, CROSS_ATTENTION_DIM, NUM_TOKENS)
        sc = 0.02
        return {'hidden_states': jax.random.normal(ks[0], (B, S, H), jnp.float32), 'encoder_hidden_states': jax.random.normal(ks[1], (B, 77 + T, CAD), jnp.float32), 'Wq': jax.random.normal(ks[2], (H, H), jnp.float32) * sc, 'Wk': jax.random.normal(ks[3], (CAD, H), jnp.float32) * sc, 'Wv': jax.random.normal(ks[4], (CAD, H), jnp.float32) * sc, 'Wq_ca': jax.random.normal(ks[5], (T, H), jnp.float32) * sc, 'Wk_ca': jax.random.normal(ks[6], (CAD, H), jnp.float32) * sc, 'Wv_ca': jax.random.normal(ks[7], (CAD, H), jnp.float32) * sc, 'Wout': jax.random.normal(ks[8], (H, H), jnp.float32) * sc, 'b_out': jnp.zeros((H,), jnp.float32)}
    _L0_xattn_all = _L0_xattn_setup()
    _L0_xattn_in = {k: v for k, v in _L0_xattn_all.items() if k in ('Wq', 'Wk', 'Wv', 'Wq_ca', 'Wk_ca', 'Wv_ca', 'Wout', 'b_out')}
    del _L0_xattn_all

    def _L1_xattn_setup():
        import jax, jax.numpy as jnp
        import numpy as np
        DIM, HEADS, DHEAD, CTX_DIM, DFF = (160, 20, 64, 96, 640)
        EPS = 1e-05
        SCALE = DHEAD ** (-0.5)

        def layer_norm(x, g, b):
            mu = jnp.mean(x, axis=-1, keepdims=True)
            var = jnp.mean(jnp.square(x - mu), axis=-1, keepdims=True)
            return (x - mu) * jax.lax.rsqrt(var + EPS) * g + b

        def cross_attention(x, ctx, wq, wk, wv, wo, bo):
            B, N, _ = x.shape
            M = ctx.shape[1]
            q = jnp.einsum('bne,ef->bnf', x, wq).reshape(B, N, HEADS, DHEAD).transpose(0, 2, 1, 3)
            k = jnp.einsum('bme,ef->bmf', ctx, wk).reshape(B, M, HEADS, DHEAD).transpose(0, 2, 1, 3)
            v = jnp.einsum('bme,ef->bmf', ctx, wv).reshape(B, M, HEADS, DHEAD).transpose(0, 2, 1, 3)
            scores = jnp.einsum('bhnd,bhmd->bhnm', q, k) * SCALE
            attn = jax.nn.softmax(scores, axis=-1)
            out = jnp.einsum('bhnm,bhmd->bhnd', attn, v)
            out = out.transpose(0, 2, 1, 3).reshape(B, N, HEADS * DHEAD)
            return jnp.einsum('bnf,fe->bne', out, wo) + bo

        def geglu_ff(x, w1, b1, w2, b2):
            h = jnp.einsum('bne,ef->bnf', x, w1) + b1
            a, gate = (h[..., :DFF], h[..., DFF:])
            h = a * jax.nn.gelu(gate)
            return jnp.einsum('bnf,fe->bne', h, w2) + b2

        def block_forward(x, context, g1, be1, wq1, wk1, wv1, wo1, bo1, g2, be2, wq2, wk2, wv2, wo2, bo2, g3, be3, w_ff1, b_ff1, w_ff2, b_ff2):
            x = cross_attention(layer_norm(x, g1, be1), layer_norm(x, g1, be1), wq1, wk1, wv1, wo1, bo1) + x
            x = cross_attention(layer_norm(x, g2, be2), context, wq2, wk2, wv2, wo2, bo2) + x
            return geglu_ff(layer_norm(x, g3, be3), w_ff1, b_ff1, w_ff2, b_ff2) + x
        key = jax.random.key(seed)
        ks = jax.random.split(key, 20)
        s = 0.02
        inner = HEADS * DHEAD
        return {'x': jax.random.normal(ks[0], (4, 128, DIM), jnp.float32), 'context': jax.random.normal(ks[1], (4, 77, CTX_DIM), jnp.float32), 'g1': jnp.ones((DIM,), jnp.float32), 'be1': jnp.zeros((DIM,), jnp.float32), 'wq1': jax.random.normal(ks[2], (DIM, inner), jnp.float32) * s, 'wk1': jax.random.normal(ks[3], (DIM, inner), jnp.float32) * s, 'wv1': jax.random.normal(ks[4], (DIM, inner), jnp.float32) * s, 'wo1': jax.random.normal(ks[5], (inner, DIM), jnp.float32) * s, 'bo1': jnp.zeros((DIM,), jnp.float32), 'g2': jnp.ones((DIM,), jnp.float32), 'be2': jnp.zeros((DIM,), jnp.float32), 'wq2': jax.random.normal(ks[6], (DIM, inner), jnp.float32) * s, 'wk2': jax.random.normal(ks[7], (CTX_DIM, inner), jnp.float32) * s, 'wv2': jax.random.normal(ks[8], (CTX_DIM, inner), jnp.float32) * s, 'wo2': jax.random.normal(ks[9], (inner, DIM), jnp.float32) * s, 'bo2': jnp.zeros((DIM,), jnp.float32), 'g3': jnp.ones((DIM,), jnp.float32), 'be3': jnp.zeros((DIM,), jnp.float32), 'w_ff1': jax.random.normal(ks[10], (DIM, 2 * DFF), jnp.float32) * s, 'b_ff1': jnp.zeros((2 * DFF,), jnp.float32), 'w_ff2': jax.random.normal(ks[11], (DFF, DIM), jnp.float32) * s, 'b_ff2': jnp.zeros((DIM,), jnp.float32)}
    _L1_xattn_all = _L1_xattn_setup()
    _L1_xattn_in = {k: v for k, v in _L1_xattn_all.items() if k in ('g1', 'be1', 'wq1', 'wk1', 'wv1', 'wo1', 'bo1', 'g2', 'be2', 'wq2', 'wk2', 'wv2', 'wo2', 'bo2', 'g3', 'be3', 'w_ff1', 'b_ff1', 'w_ff2', 'b_ff2')}
    del _L1_xattn_all
    return {'x': x, 'ctx_768': ctx_768, 'L0_xattn_Wq': _L0_xattn_in['Wq'], 'L0_xattn_Wk': _L0_xattn_in['Wk'], 'L0_xattn_Wv': _L0_xattn_in['Wv'], 'L0_xattn_Wq_ca': _L0_xattn_in['Wq_ca'], 'L0_xattn_Wk_ca': _L0_xattn_in['Wk_ca'], 'L0_xattn_Wv_ca': _L0_xattn_in['Wv_ca'], 'L0_xattn_Wout': _L0_xattn_in['Wout'], 'L0_xattn_b_out': _L0_xattn_in['b_out'], 'L1_xattn_g1': _L1_xattn_in['g1'], 'L1_xattn_be1': _L1_xattn_in['be1'], 'L1_xattn_wq1': _L1_xattn_in['wq1'], 'L1_xattn_wk1': _L1_xattn_in['wk1'], 'L1_xattn_wv1': _L1_xattn_in['wv1'], 'L1_xattn_wo1': _L1_xattn_in['wo1'], 'L1_xattn_bo1': _L1_xattn_in['bo1'], 'L1_xattn_g2': _L1_xattn_in['g2'], 'L1_xattn_be2': _L1_xattn_in['be2'], 'L1_xattn_wq2': _L1_xattn_in['wq2'], 'L1_xattn_wk2': _L1_xattn_in['wk2'], 'L1_xattn_wv2': _L1_xattn_in['wv2'], 'L1_xattn_wo2': _L1_xattn_in['wo2'], 'L1_xattn_bo2': _L1_xattn_in['bo2'], 'L1_xattn_g3': _L1_xattn_in['g3'], 'L1_xattn_be3': _L1_xattn_in['be3'], 'L1_xattn_w_ff1': _L1_xattn_in['w_ff1'], 'L1_xattn_b_ff1': _L1_xattn_in['b_ff1'], 'L1_xattn_w_ff2': _L1_xattn_in['w_ff2'], 'L1_xattn_b_ff2': _L1_xattn_in['b_ff2']}

def reference(x, ctx_768, L0_xattn_Wq, L0_xattn_Wk, L0_xattn_Wv, L0_xattn_Wq_ca, L0_xattn_Wk_ca, L0_xattn_Wv_ca, L0_xattn_Wout, L0_xattn_b_out, L1_xattn_g1, L1_xattn_be1, L1_xattn_wq1, L1_xattn_wk1, L1_xattn_wv1, L1_xattn_wo1, L1_xattn_bo1, L1_xattn_g2, L1_xattn_be2, L1_xattn_wq2, L1_xattn_wk2, L1_xattn_wv2, L1_xattn_wo2, L1_xattn_bo2, L1_xattn_g3, L1_xattn_be3, L1_xattn_w_ff1, L1_xattn_b_ff1, L1_xattn_w_ff2, L1_xattn_b_ff2):
    import jax
    import jax.numpy as jnp

    def _L0_xattn_ref(hidden_states, encoder_hidden_states, Wq, Wk, Wv, Wq_ca, Wk_ca, Wv_ca, Wout, b_out):
        import jax, jax.numpy as jnp
        import numpy as np
        HEADS = 8
        NUM_TOKENS = 4
        CROSS_ATTENTION_DIM = 96

        def _mha(q, k, v, heads=HEADS):
            B, Sq, H = q.shape
            Sk = k.shape[1]
            d = H // heads
            qh = q.reshape(B, Sq, heads, d).transpose(0, 2, 1, 3)
            kh = k.reshape(B, Sk, heads, d).transpose(0, 2, 1, 3)
            vh = v.reshape(B, Sk, heads, d).transpose(0, 2, 1, 3)
            scores = jnp.einsum('bhqd,bhkd->bhqk', qh, kh) * jnp.asarray(d, q.dtype) ** (-0.5)
            probs = jax.nn.softmax(scores, axis=-1)
            out = jnp.einsum('bhqk,bhkd->bhqd', probs, vh)
            return out.transpose(0, 2, 1, 3).reshape(B, Sq, H)
        residual = hidden_states
        unet_size = residual.shape[1]
        end_pos = encoder_hidden_states.shape[1] - NUM_TOKENS
        enc = encoder_hidden_states[:, :end_pos, :]
        ca = encoder_hidden_states[:, end_pos:, :]
        query = hidden_states @ Wq
        keyt = enc @ Wk
        valt = enc @ Wv
        hs = _mha(query, keyt, valt)
        ca_q1 = jnp.einsum('btc,th->bch', ca, Wq_ca)
        indices = np.linspace(0, CROSS_ATTENTION_DIM - 1, unet_size).astype(np.int64)
        ca_q1 = ca_q1[:, indices, :]
        ca_hs1 = _mha(ca_q1, residual, residual)
        ca_q2 = ca_hs1 @ Wq
        ca_k2 = ca @ Wk_ca
        ca_v2 = ca @ Wv_ca
        ca_hs2 = _mha(ca_q2, ca_k2, ca_v2)
        out = hs + ca_hs2
        out = out @ Wout + b_out
        out = out + residual
        return out

    def _L1_xattn_ref(x, context, g1, be1, wq1, wk1, wv1, wo1, bo1, g2, be2, wq2, wk2, wv2, wo2, bo2, g3, be3, w_ff1, b_ff1, w_ff2, b_ff2):
        import jax, jax.numpy as jnp
        import numpy as np
        DIM, HEADS, DHEAD, CTX_DIM, DFF = (160, 20, 64, 96, 640)
        EPS = 1e-05
        SCALE = DHEAD ** (-0.5)

        def layer_norm(x, g, b):
            mu = jnp.mean(x, axis=-1, keepdims=True)
            var = jnp.mean(jnp.square(x - mu), axis=-1, keepdims=True)
            return (x - mu) * jax.lax.rsqrt(var + EPS) * g + b

        def cross_attention(x, ctx, wq, wk, wv, wo, bo):
            B, N, _ = x.shape
            M = ctx.shape[1]
            q = jnp.einsum('bne,ef->bnf', x, wq).reshape(B, N, HEADS, DHEAD).transpose(0, 2, 1, 3)
            k = jnp.einsum('bme,ef->bmf', ctx, wk).reshape(B, M, HEADS, DHEAD).transpose(0, 2, 1, 3)
            v = jnp.einsum('bme,ef->bmf', ctx, wv).reshape(B, M, HEADS, DHEAD).transpose(0, 2, 1, 3)
            scores = jnp.einsum('bhnd,bhmd->bhnm', q, k) * SCALE
            attn = jax.nn.softmax(scores, axis=-1)
            out = jnp.einsum('bhnm,bhmd->bhnd', attn, v)
            out = out.transpose(0, 2, 1, 3).reshape(B, N, HEADS * DHEAD)
            return jnp.einsum('bnf,fe->bne', out, wo) + bo

        def geglu_ff(x, w1, b1, w2, b2):
            h = jnp.einsum('bne,ef->bnf', x, w1) + b1
            a, gate = (h[..., :DFF], h[..., DFF:])
            h = a * jax.nn.gelu(gate)
            return jnp.einsum('bnf,fe->bne', h, w2) + b2

        def block_forward(x, context, g1, be1, wq1, wk1, wv1, wo1, bo1, g2, be2, wq2, wk2, wv2, wo2, bo2, g3, be3, w_ff1, b_ff1, w_ff2, b_ff2):
            x = cross_attention(layer_norm(x, g1, be1), layer_norm(x, g1, be1), wq1, wk1, wv1, wo1, bo1) + x
            x = cross_attention(layer_norm(x, g2, be2), context, wq2, wk2, wv2, wo2, bo2) + x
            return geglu_ff(layer_norm(x, g3, be3), w_ff1, b_ff1, w_ff2, b_ff2) + x
        return block_forward(x, context, g1, be1, wq1, wk1, wv1, wo1, bo1, g2, be2, wq2, wk2, wv2, wo2, bo2, g3, be3, w_ff1, b_ff1, w_ff2, b_ff2)
    x = _L0_xattn_ref(x, ctx_768, L0_xattn_Wq, L0_xattn_Wk, L0_xattn_Wv, L0_xattn_Wq_ca, L0_xattn_Wk_ca, L0_xattn_Wv_ca, L0_xattn_Wout, L0_xattn_b_out)
    x = _L1_xattn_ref(x, ctx_768, L1_xattn_g1, L1_xattn_be1, L1_xattn_wq1, L1_xattn_wk1, L1_xattn_wv1, L1_xattn_wo1, L1_xattn_bo1, L1_xattn_g2, L1_xattn_be2, L1_xattn_wq2, L1_xattn_wk2, L1_xattn_wv2, L1_xattn_wo2, L1_xattn_bo2, L1_xattn_g3, L1_xattn_be3, L1_xattn_w_ff1, L1_xattn_b_ff1, L1_xattn_w_ff2, L1_xattn_b_ff2)
    return x

_drawn_inputs = setup_inputs


def setup_inputs(seed=0):
    import zlib

    import numpy as np

    out = dict(_drawn_inputs(seed))
    spreads = {'L0_xattn_b_out': (0.0, 0.1),
     'L1_xattn_g1': (1.0, 0.6),
     'L1_xattn_be1': (0.0, 0.376),
     'L1_xattn_bo1': (0.0, 0.1),
     'L1_xattn_g2': (1.0, 0.6),
     'L1_xattn_be2': (0.0, 0.8),
     'L1_xattn_bo2': (0.0, 0.1),
     'L1_xattn_g3': (1.0, 0.6),
     'L1_xattn_be3': (0.0, 0.8),
     'L1_xattn_b_ff1': (0.0, 0.8),
     'L1_xattn_b_ff2': (0.0, 0.1)}
    factors = {'L0_xattn_Wq': 8.0,
     'L0_xattn_Wk': 8.0,
     'L0_xattn_Wq_ca': 64.0,
     'L0_xattn_Wk_ca': 64.0,
     'L1_xattn_wq1': 8.0,
     'L1_xattn_wk1': 8.0,
     'L1_xattn_wq2': 8.0,
     'L1_xattn_wk2': 8.0}
    for name, (base, spread) in spreads.items():
        noise = np.random.default_rng([zlib.crc32(name.encode()), seed]).standard_normal(out[name].shape)
        drawn = base * np.exp(spread * noise) if base else spread * noise
        out[name] = jnp.asarray(drawn.astype(out[name].dtype))
    for name, factor in factors.items():
        out[name] = (out[name] * factor).astype(out[name].dtype)
    return out
```

```python
from contextlib import ExitStack

import numpy as np

import concourse.bass as bass
from concourse import mybir

F32 = mybir.dt.float32
F32R = mybir.dt.float32r
ALU = mybir.AluOpType
ACT = mybir.ActivationFunctionType
AX_X = mybir.AxisListType.X

B, S, D = 4, 512, 160
P = 128
QT = S // P
DT = D - P
SK, CTX = 77, 96
NCA = 4
SE = SK - NCA
H0, HD0, HP = 8, 20, 32
G = H0 * HP // P
HG = H0 // G
H1, HD = 20, 64
INNER = H1 * HD
NPAIR = H1 // 2
DFF = 640
NF = DFF // P
EPS = 1e-5
SCALE0 = float(HD0) ** -0.5
SCALE1 = float(HD) ** -0.5


class Signal:

    def __init__(self, ctx, nc, name, per, credit=0, step=1):
        self.sem = ctx.enter_context(nc.semaphore(name))
        self.per, self.credit, self.step = per, credit, step

    def at(self, b, k):
        return (b * self.per + (k + 1) + self.credit) * self.step


def over_batches(eng, body, peel=True):
    if not peel:
        with eng.Fori(0, B) as b:
            body(b, False)
        return
    with eng.Fori(0, B - 1) as b:
        body(b, True)
    body(B - 1, False)


class Norm:

    def __init__(self, ctx, nc, name, x, hat, hi, lo, tail, full, full_tail, gain, shift, banks):
        self.nc, self.x, self.hat = nc, x, hat
        self.hi, self.lo, self.tail = hi, lo, tail
        self.full, self.full_tail, self.gain, self.shift = full, full_tail, gain, shift
        self.banks = banks
        sb = lambda n, s: ctx.enter_context(nc.sbuf_tensor(name + n, s, F32))
        self.stats = sb("stats", [P, QT, 6])
        self.moments = sb("moments", [P, QT, 2])
        self.veps = sb("veps", [P, QT])
        self.half = sb("half", [P, QT])
        self.eps = sb("eps", [P, QT])
        self.rstd = sb("rstd", [P, QT])
        sig = lambda n, per, credit=0: Signal(ctx, nc, name + n, per, credit)
        self.s_stats = sig("stats_made", QT)
        self.s_noted = ctx.enter_context(nc.semaphore(name + "stats_noted"))
        self.s_moments = sig("moments_made", QT)
        self.s_half = sig("constants_set", 2)
        self.s_veps = sig("veps_made", 1)
        self.s_rstd = sig("rstd_made", 1)
        self.s_hat = sig("hat_made", QT)
        self.s_turned = sig("turned", 2, 2)
        self.s_full = sig("full_made", 2, 2)
        self.s_hi = sig("hi_made", 3, 3)
        self.s_lo = sig("lo_made", 2, 2)

    def start_gpsimd(self, pool):
        pool.memset(self.half[:], -0.5).then_inc(self.s_half.sem, 1)
        pool.memset(self.eps[:], EPS).then_inc(self.s_half.sem, 1)
        pool.wait_ge(self.s_half.sem, 2)

    def start_tensor(self, pe):
        pe.sem_inc(self.s_turned.sem, 2)

    def start_scalar(self, act):
        act.sem_inc(self.s_full.sem, 2)
        act.sem_inc(self.s_hi.sem, 3)

    def start_vector(self, dve):
        dve.sem_inc(self.s_lo.sem, 2)

    def statistics(self, dve, b):
        for q in range(QT):
            dve.bn_stats(self.stats[:, q, :], self.x[:, bass.ds(b * QT + q, 1), :].rearrange("p a d -> p (a d)")).then_inc(self.s_stats.sem, 1)
        dve.wait_ge(self.s_stats.sem, self.s_stats.at(b, QT - 1))
        dve.sem_inc(self.s_noted, 1)
        for q in range(QT):
            dve.bn_aggr(self.moments[:, q, :], self.stats[:, q, :]).then_inc(self.s_moments.sem, 1)

    def deviations(self, pool, b):
        pool.wait_ge(self.s_moments.sem, self.s_moments.at(b, QT - 1))
        pool.tensor_tensor(self.veps[:], self.moments[:, :, 1], self.eps[:], ALU.add).then_inc(self.s_veps.sem, 1)
        pool.wait_ge(self.s_veps.sem, self.s_veps.at(b, 0))
        pool.tensor_tensor(self.rstd[:], self.veps[:], self.half[:], ALU.pow).then_inc(self.s_rstd.sem, 1)

    def standardize(self, dve, b):
        dve.wait_ge(self.s_rstd.sem, self.s_rstd.at(b, 0))
        dve.wait_ge(self.s_turned.sem, self.s_turned.at(b, -1))
        for q in range(QT):
            dve.tensor_scalar(self.hat[:, q, :], self.x[:, bass.ds(b * QT + q, 1), :].rearrange("p a d -> p (a d)"),
                              self.moments[:, q, 0:1], self.rstd[:, q:q + 1], ALU.subtract, ALU.mult).then_inc(self.s_hat.sem, 1)

    def turn(self, pe, b, ident, bank_free):
        pe.wait_ge(self.s_hat.sem, self.s_hat.at(b, QT - 1))
        bank_free(0)
        for q in range(QT):
            last = pe.transpose(self.banks[0][:, q * P:(q + 1) * P], self.hat[:, q, 0:P], ident[:])
        last.then_inc(self.s_turned.sem, 1)
        bank_free(1)
        for q in range(QT):
            last = pe.transpose(self.banks[1][0:DT, q * P:(q + 1) * P], self.hat[:, q, P:D], ident[:])
        last.then_inc(self.s_turned.sem, 1)

    def scale_and_round(self, act, b, operands_free):
        act.wait_ge(self.s_turned.sem, self.s_turned.at(b, 0))
        act.wait_ge(self.s_lo.sem, self.s_lo.at(b, -1))
        act.wait_ge(self.s_hi.sem, self.s_hi.at(b, -1))
        act.activation(self.full[:], self.banks[0], ACT.Identity, bias=self.shift[:, 0:1], scale=self.gain[:, 0:1]).then_inc(self.s_full.sem, 1)
        act.wait_ge(self.s_turned.sem, self.s_turned.at(b, 1))
        act.activation(self.full_tail[:], self.banks[1][0:DT, :], ACT.Identity, bias=self.shift[0:DT, 1:2], scale=self.gain[0:DT, 1:2]).then_inc(self.s_full.sem, 1)
        operands_free(act)
        act.wait_ge(self.s_full.sem, self.s_full.at(b, 0))
        act.copy(self.hi[:], self.full[:]).then_inc(self.s_hi.sem, 1)
        act.wait_ge(self.s_full.sem, self.s_full.at(b, 1))
        act.copy(self.tail[0:DT, :], self.full_tail[:]).then_inc(self.s_hi.sem, 1)
        act.copy(self.tail[2 * DT:3 * DT, :], self.full_tail[:]).then_inc(self.s_hi.sem, 1)

    def remainder(self, dve, b, operands_free):
        operands_free(dve)
        dve.wait_ge(self.s_hi.sem, self.s_hi.at(b, 0))
        dve.tensor_tensor(self.lo[:], self.full[:], self.hi[:].bitcast(F32), ALU.subtract).then_inc(self.s_lo.sem, 1)
        dve.wait_ge(self.s_hi.sem, self.s_hi.at(b, 1))
        dve.tensor_tensor(self.tail[DT:2 * DT, :], self.full_tail[:], self.tail[0:DT, :].bitcast(F32), ALU.subtract).then_inc(self.s_lo.sem, 1)

    def ready(self, pe, b):
        pe.wait_ge(self.s_hi.sem, self.s_hi.at(b, 2))
        pe.wait_ge(self.s_lo.sem, self.s_lo.at(b, 1))

    def project(self, pe, bank, w, c0, n=P):
        c = slice(c0, c0 + n)
        pe.matmul(bank, w.hi[:, c], self.hi[:], start=True, stop=False)
        pe.matmul(bank, w.hi[:, c], self.lo[:], start=False, stop=False)
        pe.matmul(bank, w.lo[:, c], self.hi[:], start=False, stop=False)
        return pe.matmul(bank, w.tail[:, c], self.tail[:], start=False, stop=True)

    def project_tokens(self, pe, bank, w, c0, q, n=P):
        c, t = slice(c0, c0 + n), slice(q * P, (q + 1) * P)
        pe.matmul(bank, self.hi[:, t], w.hi[:, c], start=True, stop=False)
        pe.matmul(bank, self.lo[:, t], w.hi[:, c], start=False, stop=False)
        pe.matmul(bank, self.hi[:, t], w.lo[:, c], start=False, stop=False)
        return pe.matmul(bank, self.tail[:, t], w.tail[:, c], start=False, stop=True)


class Split:

    def __init__(self, ctx, nc, name):
        sb = lambda n, s: ctx.enter_context(nc.sbuf_tensor(name + n, s, F32R))
        self.hi, self.lo, self.tail = sb("hi", [P, INNER]), sb("lo", [P, INNER]), sb("tail", [3 * DT, INNER])


def split_weights(ctx, nc, name, jobs, raw, raw_tail):
    n = len(jobs)
    s_raw = [ctx.enter_context(nc.semaphore(f"{name}raw_loaded{i}")) for i in range(n)]
    s_round = ctx.enter_context(nc.semaphore(f"{name}weights_rounded"))
    s_rest = ctx.enter_context(nc.semaphore(f"{name}weights_rest"))
    with nc.Block() as block:
        @block.sync
        def _(sp):
            for i, (w, _) in enumerate(jobs):
                if i >= 2:
                    sp.wait_ge(s_rest, 2 * (i - 1))
                    sp.wait_ge(s_round, 2 * (i - 1))
                sp.dma_start(raw[:, i % 2, :], w[0:P, :]).then_inc(s_raw[i], 16)
                for r in range(3):
                    sp.dma_start(raw_tail[r * DT:(r + 1) * DT, i % 2, :], w[P:D, :]).then_inc(s_raw[i], 16)

        @block.scalar
        def _(act):
            for i, (_, parts) in enumerate(jobs):
                act.wait_ge(s_raw[i], 64)
                act.copy(parts.hi[:], raw[:, i % 2, :]).then_inc(s_round, 1)
                act.copy(parts.tail[:], raw_tail[:, i % 2, :]).then_inc(s_round, 1)

        @block.vector
        def _(dve):
            for i, (_, parts) in enumerate(jobs):
                dve.wait_ge(s_raw[i], 64)
                dve.wait_ge(s_round, 2 * i + 2)
                dve.tensor_tensor(parts.lo[:], raw[:, i % 2, :], parts.hi[:].bitcast(F32), ALU.subtract).then_inc(s_rest, 1)
                dve.tensor_tensor(parts.tail[2 * DT:3 * DT, :], raw_tail[2 * DT:3 * DT, i % 2, :],
                                  parts.tail[2 * DT:3 * DT, :].bitcast(F32), ALU.subtract).then_inc(s_rest, 1)


def selfattn(nc, x, ident, norm_args, w_q, w_k, w_v, w_o, bias_o, banks):
    LEAD, LAG = 6, 2
    NB = H1 * QT
    PAIRB = 2 * QT
    VS = 5
    PS = 4
    TS = 4
    LN_AT = 44
    with ExitStack() as ctx:
        sb = lambda n, s, d=F32: ctx.enter_context(nc.sbuf_tensor("sa_" + n, s, d))
        sig = lambda n, per, credit=0, step=1: Signal(ctx, nc, "sa_" + n, per, credit, step)
        q_stack = sb("q_stack", [P, 2, 2, S], F32R)
        k_stack = sb("k_stack", [P, 2, 2, 2, S], F32R)
        q_parts = sb("q_parts", [P, 2, S], F32R)
        k_parts = sb("k_parts", [P, 2, S], F32R)
        v = sb("v", [P, VS, QT, P])
        probs = sb("probs", [P, PS, QT, S])
        turned = sb("turned", [P, TS, S])
        att = sb("att", [P, NPAIR, S])
        hat = sb("hat", [P, QT, D])
        full = sb("full", [P, S])
        full_tail = sb("full_tail", [DT, S])
        hi, lo, tail = sb("y_hi", [P, S], F32R), sb("y_lo", [P, S], F32R), sb("y_tail", [3 * DT, S], F32R)
        negmax = sb("negmax", [P, 4 * QT])
        total = sb("total", [P, 4 * QT])
        inverse = sb("inverse", [P, 4 * QT])

        b_scores, b_turn, b_out, b_proj = banks[0:2], banks[2:4], banks[4:6], banks[6:8]
        ln = Norm(ctx, nc, "sa_ln_", x, hat, hi, lo, tail, full, full_tail, *norm_args, b_proj)

        s_q = sig("q_projected", NPAIR, 2)
        s_k = sig("k_projected", NPAIR, 2)
        s_v = sig("v_projected", NPAIR, 2)
        s_qhi = sig("q_rounded", NPAIR)
        s_khi = sig("k_rounded", NPAIR)
        s_qlo = sig("q_rest", NPAIR, 2)
        s_klo = sig("k_rest", NPAIR, 2)
        s_vsb = sig("v_copied", NPAIR, 2)
        s_stack = [sig(f"stacked{i}", NPAIR // 2, 0, 8 * 16) for i in range(2)]
        s_scores = sig("scores_made", NB, 8 * QT)
        s_max = sig("max_made", NB)
        s_exp = sig("exp_made", NB, 4 * QT)
        s_inv = sig("inverse_made", NB)
        s_norm = sig("probs_scaled", NB)
        s_noted = ctx.enter_context(nc.semaphore("sa_inverse_noted"))
        s_noted_sp = ctx.enter_context(nc.semaphore("sa_parts_noted"))
        s_turn = sig("turned_made", NB, 4 * QT)
        s_evac = sig("turned_copied", NB, 4)
        s_pv = sig("pv_made", NB, 6 * QT * 2)
        s_att = sig("att_copied", NPAIR, 2)
        s_o = sig("out_projected", 2, 2)
        s_bias = sig("bias_added", 1)
        s_x = sig("x_updated", QT, QT)

        block = ctx.enter_context(nc.Block())

        @block.sync
        def _(sp):
            def stack(b, j):
                s = j % 2
                sp.wait_ge(s_klo.sem, s_klo.at(b, j))
                sp.sem_inc(s_noted_sp, 1)
                sp.wait_ge(s_scores.sem, s_scores.at(b, PAIRB * (j - 1) - 1))
                for e in range(2):
                    rows = slice(e * HD, (e + 1) * HD)
                    for half in range(2):
                        to = slice(half * HD, (half + 1) * HD)
                        sp.dma_start(q_stack[to, s, e, :].bitcast(F32), q_parts[rows, half, :].bitcast(F32)).then_inc(s_stack[s].sem, 16)
                        sp.dma_start(k_stack[to, s, e, :, :].bitcast(F32), k_parts[rows, :, :].bitcast(F32)).then_inc(s_stack[s].sem, 16)

            stack(0, 0)
            stack(0, 1)

            def batch(b, more):
                for j in range(2, NPAIR):
                    stack(b, j)
                if more:
                    stack(b + 1, 0)
                    stack(b + 1, 1)

            over_batches(sp, batch)

        @block.tensor
        def _(pe):
            ln.start_tensor(pe)
            for s in (s_q, s_k, s_v, s_scores, s_turn, s_pv, s_o):
                pe.sem_inc(s.sem, s.credit)

            def turn_norm(b):
                def bank_free(i):
                    if i == 0:
                        pe.wait_ge(s_vsb.sem, s_vsb.at(b, -1))
                    else:
                        pe.wait_ge(s_klo.sem, s_klo.at(b, -1))
                ln.turn(pe, b, ident, bank_free)

            def project(b, j, what):
                if j == 0 and what == 0:
                    ln.ready(pe, b)
                if what == 0:
                    if j > 0:
                        pe.wait_ge(s_vsb.sem, s_vsb.at(b, j - 1))
                    ln.project(pe, b_proj[0], w_q, j * P).then_inc(s_q.sem, 1)
                elif what == 1:
                    if j > 0:
                        pe.wait_ge(s_klo.sem, s_klo.at(b, j - 1))
                    ln.project(pe, b_proj[1], w_k, j * P).then_inc(s_k.sem, 1)
                else:
                    pe.wait_ge(s_qlo.sem, s_qlo.at(b, j))
                    for q in range(QT):
                        last = ln.project_tokens(pe, b_proj[0][:, q * P:(q + 1) * P], w_v, j * P, q)
                    last.then_inc(s_v.sem, 1)

            def scores(b, n):
                h, q = divmod(n, QT)
                j, e = divmod(h, 2)
                if n % PAIRB == 0:
                    pe.wait_ge(s_stack[j % 2].sem, s_stack[j % 2].at(b, j // 2))
                pe.wait_ge(s_exp.sem, s_exp.at(b, n - 2))
                lhs = q_stack[:, j % 2, e, q * P:(q + 1) * P]
                bank = b_scores[n % 2]
                pe.matmul(bank, lhs, k_stack[:, j % 2, e, 0, :], start=True, stop=False)
                pe.matmul(bank, lhs, k_stack[:, j % 2, e, 1, :], start=False, stop=True).then_inc(s_scores.sem, 1)

            def turns(b, n):
                h, k = divmod(n, QT)
                if k == 0:
                    pe.wait_ge(s_norm.sem, s_norm.at(b, QT * h + QT - 1))
                pe.wait_ge(s_evac.sem, s_evac.at(b, n - 2))
                for q in range(QT):
                    last = pe.transpose(b_turn[n % 2][:, q * P:(q + 1) * P], probs[:, h % PS, q, k * P:(k + 1) * P], ident[:])
                last.then_inc(s_turn.sem, 1)

            def pv(b, n):
                h, k = divmod(n, QT)
                j, e = divmod(h, 2)
                pe.wait_ge(s_evac.sem, s_evac.at(b, n))
                if n % PAIRB == 0:
                    pe.wait_ge(s_vsb.sem, s_vsb.at(b, j))
                    if j >= 2:
                        pe.wait_ge(s_att.sem, s_att.at(b, j - 2))
                    else:
                        pe.wait_ge(s_x.sem, s_x.at(b, 2 * j - 1 - QT + 2))
                pe.matmul(b_out[j % 2][e * HD:(e + 1) * HD, :], v[:, j % VS, k, e * HD:(e + 1) * HD],
                          turned[:, n % TS, :], start=(k == 0), stop=(k == QT - 1)).then_inc(s_pv.sem, 1)

            def project_out(b, half):
                if half == 0:
                    pe.wait_ge(s_att.sem, s_att.at(b, NPAIR - 2))
                else:
                    pe.wait_ge(s_att.sem, s_att.at(b, NPAIR - 1))
                for t in range(2):
                    q = 2 * half + t
                    for j in range(NPAIR):
                        if half == 0 and t == 0 and j == NPAIR - 1:
                            pe.wait_ge(s_att.sem, s_att.at(b, NPAIR - 1))
                        last = pe.matmul(b_out[half][:, t * D:(t + 1) * D], att[:, j, q * P:(q + 1) * P],
                                         w_o[:, j, :], start=(j == 0), stop=(j == NPAIR - 1))
                last.then_inc(s_o.sem, 1)

            turn_norm(0)
            for what in range(3):
                project(0, 0, what)
            scores(0, 0)
            for what in range(3):
                project(0, 1, what)
            for n in range(1, LEAD):
                scores(0, n)

            def batch(b, more):
                for n in range(NB):
                    m = n + LEAD
                    if m < NB:
                        scores(b, m)
                    elif more:
                        scores(b + 1, m - NB)
                    if n >= LAG:
                        pv(b, n - LAG)
                    turns(b, n)
                    j, what = n // PAIRB + 2, n % PAIRB - 2
                    if what in (0, 1, 2):
                        if j < NPAIR:
                            project(b, j, what)
                        elif more:
                            project(b + 1, j - NPAIR, what)
                    if n == PAIRB * (NPAIR - 3) + 5 and more:
                        turn_norm(b + 1)
                for n in range(NB - LAG, NB):
                    pv(b, n)
                project_out(b, 0)
                project_out(b, 1)

            over_batches(pe, batch)

        @block.scalar
        def _(act):
            ln.start_scalar(act)
            for s in (s_vsb, s_exp, s_att):
                act.sem_inc(s.sem, s.credit)

            def operands_free(b):
                def wait(eng):
                    eng.wait_ge(s_v.sem, s_v.at(b, -1))
                return wait

            def round_part(b, j, what):
                if what == 0:
                    act.wait_ge(s_q.sem, s_q.at(b, j))
                    act.wait_ge(s_scores.sem, s_scores.at(b, PAIRB * (j - 1)))
                    act.activation(q_parts[:, 0, :], b_proj[0], ACT.Copy, scale=SCALE1).then_inc(s_qhi.sem, 1)
                elif what == 1:
                    act.wait_ge(s_k.sem, s_k.at(b, j))
                    act.copy(k_parts[:, 0, :], b_proj[1]).then_inc(s_khi.sem, 1)
                else:
                    act.wait_ge(s_v.sem, s_v.at(b, j))
                    act.wait_ge(s_pv.sem, s_pv.at(b, PAIRB * (j - VS + 1) - 1))
                    act.copy(v[:, j % VS, :, :].rearrange("p a c -> p (a c)"), b_proj[0]).then_inc(s_vsb.sem, 1)

            def exps(b, n):
                h, q = divmod(n, QT)
                c = n % (4 * QT)
                act.wait_ge(s_max.sem, s_max.at(b, n))
                if q == 0:
                    act.wait_ge(s_turn.sem, s_turn.at(b, QT * (h - PS) + QT - 1))
                act.activation(probs[:, h % PS, q, :], b_scores[n % 2], ACT.Exp, bias=negmax[:, c:c + 1],
                               accum_out=total[:, c:c + 1]).then_inc(s_exp.sem, 1)

            def copy_att(b, j):
                act.wait_ge(s_pv.sem, s_pv.at(b, PAIRB * j + PAIRB - 1))
                act.wait_ge(s_o.sem, s_o.at(b, -1))
                act.copy(att[:, j, :], b_out[j % 2]).then_inc(s_att.sem, 1)

            ln.scale_and_round(act, 0, operands_free(0))
            for what in range(3):
                round_part(0, 0, what)
            exps(0, 0)
            for what in range(3):
                round_part(0, 1, what)
            for n in range(1, LEAD):
                exps(0, n)

            def batch(b, more):
                for n in range(NB):
                    m = n + LEAD
                    if m < NB:
                        exps(b, m)
                    elif more:
                        exps(b + 1, m - NB)
                    j, what = n // PAIRB + 2, n % PAIRB - 2
                    if what in (0, 1, 2):
                        if j < NPAIR:
                            round_part(b, j, what)
                        elif more:
                            round_part(b + 1, j - NPAIR, what)
                    if n % PAIRB == LAG + 1 and n > PAIRB:
                        copy_att(b, n // PAIRB - 1)
                    if n == PAIRB * (NPAIR - 3) + 5 and more:
                        ln.scale_and_round(act, b + 1, operands_free(b + 1))
                copy_att(b, NPAIR - 1)

            over_batches(act, batch)

        @block.vector
        def _(dve):
            ln.start_vector(dve)
            for s in (s_qlo, s_klo, s_evac, s_x):
                dve.sem_inc(s.sem, s.credit)

            def operands_free(b):
                def wait(eng):
                    eng.wait_ge(s_v.sem, s_v.at(b, -1))
                return wait

            def rest(b, j, what):
                if what == 0:
                    dve.wait_ge(s_qhi.sem, s_qhi.at(b, j))
                    dve.scalar_tensor_tensor(out=q_parts[:, 1, :], in0=b_proj[0], scalar=SCALE1, in1=q_parts[:, 0, :].bitcast(F32),
                                             op0=ALU.mult, op1=ALU.subtract).then_inc(s_qlo.sem, 1)
                else:
                    dve.wait_ge(s_khi.sem, s_khi.at(b, j))
                    dve.tensor_tensor(k_parts[:, 1, :], b_proj[1], k_parts[:, 0, :].bitcast(F32), ALU.subtract).then_inc(s_klo.sem, 1)

            def maxima(b, n):
                c = n % (4 * QT)
                dve.wait_ge(s_scores.sem, s_scores.at(b, n))
                dve.tensor_reduce(negmax[:, c:c + 1], b_scores[n % 2], AX_X, ALU.max, negate=True).then_inc(s_max.sem, 1)

            def inverses(b, n):
                c = n % (4 * QT)
                dve.wait_ge(s_exp.sem, s_exp.at(b, n))
                dve.reciprocal(inverse[:, c:c + 1], total[:, c:c + 1]).then_inc(s_inv.sem, 1)

            def copy_turned(b, n):
                dve.wait_ge(s_turn.sem, s_turn.at(b, n))
                dve.wait_ge(s_pv.sem, s_pv.at(b, n - TS))
                dve.tensor_copy(turned[:, n % TS, :], b_turn[n % 2]).then_inc(s_evac.sem, 1)

            def update(b):
                for half in range(2):
                    dve.wait_ge(s_o.sem, s_o.at(b, half))
                    if half == 0:
                        dve.wait_ge(s_bias.sem, s_bias.at(b, 0))
                    for t in range(2):
                        xt = x[:, bass.ds(b * QT + 2 * half + t, 1), :].rearrange("p a d -> p (a d)")
                        dve.tensor_tensor(xt, b_out[half][:, t * D:(t + 1) * D], xt, ALU.add).then_inc(s_x.sem, 1)

            ln.statistics(dve, 0)
            ln.standardize(dve, 0)
            ln.remainder(dve, 0, operands_free(0))
            for what in range(2):
                rest(0, 0, what)
            maxima(0, 0)
            for what in range(2):
                rest(0, 1, what)
            for n in range(1, LEAD):
                maxima(0, n)
                inverses(0, n - 1)

            def batch(b, more):
                for n in range(NB):
                    m = n + LEAD
                    if m < NB:
                        maxima(b, m)
                    elif more:
                        maxima(b + 1, m - NB)
                    if m - 1 < NB:
                        inverses(b, m - 1)
                    elif more:
                        inverses(b + 1, m - 1 - NB)
                    copy_turned(b, n)
                    j, what = n // PAIRB + 2, n % PAIRB - 2
                    if what in (0, 1):
                        if j < NPAIR:
                            rest(b, j, what)
                        elif more:
                            rest(b + 1, j - NPAIR, what)
                    if more and n == LN_AT:
                        ln.statistics(dve, b + 1)
                    if more and n == LN_AT + 4:
                        ln.standardize(dve, b + 1)
                    if n == PAIRB * (NPAIR - 3) + 5 and more:
                        ln.remainder(dve, b + 1, operands_free(b + 1))
                update(b)

            over_batches(dve, batch)

        @block.gpsimd
        def _(pool):
            ln.start_gpsimd(pool)

            def scale(b, n):
                h, q = divmod(n, QT)
                c = n % (4 * QT)
                pool.wait_ge(s_inv.sem, s_inv.at(b, n))
                pool.sem_inc(s_noted, 1)
                pool.tensor_scalar(probs[:, h % PS, q, :], probs[:, h % PS, q, :], inverse[:, c:c + 1], 1.0,
                                   ALU.mult, ALU.mult).then_inc(s_norm.sem, 1)

            def add_bias(b):
                pool.wait_ge(ln.s_hat.sem, ln.s_hat.at(b, QT - 1))
                xt = x[:, bass.ds(b * QT, QT), :]
                pool.tensor_tensor(xt, xt, bias_o[:].unsqueeze(1).broadcast_to([P, QT, D]), ALU.add).then_inc(s_bias.sem, 1)

            ln.deviations(pool, 0)
            add_bias(0)
            for n in range(LEAD - 1):
                scale(0, n)

            def batch(b, more):
                for n in range(NB):
                    m = n + LEAD - 1
                    if m < NB:
                        scale(b, m)
                    elif more:
                        scale(b + 1, m - NB)
                    if more and n == LN_AT + 2:
                        ln.deviations(pool, b + 1)
                    if more and n == LN_AT + 8:
                        add_bias(b + 1)

            over_batches(pool, batch)


def adapter(nc, t, x, ident, ctx_t, banks):
    w = lambda n: t["L0_xattn_" + n]
    with ExitStack() as ctx:
        sb = lambda n, s, d=F32: ctx.enter_context(nc.sbuf_tensor("ad_" + n, s, d))
        sig = lambda n, per, credit=0, step=1: Signal(ctx, nc, "ad_" + n, per, credit, step)
        HC = H0 * HP
        wq = sb("wq", [P, G, H0, HP])
        wo = sb("wo", [P, G, D])
        wk, wv, wk_ca, wv_ca = (sb(n, [CTX, H0, HP]) for n in ("wk", "wv", "wk_ca", "wv_ca"))
        wq_ca = sb("wq_ca", [NCA, H0, HP])
        b_o = sb("b_out", [P, D])
        expand = sb("expand", [CTX, S])
        own = sb("own", [H0 * NCA, HC])
        context = sb("context", [SK, CTX])
        tokens = sb("tokens", [NCA, CTX])
        x_pad = sb("x_pad", [P, QT, H0, HP])
        x_t = sb("x_t", [P, G, S])
        c_t = sb("c_t", [CTX, SK])
        c_rep = sb("c_rep", [CTX, H0, NCA])
        q_t = sb("q_t", [P, G, S])
        q1_diag = sb("q1_diag", [P, H0, CTX])
        k_diag = sb("k_diag", [P, G, HG, SE])
        k2_diag = sb("k2_diag", [P, G, HG, NCA])
        v = sb("v", [SE, HC])
        v2 = sb("v2", [H0 * NCA, HC])
        probs = sb("probs", [P, QT, G, HG, SE])
        turned = sb("turned", [SE, 2, S])
        probs1 = sb("probs1", [CTX, 2, S])
        turned1 = sb("turned1", [P, 2, QT, CTX])
        hs1 = sb("hs1", [P, G, CTX])
        q2 = sb("q2", [P, G, CTX])
        probs2 = sb("probs2", [CTX, H0, NCA])
        probs2x = sb("probs2x", [H0 * NCA, S])
        heads = sb("heads", [P, G, S])
        negmax1, total1, inverse1 = (sb(n, [CTX, 2]) for n in ("negmax1", "total1", "inverse1"))
        top, total, inverse = (sb(n, [P, QT * G, HG]) for n in ("top", "total", "inverse"))
        top2, total2, inverse2 = (sb(n, [CTX, H0]) for n in ("top2", "total2", "inverse2"))
        flat = lambda tile: tile.rearrange("p a b -> p (a b)")

        NU = QT * G
        s_w = ctx.enter_context(nc.semaphore("ad_weights_loaded"))
        s_zero = ctx.enter_context(nc.semaphore("ad_cleared"))
        s_ctx = sig("context_loaded", 2, 0, 16)
        s_noted = ctx.enter_context(nc.semaphore("ad_noted"))
        s_noted_pool = ctx.enter_context(nc.semaphore("ad_noted_pool"))
        s_noted_dve = ctx.enter_context(nc.semaphore("ad_noted_dve"))
        s_pad = sig("x_padded", 1)
        s_bias = sig("bias_added", 1)
        s_xturn = sig("x_turned", G)
        s_xt = sig("x_t_copied", G)
        s_cturn = sig("c_turned", 1)
        s_ct = sig("c_t_copied", 1)
        s_ctall = sig("c_t_kept", 1, 1)
        s_crep = sig("c_rep_made", 1)
        s_q1p = sig("q1_projected", 1)
        s_q1 = sig("q1_placed", HG)
        s_kp = sig("k_projected", 1)
        s_kd = sig("k_placed", 2 * HG)
        s_vp = sig("v_projected", 1, 1)
        s_vd = sig("v_placed", 2)
        s_qp = sig("q_projected", G)
        s_q = sig("q_copied", G)
        s_s1 = sig("scores1_made", H0)
        s_max1 = sig("max1_made", H0)
        s_exp1 = sig("exp1_made", H0, 2)
        s_inv1 = sig("inverse1_made", H0)
        s_norm1 = sig("probs1_scaled", H0)
        s_turn1 = sig("turned1_made", H0, 2)
        s_evac1 = sig("turned1_copied", H0, 2)
        s_pv1 = sig("pv1_made", H0, 2)
        s_s = sig("scores_made", NU, 1)
        s_max = sig("max_made", NU)
        s_sub = sig("shifted", NU, 2)
        s_exp = sig("exp_made", NU)
        s_sum = sig("sum_made", NU)
        s_inv = sig("inverse_made", NU)
        s_norm = sig("probs_scaled", NU)
        s_hs1 = sig("hs1_copied", 1)
        s_q2p = sig("q2_projected", 1)
        s_q2 = sig("q2_copied", 1)
        s_s2 = sig("scores2_made", 1)
        s_soft2 = sig("softmax2_steps", 6)
        s_px = sig("probs2_expanded", 1)
        s_p2x = sig("probs2x_copied", 1, 1)
        s_turn = sig("turned_made", H0, 2)
        s_evac = sig("turned_copied", H0, 2)
        s_pv = sig("pv_made", H0, 2)
        s_add2 = sig("adapter_added", G, 2)
        s_heads = sig("heads_copied", G, 2)
        s_o = sig("out_projected", 2, 1)
        s_x = sig("x_updated", QT, QT)
        N_W = 2 * H0 + 8

        block = ctx.enter_context(nc.Block())

        @block.sync
        def _(sp):
            sp.wait_ge(s_zero, 11)
            by_head = lambda ap: ap.rearrange("r (h c) -> r h c", h=H0)
            for h in range(H0):
                to = slice(HP * (h % HG), HP * (h % HG) + HD0)
                rows = slice(h * HD0, (h + 1) * HD0)
                sp.dma_start(wq[to, h // HG, :, 0:HD0], by_head(w("Wq")[rows, :])).then_inc(s_w, 16)
                sp.dma_start(wo[to, h // HG, :], w("Wout")[rows, :]).then_inc(s_w, 16)
            for tile, name in ((wk, "Wk"), (wv, "Wv"), (wk_ca, "Wk_ca"), (wv_ca, "Wv_ca"), (wq_ca, "Wq_ca")):
                sp.dma_start(tile[:, :, 0:HD0], by_head(w(name))).then_inc(s_w, 16)
            sp.dma_start(b_o[:], w("b_out").unsqueeze(0).broadcast_to([P, D])).then_inc(s_w, 16)
            sp.dma_start(expand[:], t["expand"]).then_inc(s_w, 16)
            sp.dma_start(own[:], t["own"]).then_inc(s_w, 16)
            rows = t["ctx_768"]
            with sp.Fori(0, B) as b:
                sp.wait_ge(s_vp.sem, s_vp.at(b, -1))
                sp.sem_inc(s_noted, 1)
                sp.dma_start(context[:], rows[bass.ds(b, 1), :, :].rearrange("a k c -> (a k) c")).then_inc(s_ctx.sem, 16)
                sp.dma_start(tokens[:], rows[bass.ds(b, 1), SE:SK, :].rearrange("a k c -> (a k) c")).then_inc(s_ctx.sem, 16)

        @block.tensor
        def _(pe):
            for s in (s_vp, s_turn1, s_pv1, s_s, s_turn, s_pv, s_add2, s_o):
                pe.sem_inc(s.sem, s.credit)
            pe.wait_ge(s_w, 16 * N_W)

            def batch(b, _):
                pe.wait_ge(s_ctx.sem, s_ctx.at(b, 1))
                pe.wait_ge(s_evac.sem, s_evac.at(b, -1))
                pe.transpose(banks[2][0:CTX, 0:SK], context[:], ident[0:SK, 0:SK]).then_inc(s_cturn.sem, 1)
                pe.wait_ge(s_pad.sem, s_pad.at(b, 0))
                pe.wait_ge(s_heads.sem, s_heads.at(b, -1))
                for g in range(G):
                    for q in range(QT):
                        last = pe.transpose(banks[g][:, q * P:(q + 1) * P], x_pad[:, q, g * HG:(g + 1) * HG, :].rearrange("p h c -> p (h c)"), ident[:])
                    last.then_inc(s_xturn.sem, 1)
                for g in range(G):
                    last = pe.matmul(banks[3][:, g * CTX:(g + 1) * CTX], flat(wq_ca[:, g * HG:(g + 1) * HG, :]), tokens[:], start=True, stop=True)
                last.then_inc(s_q1p.sem, 1)
                pe.wait_ge(s_ct.sem, s_ct.at(b, 0))
                for g in range(G):
                    cols = slice(g * HG, (g + 1) * HG)
                    pe.matmul(banks[2][:, g * SE:(g + 1) * SE], flat(wk[:, cols, :]), c_t[:, 0:SE], start=True, stop=True)
                    last = pe.matmul(banks[2][:, G * SE + g * NCA:G * SE + (g + 1) * NCA], flat(wk_ca[:, cols, :]), c_t[:, SE:SK], start=True, stop=True)
                last.then_inc(s_kp.sem, 1)
                pe.wait_ge(s_crep.sem, s_crep.at(b, 0))
                pe.wait_ge(s_p2x.sem, s_p2x.at(b, -1))
                pe.matmul(banks[4][0:SE, 0:HC], c_t[:, 0:SE], flat(wv[:]), start=True, stop=True)
                pe.matmul(banks[4][0:H0 * NCA, HC:2 * HC], flat(c_rep[:]), flat(wv_ca[:]), start=True, stop=True).then_inc(s_vp.sem, 1)
                pe.wait_ge(s_x.sem, s_x.at(b, -1))
                for g in range(G):
                    for k in range(G):
                        if g == 0:
                            pe.wait_ge(s_xt.sem, s_xt.at(b, k))
                        last = pe.matmul(banks[5 + g], flat(wq[:, k, g * HG:(g + 1) * HG, :]), x_t[:, k, :], start=(k == 0), stop=(k == G - 1))
                    last.then_inc(s_qp.sem, 1)

                def scores1(h):
                    if h == 0:
                        pe.wait_ge(s_q1.sem, s_q1.at(b, HG - 1))
                    if h >= 2:
                        pe.wait_ge(s_exp1.sem, s_exp1.at(b, h - 2))
                    pe.matmul(banks[h % 2][0:CTX, :], q1_diag[:, h, :], x_t[:, h // HG, :], start=True, stop=True).then_inc(s_s1.sem, 1)

                def scores(u):
                    q, g = divmod(u, G)
                    if u < 2:
                        pe.wait_ge(s_q.sem, s_q.at(b, G - 1))
                    else:
                        pe.wait_ge(s_sub.sem, s_sub.at(b, u - 2))
                    if u == 0:
                        pe.wait_ge(s_kd.sem, s_kd.at(b, 2 * HG - 1))
                    pe.matmul(banks[5 + g][:, 0:HG * SE], q_t[:, g, q * P:(q + 1) * P], k_diag[:, g, :, :].rearrange("p h k -> p (h k)"),
                              start=True, stop=True).then_inc(s_s.sem, 1)

                def turns1(h):
                    pe.wait_ge(s_norm1.sem, s_norm1.at(b, h))
                    if h == 0:
                        pe.wait_ge(s_kd.sem, s_kd.at(b, 2 * HG - 1))
                    elif h >= 2:
                        pe.wait_ge(s_evac1.sem, s_evac1.at(b, h - 2))
                    for k in range(QT):
                        last = pe.transpose(banks[2 + h % 2][:, k * CTX:(k + 1) * CTX], probs1[:, h % 2, k * P:(k + 1) * P], ident[0:CTX, 0:CTX])
                    last.then_inc(s_turn1.sem, 1)

                def pv1(h):
                    g, j = divmod(h, HG)
                    pe.wait_ge(s_evac1.sem, s_evac1.at(b, h))
                    for k in range(QT):
                        last = pe.matmul(banks[7][j * HP:(j + 1) * HP, g * CTX:(g + 1) * CTX], x_pad[:, k, h, :], turned1[:, h % 2, k, :],
                                         start=(k == 0), stop=(k == QT - 1))
                    last.then_inc(s_pv1.sem, 1)

                for i in range(H0 + 3):
                    if i < H0:
                        scores1(i)
                        scores(i)
                    if 2 <= i < H0 + 2:
                        turns1(i - 2)
                    if i >= 3:
                        pv1(i - 3)

                pe.wait_ge(s_hs1.sem, s_hs1.at(b, 0))
                for g in range(G):
                    for k in range(G):
                        last = pe.matmul(banks[7][:, g * CTX:(g + 1) * CTX], flat(wq[:, k, g * HG:(g + 1) * HG, :]), hs1[:, k, :], start=(k == 0), stop=(k == G - 1))
                last.then_inc(s_q2p.sem, 1)

                def turns(h):
                    if h == 0:
                        pe.wait_ge(s_norm.sem, s_norm.at(b, NU - 1))
                    if h < 2:
                        pe.wait_ge(s_evac1.sem, s_evac1.at(b, H0 - 1))
                    else:
                        pe.wait_ge(s_evac.sem, s_evac.at(b, h - 2))
                    for q in range(QT):
                        last = pe.transpose(banks[2 + h % 2][0:SE, q * P:(q + 1) * P], probs[:, q, h // HG, h % HG, :], ident[:])
                    last.then_inc(s_turn.sem, 1)

                def pv(h):
                    g, j = divmod(h, HG)
                    pe.wait_ge(s_evac.sem, s_evac.at(b, h))
                    pe.matmul(banks[g][j * HP:(j + 1) * HP, :], v[:, h * HP:(h + 1) * HP], turned[:, h % 2, :],
                              start=True, stop=False, skip_group_check=True).then_inc(s_pv.sem, 1)

                turns(0)
                pe.wait_ge(s_q2.sem, s_q2.at(b, 0))
                for g in range(G):
                    last = pe.matmul(banks[7][0:CTX, g * HG * NCA:(g + 1) * HG * NCA], q2[:, g, :], k2_diag[:, g, :, :].rearrange("p h k -> p (h k)"), start=True, stop=True)
                last.then_inc(s_s2.sem, 1)
                for h in range(1, H0):
                    turns(h)
                    pv(h - 1)
                pv(H0 - 1)
                pe.wait_ge(s_soft2.sem, s_soft2.at(b, 5))
                pe.matmul(banks[4][0:H0 * NCA, :], flat(probs2[:]), expand[:], start=True, stop=True).then_inc(s_px.sem, 1)
                pe.wait_ge(s_p2x.sem, s_p2x.at(b, 0))
                for g in range(G):
                    pe.matmul(banks[g], v2[:, g * P:(g + 1) * P], probs2x[:], start=False, stop=True, skip_group_check=True).then_inc(s_add2.sem, 1)
                for half in range(2):
                    for i in range(2):
                        q = 2 * half + i
                        for g in range(G):
                            if q == 0:
                                pe.wait_ge(s_heads.sem, s_heads.at(b, g))
                            last = pe.matmul(banks[5 + half][:, i * D:(i + 1) * D], heads[:, g, q * P:(q + 1) * P], wo[:, g, :], start=(g == 0), stop=(g == G - 1))
                    last.then_inc(s_o.sem, 1)

            over_batches(pe, batch, peel=False)

        @block.scalar
        def _(act):
            for s in (s_exp1, s_evac1, s_evac, s_p2x, s_heads):
                act.sem_inc(s.sem, s.credit)

            def batch(b, _):
                act.wait_ge(s_cturn.sem, s_cturn.at(b, 0))
                act.wait_ge(s_vp.sem, s_vp.at(b, -1))
                act.wait_ge(s_ctall.sem, s_ctall.at(b, -1))
                act.copy(c_t[:], banks[2][0:CTX, 0:SK]).then_inc(s_ct.sem, 1)
                for g in range(G):
                    act.wait_ge(s_xturn.sem, s_xturn.at(b, g))
                    act.copy(x_t[:, g, :], banks[g]).then_inc(s_xt.sem, 1)
                for g in range(G):
                    act.wait_ge(s_qp.sem, s_qp.at(b, g))
                    act.activation(q_t[:, g, :], banks[5 + g], ACT.Copy, scale=SCALE0).then_inc(s_q.sem, 1)

                def exp1(h):
                    act.wait_ge(s_max1.sem, s_max1.at(b, h))
                    act.wait_ge(s_turn1.sem, s_turn1.at(b, h - 2))
                    act.activation(probs1[:, h % 2, :], banks[h % 2][0:CTX, :], ACT.Exp, bias=negmax1[:, h % 2:h % 2 + 1],
                                   accum_out=total1[:, h % 2:h % 2 + 1]).then_inc(s_exp1.sem, 1)

                def exp(u):
                    q, g = divmod(u, G)
                    act.wait_ge(s_sub.sem, s_sub.at(b, u))
                    p = probs[:, q, g, :, :].rearrange("p h k -> p (h k)")
                    act.activation(p, p, ACT.Exp).then_inc(s_exp.sem, 1)

                def copy_turned1(h):
                    act.wait_ge(s_turn1.sem, s_turn1.at(b, h))
                    act.wait_ge(s_pv1.sem, s_pv1.at(b, h - 2))
                    act.copy(turned1[:, h % 2, :, :].rearrange("p k c -> p (k c)"), banks[2 + h % 2][:, 0:QT * CTX]).then_inc(s_evac1.sem, 1)

                for i in range(H0 + 2):
                    if i < H0:
                        exp1(i)
                        exp(i)
                    if i >= 2:
                        copy_turned1(i - 2)
                act.wait_ge(s_pv1.sem, s_pv1.at(b, H0 - 1))
                act.copy(flat(hs1[:]), banks[7][:, 0:G * CTX]).then_inc(s_hs1.sem, 1)
                act.wait_ge(s_q2p.sem, s_q2p.at(b, 0))
                act.activation(flat(q2[:]), banks[7][:, 0:G * CTX], ACT.Copy, scale=SCALE0).then_inc(s_q2.sem, 1)

                def copy_turned(h):
                    act.wait_ge(s_turn.sem, s_turn.at(b, h))
                    act.wait_ge(s_pv.sem, s_pv.at(b, h - 2))
                    act.copy(turned[:, h % 2, :], banks[2 + h % 2][0:SE, :]).then_inc(s_evac.sem, 1)

                for h in range(H0):
                    copy_turned(h)
                    if h == 2:
                        act.wait_ge(s_soft2.sem, s_soft2.at(b, 1))
                        act.activation(flat(probs2[:]), flat(probs2[:]), ACT.Exp).then_inc(s_soft2.sem, 1)
                act.wait_ge(s_px.sem, s_px.at(b, 0))
                act.wait_ge(s_add2.sem, s_add2.at(b, -1))
                act.copy(probs2x[:], banks[4][0:H0 * NCA, :]).then_inc(s_p2x.sem, 1)
                act.wait_ge(s_o.sem, s_o.at(b, -1))
                for g in range(G):
                    act.wait_ge(s_add2.sem, s_add2.at(b, g))
                    act.copy(heads[:, g, :], banks[g]).then_inc(s_heads.sem, 1)

            over_batches(act, batch, peel=False)

        @block.vector
        def _(dve):
            for s in (s_sub, s_x):
                dve.sem_inc(s.sem, s.credit)
            for tile in (q1_diag, k_diag, k2_diag):
                dve.memset(tile[:], 0.0).then_inc(s_zero, 1)
            dve.wait_ge(s_zero, 11)
            dve.wait_ge(s_w, 16 * N_W)

            def batch(b, _):
                xb = x[:, bass.ds(b * QT, QT), :]
                dve.wait_ge(s_pv1.sem, s_pv1.at(b, -1))
                dve.sem_inc(s_noted_dve, 1)
                dve.tensor_copy(x_pad[:, :, :, 0:HD0].rearrange("p q h c -> p (q h) c"),
                                xb.rearrange("p q (h c) -> p (q h) c", h=H0)).then_inc(s_pad.sem, 1)
                dve.wait_ge(s_ct.sem, s_ct.at(b, 0))
                dve.wait_ge(s_vp.sem, s_vp.at(b, -1))
                dve.tensor_copy(c_rep[:], c_t[:, SE:SK].unsqueeze(1).broadcast_to([CTX, H0, NCA])).then_inc(s_crep.sem, 1)
                dve.wait_ge(s_q1p.sem, s_q1p.at(b, 0))
                for j in range(HG):
                    rows = slice(j * HP, (j + 1) * HP)
                    dve.tensor_scalar(q1_diag[rows, j::HG, :], banks[3][rows, 0:G * CTX].rearrange("p (g c) -> p g c", g=G),
                                      SCALE0, None, ALU.mult).then_inc(s_q1.sem, 1)
                dve.wait_ge(s_kp.sem, s_kp.at(b, 0))
                for j in range(HG):
                    rows = slice(j * HP, (j + 1) * HP)
                    dve.tensor_copy(k_diag[rows, :, j, :], banks[2][rows, 0:G * SE].rearrange("p (g k) -> p g k", g=G)).then_inc(s_kd.sem, 1)
                    dve.tensor_copy(k2_diag[rows, :, j, :], banks[2][rows, G * SE:G * (SE + NCA)].rearrange("p (g k) -> p g k", g=G)).then_inc(s_kd.sem, 1)
                dve.wait_ge(s_vp.sem, s_vp.at(b, 0))
                dve.wait_ge(s_add2.sem, s_add2.at(b, -1))
                dve.tensor_copy(v[:], banks[4][0:SE, 0:HC]).then_inc(s_vd.sem, 1)
                dve.tensor_tensor(v2[:], banks[4][0:H0 * NCA, HC:2 * HC], own[:], ALU.mult).then_inc(s_vd.sem, 1)

                def max1(h):
                    dve.wait_ge(s_s1.sem, s_s1.at(b, h))
                    dve.tensor_reduce(negmax1[:, h % 2:h % 2 + 1], banks[h % 2][0:CTX, :], AX_X, ALU.max, negate=True).then_inc(s_max1.sem, 1)

                def inverses1(h):
                    dve.wait_ge(s_exp1.sem, s_exp1.at(b, h))
                    dve.reciprocal(inverse1[:, h % 2:h % 2 + 1], total1[:, h % 2:h % 2 + 1]).then_inc(s_inv1.sem, 1)

                def shift(u):
                    q, g = divmod(u, G)
                    s3 = banks[5 + g][:, 0:HG * SE].rearrange("p (h k) -> p h k", h=HG)
                    dve.wait_ge(s_s.sem, s_s.at(b, u))
                    dve.tensor_reduce(top[:, u, :], s3, AX_X, ALU.max).then_inc(s_max.sem, 1)
                    dve.wait_ge(s_max.sem, s_max.at(b, u))
                    if u == 0:
                        dve.wait_ge(s_turn.sem, s_turn.at(b, -1))
                    dve.tensor_tensor(probs[:, q, g, :, :], s3, top[:, u, :].unsqueeze(2).broadcast_to([P, HG, SE]), ALU.subtract).then_inc(s_sub.sem, 1)

                def scale(u):
                    q, g = divmod(u, G)
                    dve.wait_ge(s_exp.sem, s_exp.at(b, u))
                    dve.tensor_reduce(total[:, u, :], probs[:, q, g, :, :], AX_X, ALU.add).then_inc(s_sum.sem, 1)
                    dve.wait_ge(s_sum.sem, s_sum.at(b, u))
                    dve.reciprocal(inverse[:, u, :], total[:, u, :]).then_inc(s_inv.sem, 1)
                    dve.wait_ge(s_inv.sem, s_inv.at(b, u))
                    dve.tensor_tensor(probs[:, q, g, :, :], probs[:, q, g, :, :], inverse[:, u, :].unsqueeze(2).broadcast_to([P, HG, SE]),
                                      ALU.mult).then_inc(s_norm.sem, 1)

                for i in range(H0 + 1):
                    if i < H0:
                        max1(i)
                        shift(i)
                    if i >= 1:
                        inverses1(i - 1)
                        scale(i - 1)
                s3 = banks[7][0:CTX, 0:H0 * NCA].rearrange("p (h k) -> p h k", h=H0)
                spread = lambda tile: tile[:].unsqueeze(2).broadcast_to([CTX, H0, NCA])
                dve.wait_ge(s_s2.sem, s_s2.at(b, 0))
                dve.tensor_reduce(top2[:], s3, AX_X, ALU.max).then_inc(s_soft2.sem, 1)
                dve.wait_ge(s_soft2.sem, s_soft2.at(b, 0))
                dve.tensor_tensor(probs2[:], s3, spread(top2), ALU.subtract).then_inc(s_soft2.sem, 1)
                dve.wait_ge(s_soft2.sem, s_soft2.at(b, 2))
                dve.tensor_reduce(total2[:], probs2[:], AX_X, ALU.add).then_inc(s_soft2.sem, 1)
                dve.wait_ge(s_soft2.sem, s_soft2.at(b, 3))
                dve.reciprocal(inverse2[:], total2[:]).then_inc(s_soft2.sem, 1)
                dve.wait_ge(s_soft2.sem, s_soft2.at(b, 4))
                dve.tensor_tensor(probs2[:], probs2[:], spread(inverse2), ALU.mult).then_inc(s_soft2.sem, 1)
                dve.wait_ge(s_bias.sem, s_bias.at(b, 0))
                for half in range(2):
                    dve.wait_ge(s_o.sem, s_o.at(b, half))
                    for i in range(2):
                        xt = x[:, bass.ds(b * QT + 2 * half + i, 1), :].rearrange("p a d -> p (a d)")
                        dve.tensor_tensor(xt, banks[5 + half][:, i * D:(i + 1) * D], xt, ALU.add).then_inc(s_x.sem, 1)

            over_batches(dve, batch, peel=False)

        @block.gpsimd
        def _(pool):
            for tile in (x_pad, wq, wo, wk, wv, wk_ca, wv_ca, wq_ca):
                pool.memset(tile[:], 0.0).then_inc(s_zero, 1)
            pool.sem_inc(s_ctall.sem, 1)
            pool.wait_ge(s_zero, 11)
            pool.wait_ge(s_w, 16 * N_W)

            def batch(b, _):
                xb = x[:, bass.ds(b * QT, QT), :]
                pool.wait_ge(s_pad.sem, s_pad.at(b, 0))
                pool.tensor_tensor(xb, xb, b_o[:].unsqueeze(1).broadcast_to([P, QT, D]), ALU.add).then_inc(s_bias.sem, 1)
                pool.wait_ge(s_ct.sem, s_ct.at(b, 0))
                pool.sem_inc(s_noted_pool, 1)
                pool.tensor_copy(ctx_t[:, bass.ds(b, 1), :].rearrange("p a k -> p (a k)"), c_t[:]).then_inc(s_ctall.sem, 1)
                for h in range(H0):
                    pool.wait_ge(s_inv1.sem, s_inv1.at(b, h))
                    pool.sem_inc(s_noted_pool, 1)
                    pool.tensor_scalar(probs1[:, h % 2, :], probs1[:, h % 2, :], inverse1[:, h % 2:h % 2 + 1], 1.0, ALU.mult, ALU.mult).then_inc(s_norm1.sem, 1)

            over_batches(pool, batch, peel=False)


def crossattn(nc, x, ident, norm_args, ctx_t, w_q, w_k, w_v, w_o, bias_o, banks):
    LN_AT = 5
    with ExitStack() as ctx:
        sb = lambda n, s, d=F32: ctx.enter_context(nc.sbuf_tensor("ca_" + n, s, d))
        sig = lambda n, per, credit=0, step=1: Signal(ctx, nc, "ca_" + n, per, credit, step)
        ctx_b = sb("ctx_b", [CTX, SK])
        q_sb = sb("q", [P, 2, S])
        k_diag = sb("k_diag", [P, 2, 2, SK])
        v_sb = sb("v", [SK, 2, P])
        probs = sb("probs", [P, 2, QT, 2, SK])
        turned = sb("turned", [SK, 2, S])
        att = sb("att", [P, NPAIR, S])
        hat = sb("hat", [P, QT, D])
        full = sb("full", [P, S])
        full_tail = sb("full_tail", [DT, S])
        hi, lo, tail = sb("y_hi", [P, S], F32R), sb("y_lo", [P, S], F32R), sb("y_tail", [3 * DT, S], F32R)
        top = sb("top", [P, 2, 2 * QT])
        total = sb("total", [P, 2, 2 * QT])
        inverse = sb("inverse", [P, 2, 2 * QT])

        b_proj, b_kv, b_turn, b_out = banks[0], banks[1], banks[2:4], banks[4:6]
        b_scores = banks.pair(6)
        used = 2 * 2 * SK
        scores_ap = b_scores[:, :, 0:used]
        ln = Norm(ctx, nc, "ca_ln_", x, hat, hi, lo, tail, full, full_tail, *norm_args, [b_proj, b_kv])

        s_zero = sig("diag_cleared", 1)
        s_ctx = sig("ctx_copied", 1)
        s_noted = ctx.enter_context(nc.semaphore("ca_use_noted"))
        s_q = sig("q_projected", NPAIR, 2)
        s_kv = sig("kv_projected", NPAIR, 2)
        s_qsb = sig("q_copied", NPAIR, 2)
        s_ksb = sig("k_copied", 3 * NPAIR, 6)
        s_scores = sig("scores_made", NPAIR, 2)
        s_max = sig("max_made", NPAIR)
        s_sub = sig("shifted", NPAIR, 2)
        s_exp = sig("exp_made", NPAIR)
        s_sum = sig("sum_made", NPAIR)
        s_inv = sig("inverse_made", NPAIR)
        s_norm = sig("probs_scaled", NPAIR)
        s_turn = sig("turned_made", 2 * NPAIR, 4)
        s_evac0 = sig("turned_copied_even", NPAIR, 1)
        s_evac1 = sig("turned_copied_odd", NPAIR, 1)
        s_pv = sig("pv_made", 2 * NPAIR, 2)
        s_att = sig("att_copied", NPAIR, 2)
        s_o = sig("out_projected", 2, 2)
        s_bias = sig("bias_added", 1)
        s_x = sig("x_updated", QT, QT)

        block = ctx.enter_context(nc.Block())

        @block.tensor
        def _(pe):
            ln.start_tensor(pe)
            for s in (s_q, s_kv, s_scores, s_turn, s_pv, s_o):
                pe.sem_inc(s.sem, s.credit)

            def turn_norm(b):
                def bank_free(i):
                    if i == 0:
                        pe.wait_ge(s_qsb.sem, s_qsb.at(b, -1))
                    else:
                        pe.wait_ge(s_ksb.sem, s_ksb.at(b, -1))
                ln.turn(pe, b, ident, bank_free)

            def project(b, j):
                if j == 0:
                    ln.ready(pe, b)
                    pe.wait_ge(s_ctx.sem, s_ctx.at(b, 0))
                pe.wait_ge(s_qsb.sem, s_qsb.at(b, j - 1))
                ln.project(pe, b_proj, w_q, j * P).then_inc(s_q.sem, 1)
                pe.wait_ge(s_ksb.sem, s_ksb.at(b, 3 * j - 1))
                pe.matmul(b_kv[:, 0:SK], w_k[:, j * P:(j + 1) * P], ctx_b[:], start=True, stop=True)
                pe.matmul(b_kv[0:SK, P:2 * P], ctx_b[:], w_v[:, j * P:(j + 1) * P], start=True, stop=True).then_inc(s_kv.sem, 1)

            def scores(b, j):
                pe.wait_ge(s_qsb.sem, s_qsb.at(b, j))
                pe.wait_ge(s_ksb.sem, s_ksb.at(b, 3 * j + 2))
                pe.wait_ge(s_sub.sem, s_sub.at(b, j - 1))
                for q in range(QT):
                    last = pe.matmul(b_scores[:, q // 2, (q % 2) * 2 * SK:(q % 2 + 1) * 2 * SK], q_sb[:, j % 2, q * P:(q + 1) * P],
                                     k_diag[:, j % 2, :, :], start=True, stop=True)
                last.then_inc(s_scores.sem, 1)

            def turns(b, j):
                pe.wait_ge(s_norm.sem, s_norm.at(b, j))
                for e in range(2):
                    s = (s_evac0, s_evac1)[e]
                    pe.wait_ge(s.sem, s.at(b, j - 1))
                    for q in range(QT):
                        last = pe.transpose(b_turn[e][0:SK, q * P:(q + 1) * P], probs[:, j % 2, q, e, :], ident[:])
                    last.then_inc(s_turn.sem, 1)

            def pv(b, j):
                if j >= 2:
                    pe.wait_ge(s_att.sem, s_att.at(b, j - 2))
                else:
                    pe.wait_ge(s_x.sem, s_x.at(b, 2 * j + 1 - QT))
                for e in range(2):
                    s = (s_evac0, s_evac1)[e]
                    pe.wait_ge(s.sem, s.at(b, j))
                    pe.matmul(b_out[j % 2][e * HD:(e + 1) * HD, :], v_sb[:, j % 2, e * HD:(e + 1) * HD],
                              turned[:, e, :], start=True, stop=True).then_inc(s_pv.sem, 1)

            def project_out(b):
                for half in range(2):
                    for t in range(2):
                        q = 2 * half + t
                        for j in range(NPAIR):
                            if q == 0:
                                pe.wait_ge(s_att.sem, s_att.at(b, NPAIR - 2 if j < NPAIR - 1 else NPAIR - 1))
                            last = pe.matmul(b_out[half][:, t * D:(t + 1) * D], att[:, j, q * P:(q + 1) * P],
                                             w_o[:, j, :], start=(j == 0), stop=(j == NPAIR - 1))
                    last.then_inc(s_o.sem, 1)

            pe.wait_ge(s_zero.sem, 1)
            turn_norm(0)
            project(0, 0)
            scores(0, 0)
            project(0, 1)

            def batch(b, more):
                for j in range(NPAIR):
                    if j + 1 < NPAIR:
                        scores(b, j + 1)
                    elif more:
                        scores(b + 1, 0)
                    turns(b, j)
                    if j + 2 < NPAIR:
                        project(b, j + 2)
                    elif more:
                        project(b + 1, j + 2 - NPAIR)
                    pv(b, j)
                    if more and j == NPAIR - 3:
                        turn_norm(b + 1)
                project_out(b)

            over_batches(pe, batch)

        @block.scalar
        def _(act):
            ln.start_scalar(act)
            for s in (s_qsb, s_evac0, s_att):
                act.sem_inc(s.sem, s.credit)

            def operands_free(b):
                def wait(eng):
                    eng.wait_ge(s_q.sem, s_q.at(b, -1))
                return wait

            def copy_q(b, j):
                act.wait_ge(s_q.sem, s_q.at(b, j))
                act.wait_ge(s_scores.sem, s_scores.at(b, j - 2))
                act.activation(q_sb[:, j % 2, :], b_proj, ACT.Copy, scale=SCALE1).then_inc(s_qsb.sem, 1)

            def exps(b, j):
                act.wait_ge(s_sub.sem, s_sub.at(b, j))
                p = probs[:, j % 2, :, :, :].rearrange("p a b c -> p (a b c)")
                act.activation(p, p, ACT.Exp).then_inc(s_exp.sem, 1)

            def copy_turned(b, j):
                act.wait_ge(s_turn.sem, s_turn.at(b, 2 * j))
                act.wait_ge(s_pv.sem, s_pv.at(b, 2 * j - 2))
                act.copy(turned[:, 0, :], b_turn[0][0:SK, :]).then_inc(s_evac0.sem, 1)

            def copy_att(b, j):
                act.wait_ge(s_pv.sem, s_pv.at(b, 2 * j + 1))
                act.wait_ge(s_o.sem, s_o.at(b, -1))
                act.copy(att[:, j, :], b_out[j % 2]).then_inc(s_att.sem, 1)

            ln.scale_and_round(act, 0, operands_free(0))
            copy_q(0, 0)
            copy_q(0, 1)
            exps(0, 0)

            def batch(b, more):
                for j in range(NPAIR):
                    copy_turned(b, j)
                    if j + 1 < NPAIR:
                        exps(b, j + 1)
                    elif more:
                        exps(b + 1, 0)
                    if j + 2 < NPAIR:
                        copy_q(b, j + 2)
                    elif more:
                        copy_q(b + 1, j + 2 - NPAIR)
                    copy_att(b, j)
                    if more and j == NPAIR - 3:
                        ln.scale_and_round(act, b + 1, operands_free(b + 1))

            over_batches(act, batch)

        @block.vector
        def _(dve):
            ln.start_vector(dve)
            for s in (s_ksb, s_sub, s_evac1, s_x):
                dve.sem_inc(s.sem, s.credit)
            dve.memset(k_diag[:], 0.0).then_inc(s_zero.sem, 1)
            dve.wait_ge(s_zero.sem, 1)

            def operands_free(b):
                def wait(eng):
                    eng.wait_ge(s_q.sem, s_q.at(b, -1))
                return wait

            def copy_kv(b, j):
                dve.wait_ge(s_kv.sem, s_kv.at(b, j))
                dve.wait_ge(s_scores.sem, s_scores.at(b, j - 2))
                for e in range(2):
                    rows = slice(e * HD, (e + 1) * HD)
                    dve.tensor_copy(k_diag[rows, j % 2, e, :], b_kv[rows, 0:SK]).then_inc(s_ksb.sem, 1)
                dve.wait_ge(s_pv.sem, s_pv.at(b, 2 * j - 3))
                dve.tensor_copy(v_sb[:, j % 2, :], b_kv[0:SK, P:2 * P]).then_inc(s_ksb.sem, 1)

            def shift(b, j):
                s4 = scores_ap.rearrange("p a (c k) -> p a c k", k=SK)
                p = probs[:, j % 2, :, :, :].rearrange("p (a q) e k -> p a (q e) k", a=2)
                m = top[:, j % 2, :]
                dve.wait_ge(s_scores.sem, s_scores.at(b, j))
                dve.tensor_reduce(m, s4, AX_X, ALU.max).then_inc(s_max.sem, 1)
                dve.wait_ge(s_max.sem, s_max.at(b, j))
                dve.wait_ge(s_turn.sem, s_turn.at(b, 2 * j - 3))
                dve.tensor_tensor(p, s4, m.rearrange("p (a c) -> p a c", a=2).unsqueeze(3).broadcast_to([P, 2, QT, SK]),
                                  ALU.subtract).then_inc(s_sub.sem, 1)

            def scale(b, j):
                p = probs[:, j % 2, :, :, :].rearrange("p q e k -> p (q e) k")
                dve.wait_ge(s_exp.sem, s_exp.at(b, j))
                dve.tensor_reduce(total[:, j % 2, :], p, AX_X, ALU.add).then_inc(s_sum.sem, 1)
                dve.wait_ge(s_sum.sem, s_sum.at(b, j))
                dve.reciprocal(inverse[:, j % 2, :], total[:, j % 2, :]).then_inc(s_inv.sem, 1)
                dve.wait_ge(s_inv.sem, s_inv.at(b, j))
                dve.tensor_tensor(p, p, inverse[:, j % 2, :].unsqueeze(2).broadcast_to([P, 2 * QT, SK]), ALU.mult).then_inc(s_norm.sem, 1)

            def copy_turned(b, j):
                dve.wait_ge(s_turn.sem, s_turn.at(b, 2 * j + 1))
                dve.wait_ge(s_pv.sem, s_pv.at(b, 2 * j - 1))
                dve.tensor_copy(turned[:, 1, :], b_turn[1][0:SK, :]).then_inc(s_evac1.sem, 1)

            def update(b):
                dve.wait_ge(s_bias.sem, s_bias.at(b, 0))
                for half in range(2):
                    dve.wait_ge(s_o.sem, s_o.at(b, half))
                    for t in range(2):
                        xt = x[:, bass.ds(b * QT + 2 * half + t, 1), :].rearrange("p a d -> p (a d)")
                        dve.tensor_tensor(xt, b_out[half][:, t * D:(t + 1) * D], xt, ALU.add).then_inc(s_x.sem, 1)

            ln.statistics(dve, 0)
            ln.standardize(dve, 0)
            ln.remainder(dve, 0, operands_free(0))
            copy_kv(0, 0)
            copy_kv(0, 1)
            shift(0, 0)
            scale(0, 0)

            def batch(b, more):
                for j in range(NPAIR):
                    if j + 1 < NPAIR:
                        shift(b, j + 1)
                    elif more:
                        shift(b + 1, 0)
                    copy_turned(b, j)
                    if j + 1 < NPAIR:
                        scale(b, j + 1)
                    elif more:
                        scale(b + 1, 0)
                    if j + 2 < NPAIR:
                        copy_kv(b, j + 2)
                    elif more:
                        copy_kv(b + 1, j + 2 - NPAIR)
                    if more and j == LN_AT:
                        ln.statistics(dve, b + 1)
                    if more and j == LN_AT + 1:
                        ln.standardize(dve, b + 1)
                    if more and j == NPAIR - 3:
                        ln.remainder(dve, b + 1, operands_free(b + 1))
                update(b)

            over_batches(dve, batch)

        @block.gpsimd
        def _(pool):
            ln.start_gpsimd(pool)

            def prepare(b):
                ln.deviations(pool, b)
                pool.wait_ge(ln.s_hat.sem, ln.s_hat.at(b, QT - 1))
                xt = x[:, bass.ds(b * QT, QT), :]
                pool.tensor_tensor(xt, xt, bias_o[:].unsqueeze(1).broadcast_to([P, QT, D]), ALU.add).then_inc(s_bias.sem, 1)
                pool.wait_ge(s_kv.sem, s_kv.at(b, -1))
                pool.sem_inc(s_noted, 1)
                pool.tensor_copy(ctx_b[:], ctx_t[:, bass.ds(b, 1), :].rearrange("p a k -> p (a k)")).then_inc(s_ctx.sem, 1)

            with pool.Fori(0, B) as b:
                prepare(b)


def feedfwd(nc, x, ident, norm_args, w_1, b_1, w_2, bias_o, banks, out):
    with ExitStack() as ctx:
        sb = lambda n, s, d=F32: ctx.enter_context(nc.sbuf_tensor("ff_" + n, s, d))
        sig = lambda n, per, credit=0, step=1: Signal(ctx, nc, "ff_" + n, per, credit, step)
        gate = sb("gate", [P, 2, S])
        h = sb("h", [P, NF, S])
        hat = sb("hat", [P, QT, D])
        full = sb("full", [P, S])
        full_tail = sb("full_tail", [DT, S])
        hi, lo, tail = sb("y_hi", [P, S], F32R), sb("y_lo", [P, S], F32R), sb("y_tail", [3 * DT, S], F32R)

        b_gate, b_a, b_out, b_ln = banks[0:2], banks[2:4], banks[4:6], banks[6:8]
        ln = Norm(ctx, nc, "ff_ln_", x, hat, hi, lo, tail, full, full_tail, *norm_args, b_ln)

        s_g = sig("gate_projected", NF)
        s_a = sig("a_projected", NF, 1)
        s_gelu = sig("gelu_made", NF, 1)
        s_h = sig("h_made", NF, 2)
        s_o = sig("out_projected", 2, 1)
        s_bias = sig("bias_added", 1)
        s_x = sig("x_updated", QT, QT)
        s_out = sig("out_stored", 1, 0, 16)
        s_noted = ctx.enter_context(nc.semaphore("ff_x_noted"))

        block = ctx.enter_context(nc.Block())

        @block.tensor
        def _(pe):
            ln.start_tensor(pe)
            for s in (s_a, s_o):
                pe.sem_inc(s.sem, s.credit)

            def turn_norm(b):
                ln.turn(pe, b, ident, lambda i: pe.wait_ge(ln.s_full.sem, ln.s_full.at(b, i - 2)))

            turn_norm(0)

            def batch(b, more):
                ln.ready(pe, b)
                for m in range(NF):
                    before = max(m - 2, -1)
                    pe.wait_ge(s_gelu.sem, s_gelu.at(b, before))
                    ln.project(pe, b_gate[m % 2], w_1, DFF + m * P).then_inc(s_g.sem, 1)
                    pe.wait_ge(s_h.sem, s_h.at(b, before))
                    ln.project(pe, b_a[m % 2], w_1, m * P).then_inc(s_a.sem, 1)
                if more:
                    turn_norm(b + 1)
                for half in range(2):
                    pe.wait_ge(s_x.sem, s_x.at(b, 2 * half + 1 - QT))
                    for t in range(2):
                        q = 2 * half + t
                        for m in range(NF):
                            if q == 0:
                                pe.wait_ge(s_h.sem, s_h.at(b, m))
                            last = pe.matmul(b_out[half][:, t * D:(t + 1) * D], h[:, m, q * P:(q + 1) * P],
                                             w_2[:, m, :], start=(m == 0), stop=(m == NF - 1))
                    last.then_inc(s_o.sem, 1)

            over_batches(pe, batch)

        @block.scalar
        def _(act):
            ln.start_scalar(act)
            act.sem_inc(s_gelu.sem, 1)

            def operands_free(b):
                return lambda eng: eng.wait_ge(s_a.sem, s_a.at(b, -1))

            ln.scale_and_round(act, 0, operands_free(0))

            def batch(b, more):
                for m in range(NF):
                    act.wait_ge(s_g.sem, s_g.at(b, m))
                    act.wait_ge(s_h.sem, s_h.at(b, max(m - 2, -1)))
                    act.activation(gate[:, m % 2, :], b_gate[m % 2], ACT.Gelu_apprx_tanh, bias=b_1[:, NF + m:NF + m + 1]).then_inc(s_gelu.sem, 1)
                if more:
                    ln.scale_and_round(act, b + 1, operands_free(b + 1))

            over_batches(act, batch)

        @block.vector
        def _(dve):
            ln.start_vector(dve)
            for s in (s_h, s_x):
                dve.sem_inc(s.sem, s.credit)

            def operands_free(b):
                return lambda eng: eng.wait_ge(s_a.sem, s_a.at(b, -1))

            ln.statistics(dve, 0)
            ln.standardize(dve, 0)
            ln.remainder(dve, 0, operands_free(0))

            def batch(b, more):
                if more:
                    ln.statistics(dve, b + 1)
                    ln.standardize(dve, b + 1)
                for m in range(NF):
                    dve.wait_ge(s_a.sem, s_a.at(b, m))
                    dve.wait_ge(s_gelu.sem, s_gelu.at(b, m))
                    dve.wait_ge(s_o.sem, s_o.at(b, -1))
                    dve.scalar_tensor_tensor(out=h[:, m, :], in0=b_a[m % 2], scalar=b_1[:, m:m + 1], in1=gate[:, m % 2, :],
                                             op0=ALU.add, op1=ALU.mult).then_inc(s_h.sem, 1)
                if more:
                    ln.remainder(dve, b + 1, operands_free(b + 1))
                dve.wait_ge(s_bias.sem, s_bias.at(b, 0))
                for half in range(2):
                    dve.wait_ge(s_o.sem, s_o.at(b, half))
                    for t in range(2):
                        xt = x[:, bass.ds(b * QT + 2 * half + t, 1), :].rearrange("p a d -> p (a d)")
                        dve.tensor_tensor(xt, b_out[half][:, t * D:(t + 1) * D], xt, ALU.add).then_inc(s_x.sem, 1)

            over_batches(dve, batch)

        @block.gpsimd
        def _(pool):
            ln.start_gpsimd(pool)

            with pool.Fori(0, B) as b:
                ln.deviations(pool, b)
                pool.wait_ge(ln.s_hat.sem, ln.s_hat.at(b, QT - 1))
                xt = x[:, bass.ds(b * QT, QT), :]
                pool.tensor_tensor(xt, xt, bias_o[:].unsqueeze(1).broadcast_to([P, QT, D]), ALU.add).then_inc(s_bias.sem, 1)

        @block.sync
        def _(sp):
            tiles = out.rearrange("b (q p) d -> p (b q) d", p=P)
            with sp.Fori(0, B) as b:
                sp.wait_ge(s_x.sem, s_x.at(b, QT - 1))
                sp.sem_inc(s_noted, 1)
                sp.dma_start(tiles[:, bass.ds(b * QT, QT), :], x[:, bass.ds(b * QT, QT), :]).then_inc(s_out.sem, 16)
            sp.wait_ge(s_out.sem, s_out.at(B - 1, 0))


class Banks:

    def __init__(self, psum):
        self.psum = psum

    def __getitem__(self, i):
        if isinstance(i, slice):
            return [self.psum[:, k, :] for k in range(*i.indices(8))]
        return self.psum[:, i, :]

    def pair(self, i):
        return self.psum[:, i:i + 2, :]


def build(nc, t, out):
    w = lambda n: t["L1_xattn_" + n]
    with ExitStack() as ctx:
        psum = ctx.enter_context(nc.psum_tensor("banks", [P, 8, 512], F32))
        banks = Banks(psum)
        keep = lambda n, s, d=F32: ctx.enter_context(nc.sbuf_tensor(n, s, d))
        x = keep("x", [P, B * QT, D])
        ident = keep("ident", [P, P])
        ctx_t = keep("ctx_t", [CTX, B, SK])
        bias = {n: keep(n, [P, D]) for n in ("bo1", "bo2", "b_ff2")}
        gains = {n: keep(n, [P, 2]) for n in ("g1", "be1", "g2", "be2", "g3", "be3")}
        b_1 = keep("b_1", [P, 2 * NF])
        s_ld = ctx.enter_context(nc.semaphore("constants_loaded"))
        wa, wb, wc = (Split(ctx, nc, f"w{c}_") for c in "abc")
        with nc.Block() as block:
            @block.sync
            def _(sp):
                n = 0
                columns = [(b_1[:, m:m + 1], w("b_ff1")[m * P:(m + 1) * P].unsqueeze(1)) for m in range(2 * NF)]
                for to, src in [(x[:], t["x"].rearrange("b (q p) d -> p (b q) d", p=P)), (ident[:], t["ident"])] + columns:
                    sp.dma_start(to, src).then_inc(s_ld, 16)
                    n += 1
                for name, to in bias.items():
                    sp.dma_start(to[:], w(name).unsqueeze(0).broadcast_to([P, D])).then_inc(s_ld, 16)
                    n += 1
                for name, to in gains.items():
                    sp.dma_start(to[:, 0:1], w(name)[0:P].unsqueeze(1)).then_inc(s_ld, 16)
                    sp.dma_start(to[0:DT, 1:2], w(name)[P:D].unsqueeze(1)).then_inc(s_ld, 16)
                    n += 2
                sp.wait_ge(s_ld, n * 16)
        adapter(nc, t, x, ident, ctx_t, banks)

        def load(name, pairs):
            s = ctx.enter_context(nc.semaphore(name))
            with nc.Block() as block:
                @block.sync
                def _(sp):
                    for to, src in pairs:
                        sp.dma_start(to, src).then_inc(s, 16)
                    sp.wait_ge(s, 16 * len(pairs))

        def split(name, jobs):
            with ExitStack() as st:
                raw = st.enter_context(nc.sbuf_tensor(name + "raw", [P, 2, INNER], F32))
                raw_tail = st.enter_context(nc.sbuf_tensor(name + "raw_tail", [3 * DT, 2, INNER], F32))
                split_weights(ctx, nc, name, jobs, raw, raw_tail)

        pairs = lambda ap: ap.rearrange("(j p) d -> p j d", p=P)
        split("sa_", [(w("wq1"), wa), (w("wk1"), wb), (w("wv1"), wc)])
        with nc.sbuf_tensor("w_o1", [P, NPAIR, D], F32) as w_o1:
            load("wo1_loaded", [(w_o1[:], pairs(w("wo1")))])
            selfattn(nc, x, ident, (gains["g1"], gains["be1"]), wa, wb, wc, w_o1, bias["bo1"], banks)
        split("ca_", [(w("wq2"), wa), (w("w_ff1"), wb)])
        with nc.sbuf_tensor("w_o2", [P, NPAIR, D], F32) as w_o2, nc.sbuf_tensor("w_k2", [CTX, INNER], F32) as w_k2, \
                nc.sbuf_tensor("w_v2", [CTX, INNER], F32) as w_v2:
            load("crossattn_weights_loaded", [(w_o2[:], pairs(w("wo2"))), (w_k2[:], w("wk2")), (w_v2[:], w("wv2"))])
            crossattn(nc, x, ident, (gains["g2"], gains["be2"]), ctx_t, wa, w_k2, w_v2, w_o2, bias["bo2"], banks)
        with nc.sbuf_tensor("w_2", [P, NF, D], F32) as w_2:
            load("feedfwd_weights_loaded", [(w_2[:], pairs(w("w_ff2")))])
            feedfwd(nc, x, ident, (gains["g3"], gains["be3"]), wb, b_1, w_2, bias["b_ff2"], banks, out)


def kernel(**inputs):
    import concourse.bacc as bacc
    from concourse.bass_utils import run_bass_kernel_spmd

    nc = bacc.Bacc("TRN2", target_bir_lowering=False, num_devices=1)
    arrays = {"in_" + n: np.ascontiguousarray(a) for n, a in inputs.items()}
    arrays["in_ident"] = np.eye(P, dtype=np.float32)
    repeated = np.linspace(0, CTX - 1, S).astype(np.int64)
    arrays["in_expand"] = (np.arange(CTX)[:, None] == repeated[None, :]).astype(np.float32)
    arrays["in_own"] = (np.arange(H0 * NCA)[:, None] // NCA == np.arange(H0 * HP)[None, :] // HP).astype(np.float32)
    t = {n[3:]: nc.dram_tensor(n, a.shape, F32, kind="ExternalInput").ap() for n, a in arrays.items()}
    out = nc.dram_tensor("out", (B, S, D), F32, kind="ExternalOutput").ap()
    build(nc, t, out)
    r = run_bass_kernel_spmd(nc, [arrays], core_ids=[0])
    return r.results[0]["out"]
```

```python
from contextlib import ExitStack

import numpy as np

import concourse.bass as bass
from concourse import mybir

F32 = mybir.dt.float32
F32R = mybir.dt.float32r
ALU = mybir.AluOpType
ACT = mybir.ActivationFunctionType
AX_X = mybir.AxisListType.X

B, S, D = 4, 512, 160
P = 128
QT = S // P
DT = D - P
SK, CTX = 77, 96
NCA = 4
SE = SK - NCA
H0, HD0, HP = 8, 20, 32
G = H0 * HP // P
HG = H0 // G
H1, HD = 20, 64
INNER = H1 * HD
NPAIR = H1 // 2
DFF = 640
NF = DFF // P
EPS = 1e-5
SCALE0 = float(HD0) ** -0.5
SCALE1 = float(HD) ** -0.5


class Signal:

    def __init__(self, ctx, nc, name, per, credit=0, step=1):
        self.sem = ctx.enter_context(nc.semaphore(name))
        self.per, self.credit, self.step = per, credit, step

    def at(self, b, k):
        return (b * self.per + (k + 1) + self.credit) * self.step


def over_batches(eng, body, peel=True):
    if not peel:
        with eng.Fori(0, B) as b:
            body(b, False)
        return
    with eng.Fori(0, B - 1) as b:
        body(b, True)
    body(B - 1, False)


class Norm:

    def __init__(self, ctx, nc, name, x, hat, hi, lo, tail, full, full_tail, gain, shift, banks):
        self.nc, self.x, self.hat = nc, x, hat
        self.hi, self.lo, self.tail = hi, lo, tail
        self.full, self.full_tail, self.gain, self.shift = full, full_tail, gain, shift
        self.banks = banks
        sb = lambda n, s: ctx.enter_context(nc.sbuf_tensor(name + n, s, F32))
        self.stats = sb("stats", [P, QT, 6])
        self.moments = sb("moments", [P, QT, 2])
        self.veps = sb("veps", [P, QT])
        self.half = sb("half", [P, QT])
        self.eps = sb("eps", [P, QT])
        self.rstd = sb("rstd", [P, QT])
        sig = lambda n, per, credit=0: Signal(ctx, nc, name + n, per, credit)
        self.s_stats = sig("stats_made", QT)
        self.s_noted = ctx.enter_context(nc.semaphore(name + "stats_noted"))
        self.s_moments = sig("moments_made", QT)
        self.s_half = sig("constants_set", 2)
        self.s_veps = sig("veps_made", 1)
        self.s_rstd = sig("rstd_made", 1)
        self.s_hat = sig("hat_made", QT)
        self.s_turned = sig("turned", 2, 2)
        self.s_full = sig("full_made", 2, 2)
        self.s_hi = sig("hi_made", 3, 3)
        self.s_lo = sig("lo_made", 2, 2)

    def start_gpsimd(self, pool):
        pool.memset(self.half[:], -0.5).then_inc(self.s_half.sem, 1)
        pool.memset(self.eps[:], EPS).then_inc(self.s_half.sem, 1)
        pool.wait_ge(self.s_half.sem, 2)

    def start_tensor(self, pe):
        pe.sem_inc(self.s_turned.sem, 2)

    def start_scalar(self, act):
        act.sem_inc(self.s_full.sem, 2)
        act.sem_inc(self.s_hi.sem, 3)

    def start_vector(self, dve):
        dve.sem_inc(self.s_lo.sem, 2)

    def statistics(self, dve, b):
        for q in range(QT):
            dve.bn_stats(self.stats[:, q, :], self.x[:, bass.ds(b * QT + q, 1), :].rearrange("p a d -> p (a d)")).then_inc(self.s_stats.sem, 1)
        dve.wait_ge(self.s_stats.sem, self.s_stats.at(b, QT - 1))
        dve.sem_inc(self.s_noted, 1)
        for q in range(QT):
            dve.bn_aggr(self.moments[:, q, :], self.stats[:, q, :]).then_inc(self.s_moments.sem, 1)

    def deviations(self, pool, b):
        pool.wait_ge(self.s_moments.sem, self.s_moments.at(b, QT - 1))
        pool.tensor_tensor(self.veps[:], self.moments[:, :, 1], self.eps[:], ALU.add).then_inc(self.s_veps.sem, 1)
        pool.wait_ge(self.s_veps.sem, self.s_veps.at(b, 0))
        pool.tensor_tensor(self.rstd[:], self.veps[:], self.half[:], ALU.pow).then_inc(self.s_rstd.sem, 1)

    def standardize(self, dve, b):
        dve.wait_ge(self.s_rstd.sem, self.s_rstd.at(b, 0))
        dve.wait_ge(self.s_turned.sem, self.s_turned.at(b, -1))
        for q in range(QT):
            dve.tensor_scalar(self.hat[:, q, :], self.x[:, bass.ds(b * QT + q, 1), :].rearrange("p a d -> p (a d)"),
                              self.moments[:, q, 0:1], self.rstd[:, q:q + 1], ALU.subtract, ALU.mult).then_inc(self.s_hat.sem, 1)

    def turn(self, pe, b, ident, bank_free):
        pe.wait_ge(self.s_hat.sem, self.s_hat.at(b, QT - 1))
        bank_free(0)
        for q in range(QT):
            last = pe.transpose(self.banks[0][:, q * P:(q + 1) * P], self.hat[:, q, 0:P], ident[:])
        last.then_inc(self.s_turned.sem, 1)
        bank_free(1)
        for q in range(QT):
            last = pe.transpose(self.banks[1][0:DT, q * P:(q + 1) * P], self.hat[:, q, P:D], ident[:])
        last.then_inc(self.s_turned.sem, 1)

    def scale_and_round(self, act, b, operands_free):
        act.wait_ge(self.s_turned.sem, self.s_turned.at(b, 0))
        act.wait_ge(self.s_lo.sem, self.s_lo.at(b, -1))
        act.wait_ge(self.s_hi.sem, self.s_hi.at(b, -1))
        act.activation(self.full[:], self.banks[0], ACT.Identity, bias=self.shift[:, 0:1], scale=self.gain[:, 0:1]).then_inc(self.s_full.sem, 1)
        act.wait_ge(self.s_turned.sem, self.s_turned.at(b, 1))
        act.activation(self.full_tail[:], self.banks[1][0:DT, :], ACT.Identity, bias=self.shift[0:DT, 1:2], scale=self.gain[0:DT, 1:2]).then_inc(self.s_full.sem, 1)
        operands_free(act)
        act.wait_ge(self.s_full.sem, self.s_full.at(b, 0))
        act.copy(self.hi[:], self.full[:]).then_inc(self.s_hi.sem, 1)
        act.wait_ge(self.s_full.sem, self.s_full.at(b, 1))
        act.copy(self.tail[0:DT, :], self.full_tail[:]).then_inc(self.s_hi.sem, 1)
        act.copy(self.tail[2 * DT:3 * DT, :], self.full_tail[:]).then_inc(self.s_hi.sem, 1)

    def remainder(self, dve, b, operands_free):
        operands_free(dve)
        dve.wait_ge(self.s_hi.sem, self.s_hi.at(b, 0))
        dve.tensor_tensor(self.lo[:], self.full[:], self.hi[:].bitcast(F32), ALU.subtract).then_inc(self.s_lo.sem, 1)
        dve.wait_ge(self.s_hi.sem, self.s_hi.at(b, 1))
        dve.tensor_tensor(self.tail[DT:2 * DT, :], self.full_tail[:], self.tail[0:DT, :].bitcast(F32), ALU.subtract).then_inc(self.s_lo.sem, 1)

    def ready(self, pe, b):
        pe.wait_ge(self.s_hi.sem, self.s_hi.at(b, 2))
        pe.wait_ge(self.s_lo.sem, self.s_lo.at(b, 1))

    def project(self, pe, bank, w, c0, n=P):
        c = slice(c0, c0 + n)
        pe.matmul(bank, w.hi[:, c], self.hi[:], start=True, stop=False)
        pe.matmul(bank, w.hi[:, c], self.lo[:], start=False, stop=False)
        pe.matmul(bank, w.lo[:, c], self.hi[:], start=False, stop=False)
        return pe.matmul(bank, w.tail[:, c], self.tail[:], start=False, stop=True)

    def project_tokens(self, pe, bank, w, c0, q, n=P):
        c, t = slice(c0, c0 + n), slice(q * P, (q + 1) * P)
        pe.matmul(bank, self.hi[:, t], w.hi[:, c], start=True, stop=False)
        pe.matmul(bank, self.lo[:, t], w.hi[:, c], start=False, stop=False)
        pe.matmul(bank, self.hi[:, t], w.lo[:, c], start=False, stop=False)
        return pe.matmul(bank, self.tail[:, t], w.tail[:, c], start=False, stop=True)


class Raw:

    def __init__(self, ctx, nc, name):
        self.main = ctx.enter_context(nc.sbuf_tensor(name + "main", [P, INNER], F32))
        self.tail = ctx.enter_context(nc.sbuf_tensor(name + "tail", [3 * DT, INNER], F32))


class Split:

    LOADS, ROUNDED, REST = 4, 2, 2

    def __init__(self, ctx, nc, name):
        sb = lambda n, s: ctx.enter_context(nc.sbuf_tensor(name + n, s, F32R))
        self.hi, self.lo, self.tail = sb("hi", [P, INNER]), sb("lo", [P, INNER]), sb("tail", [3 * DT, INNER])

    @staticmethod
    def load(sp, w, raw, loaded):
        sp.dma_start(raw.main[:], w[0:P, :]).then_inc(loaded, 16)
        for r in range(3):
            sp.dma_start(raw.tail[r * DT:(r + 1) * DT, :], w[P:D, :]).then_inc(loaded, 16)

    def round(self, act, raw, c, rounded):
        act.copy(self.hi[:, c], raw.main[:, c]).then_inc(rounded, 1)
        act.copy(self.tail[:, c], raw.tail[:, c]).then_inc(rounded, 1)

    def rest(self, dve, raw, c, made):
        low = slice(2 * DT, 3 * DT)
        dve.tensor_tensor(self.lo[:, c], raw.main[:, c], self.hi[:, c].bitcast(F32), ALU.subtract).then_inc(made, 1)
        dve.tensor_tensor(self.tail[low, c], raw.tail[low, c], self.tail[low, c].bitcast(F32), ALU.subtract).then_inc(made, 1)


def selfattn(nc, x, ident, norm_args, w_q, w_k, w_v, w_o, bias_o, banks, next_w_q, raw):
    LEAD, LAG = 6, 2
    NB = H1 * QT
    PAIRB = 2 * QT
    V_BUF = (0, 1, 2, 0, 1)
    V_BEFORE = (3 - 5, 4 - 5, 2 - 5, 0, 1)
    PS = 4
    TS = 4
    LN_AT = 44
    TURN_AT = (NPAIR - 3) * PAIRB + 7
    PROJECT_AT, ROUND_AT, REST_AT = {0: 0, 1: 1, 5: 2}, {1: 0, 2: 1, 6: 2}, {2: 0, 3: 1}
    with ExitStack() as ctx:
        sb = lambda n, s, d=F32: ctx.enter_context(nc.sbuf_tensor("sa_" + n, s, d))
        sig = lambda n, per, credit=0, step=1: Signal(ctx, nc, "sa_" + n, per, credit, step)
        q_stack = sb("q_stack", [P, 2, 2, S], F32R)
        k_stack = sb("k_stack", [P, 2, 2, 2, S], F32R)
        q_parts = sb("q_parts", [P, 2, S], F32R)
        k_parts = sb("k_parts", [P, 2, S], F32R)
        v = sb("v", [P, 3, QT, 2 * P])
        probs = sb("probs", [P, PS, QT, S])
        turned = sb("turned", [P, TS, S])
        att = sb("att", [P, NPAIR, S])
        hat = sb("hat", [P, QT, D])
        full = sb("full", [P, S])
        full_tail = sb("full_tail", [DT, S])
        hi, lo, tail = sb("y_hi", [P, S], F32R), sb("y_lo", [P, S], F32R), sb("y_tail", [3 * DT, S], F32R)
        negmax = sb("negmax", [P, 4 * QT])
        total = sb("total", [P, 4 * QT])
        inverse = sb("inverse", [P, 4 * QT])

        b_scores, b_turn, b_out, b_proj = banks[0:2], banks[2:4], banks[4:6], banks[6:8]
        ln = Norm(ctx, nc, "sa_ln_", x, hat, hi, lo, tail, full, full_tail, *norm_args, b_proj)

        s_q = sig("q_projected", NPAIR, 2)
        s_k = sig("k_projected", NPAIR, 2)
        s_v = sig("v_projected", NPAIR, 2)
        s_qhi = sig("q_rounded", NPAIR)
        s_khi = sig("k_rounded", NPAIR)
        s_qlo = sig("q_rest", NPAIR, 2)
        s_klo = sig("k_rest", NPAIR, 2)
        s_vsb = sig("v_copied", NPAIR, 2)
        s_stack = [sig(f"stacked{i}", NPAIR // 2, 0, 8 * 16) for i in range(2)]
        s_scores = sig("scores_made", NB, 8 * QT)
        s_max = sig("max_made", NB)
        s_exp = sig("exp_made", NB, 4 * QT)
        s_inv = sig("inverse_made", NB)
        s_norm = sig("probs_scaled", NB)
        s_noted = ctx.enter_context(nc.semaphore("sa_inverse_noted"))
        s_noted_sp = ctx.enter_context(nc.semaphore("sa_parts_noted"))
        s_turn = sig("turned_made", NB, 4 * QT)
        s_evac = sig("turned_copied", NB * 3 // 4, 3)
        s_evac_act = sig("turned_copied_act", NB // 4, 1)
        s_pv = sig("pv_made", NB, 6 * QT * 2)
        s_att = sig("att_copied", NPAIR, 2)
        s_o = sig("out_projected", 2, 2)
        s_bias = sig("bias_added", 1)
        s_x = sig("x_updated", QT, QT)
        s_next, s_rounded, s_rest = (ctx.enter_context(nc.semaphore("sa_next_w_q_" + n)) for n in ("loaded", "rounded", "rest"))
        every = slice(0, INNER)

        def wait_turned_copied(eng, b, n):
            g, k = divmod(n, 4)
            if k == 3:
                eng.wait_ge(s_evac_act.sem, s_evac_act.at(b, g))
            else:
                eng.wait_ge(s_evac.sem, s_evac.at(b, 3 * g + k))

        block = ctx.enter_context(nc.Block())

        @block.sync
        def _(sp):
            def stack(b, j):
                s = j % 2
                places = [(e, slice(e * HD, (e + 1) * HD), half, slice(half * HD, (half + 1) * HD)) for e in range(2) for half in range(2)]
                sp.wait_ge(s_scores.sem, s_scores.at(b, PAIRB * (j - 1) - 1))
                sp.sem_inc(s_noted_sp, 1)
                sp.wait_ge(s_qlo.sem, s_qlo.at(b, j))
                for e, rows, half, to in places:
                    sp.dma_start(q_stack[to, s, e, :].bitcast(F32), q_parts[rows, half, :].bitcast(F32)).then_inc(s_stack[s].sem, 16)
                sp.sem_inc(s_noted_sp, 1)
                sp.wait_ge(s_klo.sem, s_klo.at(b, j))
                for e, rows, half, to in places:
                    sp.dma_start(k_stack[to, s, e, :, :].bitcast(F32), k_parts[rows, :, :].bitcast(F32)).then_inc(s_stack[s].sem, 16)

            stack(0, 0)
            stack(0, 1)

            def batch(b, more):
                for j in range(2, NPAIR):
                    stack(b, j)
                if more:
                    stack(b + 1, 0)
                    stack(b + 1, 1)
                else:
                    sp.wait_ge(s_q.sem, s_q.at(b, NPAIR - 1))
                    w_q.load(sp, next_w_q, raw, s_next)

            over_batches(sp, batch)

        @block.tensor
        def _(pe):
            ln.start_tensor(pe)
            for s in (s_q, s_k, s_v, s_scores, s_turn, s_pv, s_o):
                pe.sem_inc(s.sem, s.credit)

            def turn_norm(b):
                def bank_free(i):
                    if i == 0:
                        pe.wait_ge(s_vsb.sem, s_vsb.at(b, -1))
                    else:
                        pe.wait_ge(s_klo.sem, s_klo.at(b, -1))
                ln.turn(pe, b, ident, bank_free)

            def project(b, j, what):
                if j == 0 and what == 0:
                    ln.ready(pe, b)
                if what == 0:
                    if j > 0:
                        pe.wait_ge(s_vsb.sem, s_vsb.at(b, j - 1))
                    ln.project(pe, b_proj[0], w_q, j * P).then_inc(s_q.sem, 1)
                elif what == 1:
                    if j > 0:
                        pe.wait_ge(s_klo.sem, s_klo.at(b, j - 1))
                    ln.project(pe, b_proj[1], w_k, j * P).then_inc(s_k.sem, 1)
                else:
                    pe.wait_ge(s_qlo.sem, s_qlo.at(b, j))
                    for t in range(2):
                        last = ln.project_tokens(pe, b_proj[0][:, t * 2 * P:(t + 1) * 2 * P], w_v, j // 2 * 2 * P, j % 2 * 2 + t, 2 * P)
                    last.then_inc(s_v.sem, 1)

            def scores(b, n):
                h, q = divmod(n, QT)
                j, e = divmod(h, 2)
                if n % PAIRB == 0:
                    pe.wait_ge(s_stack[j % 2].sem, s_stack[j % 2].at(b, j // 2))
                pe.wait_ge(s_exp.sem, s_exp.at(b, n - 2))
                lhs = q_stack[:, j % 2, e, q * P:(q + 1) * P]
                bank = b_scores[n % 2]
                pe.matmul(bank, lhs, k_stack[:, j % 2, e, 0, :], start=True, stop=False)
                pe.matmul(bank, lhs, k_stack[:, j % 2, e, 1, :], start=False, stop=True).then_inc(s_scores.sem, 1)

            def turns(b, n):
                h, k = divmod(n, QT)
                if k == 0:
                    pe.wait_ge(s_norm.sem, s_norm.at(b, QT * h + QT - 1))
                wait_turned_copied(pe, b, n - 2)
                for q in range(QT):
                    last = pe.transpose(b_turn[n % 2][:, q * P:(q + 1) * P], probs[:, h % PS, q, k * P:(k + 1) * P], ident[:])
                last.then_inc(s_turn.sem, 1)

            def pv(b, n):
                h, k = divmod(n, QT)
                j, e = divmod(h, 2)
                wait_turned_copied(pe, b, n)
                if n % PAIRB == 0:
                    pe.wait_ge(s_vsb.sem, s_vsb.at(b, j | 1))
                    if j >= 2:
                        pe.wait_ge(s_att.sem, s_att.at(b, j - 2))
                    else:
                        pe.wait_ge(s_x.sem, s_x.at(b, 2 * j - 1 - QT + 2))
                pe.matmul(b_out[j % 2][e * HD:(e + 1) * HD, :], v[:, V_BUF[j // 2], k, j % 2 * P + e * HD:j % 2 * P + (e + 1) * HD],
                          turned[:, n % TS, :], start=(k == 0), stop=(k == QT - 1)).then_inc(s_pv.sem, 1)

            def project_out(b, half):
                if half == 0:
                    pe.wait_ge(s_att.sem, s_att.at(b, NPAIR - 2))
                else:
                    pe.wait_ge(s_att.sem, s_att.at(b, NPAIR - 1))
                for t in range(2):
                    q = 2 * half + t
                    for j in range(NPAIR):
                        if half == 0 and t == 0 and j == NPAIR - 1:
                            pe.wait_ge(s_att.sem, s_att.at(b, NPAIR - 1))
                        last = pe.matmul(b_out[half][:, t * D:(t + 1) * D], att[:, j, q * P:(q + 1) * P],
                                         w_o[:, j, :], start=(j == 0), stop=(j == NPAIR - 1))
                last.then_inc(s_o.sem, 1)

            turn_norm(0)
            for what in range(3):
                project(0, 0, what)
            scores(0, 0)
            for what in range(3):
                project(0, 1, what)
            for n in range(1, LEAD):
                scores(0, n)

            def batch(b, more):
                for n in range(NB):
                    m = n + LEAD
                    if m < NB:
                        scores(b, m)
                    elif more:
                        scores(b + 1, m - NB)
                    if n >= LAG:
                        pv(b, n - LAG)
                    turns(b, n)
                    if n % PAIRB in PROJECT_AT:
                        j, what = n // PAIRB + 2, PROJECT_AT[n % PAIRB]
                        if j < NPAIR:
                            project(b, j, what)
                        elif more:
                            project(b + 1, j - NPAIR, what)
                    if n == TURN_AT and more:
                        turn_norm(b + 1)
                for n in range(NB - LAG, NB):
                    pv(b, n)
                project_out(b, 0)
                project_out(b, 1)

            over_batches(pe, batch)

        @block.scalar
        def _(act):
            ln.start_scalar(act)
            for s in (s_vsb, s_exp, s_att, s_evac_act):
                act.sem_inc(s.sem, s.credit)

            def operands_free(b):
                def wait(eng):
                    eng.wait_ge(s_v.sem, s_v.at(b, -1))
                return wait

            def round_part(b, j, what):
                if what == 0:
                    act.wait_ge(s_q.sem, s_q.at(b, j))
                    if j >= 1:
                        act.wait_ge(s_stack[(j - 1) % 2].sem, s_stack[(j - 1) % 2].at(b, (j - 1) // 2))
                    else:
                        act.wait_ge(s_scores.sem, s_scores.at(b, -PAIRB))
                    act.activation(q_parts[:, 0, :], b_proj[0], ACT.Copy, scale=SCALE1).then_inc(s_qhi.sem, 1)
                elif what == 1:
                    act.wait_ge(s_k.sem, s_k.at(b, j))
                    act.copy(k_parts[:, 0, :], b_proj[1]).then_inc(s_khi.sem, 1)
                else:
                    act.wait_ge(s_v.sem, s_v.at(b, j))
                    act.wait_ge(s_pv.sem, s_pv.at(b, 2 * PAIRB * (V_BEFORE[j // 2] + 1) - 1))
                    act.copy(v[:, V_BUF[j // 2], j % 2 * 2:j % 2 * 2 + 2, :].rearrange("p a c -> p (a c)"), b_proj[0]).then_inc(s_vsb.sem, 1)

            def exps(b, n):
                h, q = divmod(n, QT)
                c = n % (4 * QT)
                act.wait_ge(s_max.sem, s_max.at(b, n))
                if q == 0:
                    act.wait_ge(s_turn.sem, s_turn.at(b, QT * (h - PS) + QT - 1))
                act.activation(probs[:, h % PS, q, :], b_scores[n % 2], ACT.Exp, bias=negmax[:, c:c + 1],
                               accum_out=total[:, c:c + 1]).then_inc(s_exp.sem, 1)

            def copy_att(b, j):
                act.wait_ge(s_pv.sem, s_pv.at(b, PAIRB * j + PAIRB - 1))
                act.wait_ge(s_o.sem, s_o.at(b, -1))
                act.copy(att[:, j, :], b_out[j % 2]).then_inc(s_att.sem, 1)

            def copy_turned(b, n):
                act.wait_ge(s_turn.sem, s_turn.at(b, n))
                act.wait_ge(s_pv.sem, s_pv.at(b, n - TS))
                act.copy(turned[:, n % TS, :], b_turn[n % 2]).then_inc(s_evac_act.sem, 1)

            ln.scale_and_round(act, 0, operands_free(0))
            for what in range(3):
                round_part(0, 0, what)
            exps(0, 0)
            for what in range(3):
                round_part(0, 1, what)
            for n in range(1, LEAD):
                exps(0, n)

            def batch(b, more):
                for n in range(NB):
                    m = n + LEAD
                    if m < NB:
                        exps(b, m)
                    elif more:
                        exps(b + 1, m - NB)
                    if n % 4 == 3:
                        copy_turned(b, n)
                    if n % PAIRB in ROUND_AT:
                        j, what = n // PAIRB + 2, ROUND_AT[n % PAIRB]
                        if j < NPAIR:
                            round_part(b, j, what)
                        elif more:
                            round_part(b + 1, j - NPAIR, what)
                    if n % PAIRB == LAG + 1 and n > PAIRB:
                        copy_att(b, n // PAIRB - 1)
                    if n == TURN_AT and more:
                        ln.scale_and_round(act, b + 1, operands_free(b + 1))
                    if not more and n == NB - 10:
                        act.wait_ge(s_next, 16 * Split.LOADS)
                        w_q.round(act, raw, every, s_rounded)
                copy_att(b, NPAIR - 1)

            over_batches(act, batch)

        @block.vector
        def _(dve):
            ln.start_vector(dve)
            for s in (s_qlo, s_klo, s_evac, s_x):
                dve.sem_inc(s.sem, s.credit)

            def operands_free(b):
                def wait(eng):
                    eng.wait_ge(s_v.sem, s_v.at(b, -1))
                return wait

            def rest(b, j, what):
                if what == 0:
                    dve.wait_ge(s_qhi.sem, s_qhi.at(b, j))
                    dve.scalar_tensor_tensor(out=q_parts[:, 1, :], in0=b_proj[0], scalar=SCALE1, in1=q_parts[:, 0, :].bitcast(F32),
                                             op0=ALU.mult, op1=ALU.subtract).then_inc(s_qlo.sem, 1)
                else:
                    dve.wait_ge(s_khi.sem, s_khi.at(b, j))
                    dve.tensor_tensor(k_parts[:, 1, :], b_proj[1], k_parts[:, 0, :].bitcast(F32), ALU.subtract).then_inc(s_klo.sem, 1)

            def maxima(b, n):
                c = n % (4 * QT)
                dve.wait_ge(s_scores.sem, s_scores.at(b, n))
                dve.tensor_reduce(negmax[:, c:c + 1], b_scores[n % 2], AX_X, ALU.max, negate=True).then_inc(s_max.sem, 1)

            def inverses(b, n):
                c = n % (4 * QT)
                dve.wait_ge(s_exp.sem, s_exp.at(b, n))
                dve.reciprocal(inverse[:, c:c + 1], total[:, c:c + 1]).then_inc(s_inv.sem, 1)

            def copy_turned(b, n):
                dve.wait_ge(s_turn.sem, s_turn.at(b, n))
                dve.wait_ge(s_pv.sem, s_pv.at(b, n - TS))
                dve.tensor_copy(turned[:, n % TS, :], b_turn[n % 2]).then_inc(s_evac.sem, 1)

            def update(b):
                for half in range(2):
                    dve.wait_ge(s_o.sem, s_o.at(b, half))
                    if half == 0:
                        dve.wait_ge(s_bias.sem, s_bias.at(b, 0))
                    for t in range(2):
                        xt = x[:, bass.ds(b * QT + 2 * half + t, 1), :].rearrange("p a d -> p (a d)")
                        dve.tensor_tensor(xt, b_out[half][:, t * D:(t + 1) * D], xt, ALU.add).then_inc(s_x.sem, 1)

            ln.statistics(dve, 0)
            ln.standardize(dve, 0)
            ln.remainder(dve, 0, operands_free(0))
            for what in range(2):
                rest(0, 0, what)
            maxima(0, 0)
            for what in range(2):
                rest(0, 1, what)
            for n in range(1, LEAD):
                maxima(0, n)
                inverses(0, n - 1)

            def batch(b, more):
                for n in range(NB):
                    m = n + LEAD
                    if m < NB:
                        maxima(b, m)
                    elif more:
                        maxima(b + 1, m - NB)
                    if m - 1 < NB:
                        inverses(b, m - 1)
                    elif more:
                        inverses(b + 1, m - 1 - NB)
                    if n % 4 != 3:
                        copy_turned(b, n)
                    if n % PAIRB in REST_AT:
                        j, what = n // PAIRB + 2, REST_AT[n % PAIRB]
                        if j < NPAIR:
                            rest(b, j, what)
                        elif more:
                            rest(b + 1, j - NPAIR, what)
                    if more and n == LN_AT:
                        ln.statistics(dve, b + 1)
                    if more and n == LN_AT + 4:
                        ln.standardize(dve, b + 1)
                    if n == TURN_AT + 1 and more:
                        ln.remainder(dve, b + 1, operands_free(b + 1))
                if not more:
                    dve.wait_ge(s_rounded, Split.ROUNDED)
                    w_q.rest(dve, raw, every, s_rest)
                update(b)

            over_batches(dve, batch)

        @block.gpsimd
        def _(pool):
            ln.start_gpsimd(pool)

            def scale(b, n):
                h, q = divmod(n, QT)
                c = n % (4 * QT)
                pool.wait_ge(s_inv.sem, s_inv.at(b, n))
                pool.sem_inc(s_noted, 1)
                pool.tensor_scalar(probs[:, h % PS, q, :], probs[:, h % PS, q, :], inverse[:, c:c + 1], 1.0,
                                   ALU.mult, ALU.mult).then_inc(s_norm.sem, 1)

            def add_bias(b):
                pool.wait_ge(ln.s_hat.sem, ln.s_hat.at(b, QT - 1))
                xt = x[:, bass.ds(b * QT, QT), :]
                pool.tensor_tensor(xt, xt, bias_o[:].unsqueeze(1).broadcast_to([P, QT, D]), ALU.add).then_inc(s_bias.sem, 1)

            ln.deviations(pool, 0)
            add_bias(0)
            for n in range(LEAD - 1):
                scale(0, n)

            def batch(b, more):
                for n in range(NB):
                    m = n + LEAD - 1
                    if m < NB:
                        scale(b, m)
                    elif more:
                        scale(b + 1, m - NB)
                    if more and n == LN_AT + 2:
                        ln.deviations(pool, b + 1)
                    if more and n == LN_AT + 8:
                        add_bias(b + 1)

            over_batches(pool, batch)


def adapter(nc, t, x, ident, ctx_t, banks, splits, later):
    w = lambda n: t["L0_xattn_" + n]
    with ExitStack() as ctx:
        sb = lambda n, s, d=F32: ctx.enter_context(nc.sbuf_tensor("ad_" + n, s, d))
        sig = lambda n, per, credit=0, step=1: Signal(ctx, nc, "ad_" + n, per, credit, step)
        N1 = 4
        HC = H0 * HP
        wq = sb("wq", [P, G, H0, HP])
        wo = sb("wo", [P, G, D])
        wk, wv, wk_ca, wv_ca = (sb(n, [CTX, H0, HP]) for n in ("wk", "wv", "wk_ca", "wv_ca"))
        wq_ca = sb("wq_ca", [NCA, H0, HP])
        b_o = sb("b_out", [P, D])
        expand = sb("expand", [CTX, S])
        own = sb("own", [H0 * NCA, HC])
        context = sb("context", [SK, CTX])
        tokens = sb("tokens", [NCA, CTX])
        x_pad = sb("x_pad", [P, QT, H0, HP])
        x_t = sb("x_t", [P, G, S])
        c_t = sb("c_t", [CTX, SK])
        c_rep = sb("c_rep", [CTX, H0, NCA])
        q_t = sb("q_t", [P, G, S])
        q1_diag = sb("q1_diag", [P, H0, CTX])
        k_diag = sb("k_diag", [P, G, HG, SE])
        k2_diag = sb("k2_diag", [P, G, HG, NCA])
        v = sb("v", [SE, HC])
        v2 = sb("v2", [H0 * NCA, HC])
        probs = sb("probs", [P, QT, G, HG, SE])
        turned = sb("turned", [SE, 2, S])
        probs1 = sb("probs1", [CTX, N1, S])
        turned1 = sb("turned1", [P, 2, QT, CTX])
        hs1 = sb("hs1", [P, G, CTX])
        q2 = sb("q2", [P, G, CTX])
        probs2 = sb("probs2", [CTX, H0, NCA])
        probs2x = sb("probs2x", [H0 * NCA, S])
        heads = sb("heads", [P, G, S])
        negmax1, total1, inverse1 = (sb(n, [CTX, N1]) for n in ("negmax1", "total1", "inverse1"))
        top, total, inverse = (sb(n, [P, QT * G, HG]) for n in ("top", "total", "inverse"))
        top2, total2, inverse2 = (sb(n, [CTX, H0]) for n in ("top2", "total2", "inverse2"))
        raws = [Raw(ctx, nc, f"ad_raw{i}_") for i in range(len(splits))]
        columns = lambda b: bass.ds(b * (INNER // B), INNER // B)
        flat = lambda tile: tile.rearrange("p a b -> p (a b)")

        NU = QT * G
        b_q1, b_k = banks[7][:, P:P + G * CTX], banks[7][:, P + G * CTX:P + G * CTX + G * SK]
        s_in, s_w, s_wq, s_wo, s_raw, s_later = (ctx.enter_context(nc.semaphore(f"ad_{n}_loaded")) for n in
                                                 ("x", "weights", "wq", "out_weights", "raw", "later"))
        s_rounded = sig("weights_rounded", Split.ROUNDED * len(splits))
        s_rest = sig("weights_rest", Split.REST * len(splits))
        s_zero = ctx.enter_context(nc.semaphore("ad_cleared"))
        s_ctx = sig("context_loaded", 2, 0, 16)
        s_noted = ctx.enter_context(nc.semaphore("ad_noted"))
        s_noted_pool = ctx.enter_context(nc.semaphore("ad_noted_pool"))
        s_noted_dve = ctx.enter_context(nc.semaphore("ad_noted_dve"))
        s_pad = sig("x_padded", 1)
        s_bias = sig("bias_added", 1)
        s_xturn = sig("x_turned", G)
        s_xt = sig("x_t_copied", G)
        s_cturn = sig("c_turned", 1)
        s_ct = sig("c_t_copied", 1)
        s_ctall = sig("c_t_kept", 1)
        s_crep = sig("c_rep_made", 1)
        s_q1p = sig("q1_projected", 1)
        s_q1 = sig("q1_placed", HG)
        s_kp = sig("k_projected", 1)
        s_kd = sig("k_placed", 2 * HG)
        s_vp = sig("v_projected", 1)
        s_vd = sig("v_placed", 2)
        s_qp = sig("q_projected", G)
        s_q = sig("q_copied", G)
        s_s1 = sig("scores1_made", H0)
        s_max1 = sig("max1_made", H0)
        s_exp1 = sig("exp1_made", H0)
        s_inv1 = sig("inverse1_made", H0)
        s_norm1 = sig("probs1_scaled", H0)
        s_turn1 = sig("turned1_made", H0, N1)
        s_evac1 = sig("turned1_copied", H0, 2)
        s_pv1 = sig("pv1_made", H0, 2)
        s_s = sig("scores_made", NU)
        s_max = sig("max_made", NU)
        s_sub = sig("shifted", NU)
        s_exp = sig("exp_made", NU)
        s_sum = sig("sum_made", NU)
        s_inv = sig("inverse_made", NU)
        s_norm = sig("probs_scaled", NU)
        s_hs1 = sig("hs1_copied", 1)
        s_q2p = sig("q2_projected", 1)
        s_q2 = sig("q2_copied", 1)
        s_s2 = sig("scores2_made", 1)
        s_soft2 = sig("softmax2_steps", 6)
        s_px = sig("probs2_expanded", 1)
        s_p2x = sig("probs2x_copied", 1)
        s_turn = sig("turned_made", H0, 1)
        s_evac = [sig(f"turned_copied{i}", H0 // 2, 1) for i in range(2)]
        s_pv = sig("pv_made", H0, 2)
        s_add2 = sig("adapter_added", G, G)
        s_heads = sig("heads_copied", G)
        s_o = sig("out_projected", 2, 1)
        s_x = sig("x_updated", QT, QT)
        N_W, N_WO = 6, H0 + 2

        block = ctx.enter_context(nc.Block())

        @block.sync
        def _(sp):
            rows = t["ctx_768"]

            def load_context(b):
                sp.dma_start(context[:], rows[bass.ds(b, 1), :, :].rearrange("a k c -> (a k) c")).then_inc(s_ctx.sem, 16)
                sp.dma_start(tokens[:], rows[bass.ds(b, 1), SE:SK, :].rearrange("a k c -> (a k) c")).then_inc(s_ctx.sem, 16)

            sp.dma_start(x[:], t["x"].rearrange("b (q p) d -> p (b q) d", p=P)).then_inc(s_in, 16)
            sp.dma_start(ident[:], t["ident"]).then_inc(s_in, 16)
            load_context(0)
            sp.dma_start(own[:], t["own"]).then_inc(s_w, 16)
            sp.wait_ge(s_zero, 11)
            by_head = lambda ap: ap.rearrange("r (h c) -> r h c", h=H0)
            for tile, name in ((wq_ca, "Wq_ca"), (wk, "Wk"), (wk_ca, "Wk_ca"), (wv, "Wv"), (wv_ca, "Wv_ca")):
                sp.dma_start(tile[:, :, 0:HD0], by_head(w(name))).then_inc(s_w, 16)
            to = lambda h: slice(HP * (h % HG), HP * (h % HG) + HD0)
            for h in range(H0):
                sp.dma_start(wq[to(h), h // HG, :, 0:HD0], by_head(w("Wq")[h * HD0:(h + 1) * HD0, :])).then_inc(s_wq, 16)
            sp.dma_start(b_o[:], w("b_out").unsqueeze(0).broadcast_to([P, D])).then_inc(s_wo, 16)
            sp.dma_start(expand[:], t["expand"]).then_inc(s_wo, 16)
            for h in range(H0):
                sp.dma_start(wo[to(h), h // HG, :], w("Wout")[h * HD0:(h + 1) * HD0, :]).then_inc(s_wo, 16)
            for (weight, parts), raw in zip(splits, raws):
                parts.load(sp, weight, raw, s_raw)
            for tile, src in later:
                sp.dma_start(tile, src).then_inc(s_later, 16)
            with sp.Fori(1, B) as b:
                sp.wait_ge(s_vp.sem, s_vp.at(b, -1))
                sp.sem_inc(s_noted, 1)
                load_context(b)
            sp.wait_ge(s_later, 16 * len(later))

        @block.tensor
        def _(pe):
            for s in (s_turn1, s_pv1, s_turn, s_pv, s_add2, s_o):
                pe.sem_inc(s.sem, s.credit)
            pe.wait_ge(s_in, 32)

            def turn_inputs(b):
                pe.wait_ge(s_ctx.sem, s_ctx.at(b, 1))
                pe.transpose(banks[7][0:CTX, 0:SK], context[:], ident[0:SK, 0:SK]).then_inc(s_cturn.sem, 1)
                pe.wait_ge(s_pad.sem, s_pad.at(b, 0))
                for g in range(G):
                    for q in range(QT):
                        last = pe.transpose(banks[2 + g][:, q * P:(q + 1) * P], x_pad[:, q, g * HG:(g + 1) * HG, :].rearrange("p h c -> p (h c)"), ident[:])
                    last.then_inc(s_xturn.sem, 1)

            def project_context(b):
                pe.wait_ge(s_w, 16 * N_W)
                pe.wait_ge(s_ct.sem, s_ct.at(b, 0))
                for g in range(G):
                    pe.matmul(b_q1[:, g * CTX:(g + 1) * CTX], flat(wq_ca[:, g * HG:(g + 1) * HG, :]), tokens[:], start=True, stop=True)
                for g in range(G):
                    cols = slice(g * HG, (g + 1) * HG)
                    pe.matmul(b_k[:, g * SE:(g + 1) * SE], flat(wk[:, cols, :]), c_t[:, 0:SE], start=True, stop=True)
                    last = pe.matmul(b_k[:, G * SE + g * NCA:G * SE + (g + 1) * NCA], flat(wk_ca[:, cols, :]), c_t[:, SE:SK], start=True, stop=True)
                last.then_inc(s_kp.sem, 1)
                pe.wait_ge(s_crep.sem, s_crep.at(b, 0))
                pe.matmul(banks[4][0:SE, 0:HC], c_t[:, 0:SE], flat(wv[:]), start=True, stop=True)
                pe.matmul(banks[4][0:H0 * NCA, HC:2 * HC], flat(c_rep[:]), flat(wv_ca[:]), start=True, stop=True).then_inc(s_vp.sem, 1)

            def project_queries(b):
                pe.wait_ge(s_wq, 16 * H0)
                pe.wait_ge(s_xt.sem, s_xt.at(b, G - 1))
                for g in range(G):
                    for k in range(G):
                        last = pe.matmul(banks[2 + g], flat(wq[:, k, g * HG:(g + 1) * HG, :]), x_t[:, k, :], start=(k == 0), stop=(k == G - 1))
                    last.then_inc(s_qp.sem, 1)

            turn_inputs(0)
            project_context(0)
            project_queries(0)

            def batch(b, more):
                def scores1(h):
                    if h == 0:
                        pe.wait_ge(s_q1.sem, s_q1.at(b, HG - 1))
                    if h >= 2:
                        pe.wait_ge(s_exp1.sem, s_exp1.at(b, h - 2))
                    pe.matmul(banks[h % 2][0:CTX, :], q1_diag[:, h, :], x_t[:, h // HG, :], start=True, stop=True).then_inc(s_s1.sem, 1)

                def scores(u):
                    q, g = divmod(u, G)
                    if u == 0:
                        pe.wait_ge(s_q.sem, s_q.at(b, G - 1))
                        pe.wait_ge(s_kd.sem, s_kd.at(b, 2 * HG - 1))
                        pe.wait_ge(s_x.sem, s_x.at(b, -1))
                    if u >= 2:
                        pe.wait_ge(s_sub.sem, s_sub.at(b, u - 2))
                    pe.matmul(banks[5 + g][:, 0:HG * SE], q_t[:, g, q * P:(q + 1) * P], k_diag[:, g, :, :].rearrange("p h k -> p (h k)"),
                              start=True, stop=True).then_inc(s_s.sem, 1)

                def turns1(h):
                    pe.wait_ge(s_norm1.sem, s_norm1.at(b, h))
                    if h >= 2:
                        pe.wait_ge(s_evac1.sem, s_evac1.at(b, h - 2))
                    for k in range(QT):
                        last = pe.transpose(banks[2 + h % 2][:, k * CTX:(k + 1) * CTX], probs1[:, h % N1, k * P:(k + 1) * P], ident[0:CTX, 0:CTX])
                    last.then_inc(s_turn1.sem, 1)

                def pv1(h):
                    g, j = divmod(h, HG)
                    pe.wait_ge(s_evac1.sem, s_evac1.at(b, h))
                    for k in range(QT):
                        last = pe.matmul(banks[7][j * HP:(j + 1) * HP, g * CTX:(g + 1) * CTX], x_pad[:, k, h, :], turned1[:, h % 2, k, :],
                                         start=(k == 0), stop=(k == QT - 1))
                    last.then_inc(s_pv1.sem, 1)

                for i in range(H0 + 4):
                    if i < H0:
                        scores1(i)
                        scores(i)
                    if 3 <= i < H0 + 3:
                        turns1(i - 3)
                    if i >= 4:
                        pv1(i - 4)

                def turns(h):
                    if h == 0:
                        pe.wait_ge(s_norm.sem, s_norm.at(b, NU - 1))
                        pe.wait_ge(s_evac1.sem, s_evac1.at(b, H0 - 1))
                    elif h >= 2:
                        pe.wait_ge(s_evac[h % 2].sem, s_evac[h % 2].at(b, h // 2 - 1))
                    for q in range(QT):
                        last = pe.transpose(banks[2 + h % 2][0:SE, q * P:(q + 1) * P], probs[:, q, h // HG, h % HG, :], ident[:])
                    last.then_inc(s_turn.sem, 1)

                def pv(h):
                    g, j = divmod(h, HG)
                    pe.wait_ge(s_evac[h % 2].sem, s_evac[h % 2].at(b, h // 2))
                    pe.matmul(banks[g][j * HP:(j + 1) * HP, :], v[:, h * HP:(h + 1) * HP], turned[:, h % 2, :],
                              start=True, stop=False, skip_group_check=True).then_inc(s_pv.sem, 1)

                turns(0)
                pe.wait_ge(s_hs1.sem, s_hs1.at(b, 0))
                for g in range(G):
                    for k in range(G):
                        last = pe.matmul(banks[7][:, g * CTX:(g + 1) * CTX], flat(wq[:, k, g * HG:(g + 1) * HG, :]), hs1[:, k, :], start=(k == 0), stop=(k == G - 1))
                last.then_inc(s_q2p.sem, 1)
                turns(1)
                pv(0)
                pe.wait_ge(s_q2.sem, s_q2.at(b, 0))
                for g in range(G):
                    last = pe.matmul(banks[7][0:CTX, g * HG * NCA:(g + 1) * HG * NCA], q2[:, g, :], k2_diag[:, g, :, :].rearrange("p h k -> p (h k)"), start=True, stop=True)
                last.then_inc(s_s2.sem, 1)
                for h in range(2, H0):
                    turns(h)
                    pv(h - 1)
                pv(H0 - 1)
                pe.wait_ge(s_wo, 16 * N_WO)
                pe.wait_ge(s_soft2.sem, s_soft2.at(b, 5))
                pe.matmul(banks[4][0:H0 * NCA, :], flat(probs2[:]), expand[:], start=True, stop=True).then_inc(s_px.sem, 1)
                if more:
                    turn_inputs(b + 1)
                pe.wait_ge(s_p2x.sem, s_p2x.at(b, 0))
                for g in range(G):
                    pe.matmul(banks[g], v2[:, g * P:(g + 1) * P], probs2x[:], start=False, stop=True, skip_group_check=True).then_inc(s_add2.sem, 1)
                if more:
                    project_context(b + 1)
                for half in range(2):
                    for i in range(2):
                        q = 2 * half + i
                        for g in range(G):
                            if q == 0:
                                pe.wait_ge(s_heads.sem, s_heads.at(b, g))
                            last = pe.matmul(banks[5 + half][:, i * D:(i + 1) * D], heads[:, g, q * P:(q + 1) * P], wo[:, g, :], start=(g == 0), stop=(g == G - 1))
                    last.then_inc(s_o.sem, 1)
                if more:
                    project_queries(b + 1)

            over_batches(pe, batch)

        @block.scalar
        def _(act):
            act.sem_inc(s_evac1.sem, s_evac1.credit)
            act.sem_inc(s_evac[0].sem, s_evac[0].credit)

            def copy_context(b):
                act.wait_ge(s_cturn.sem, s_cturn.at(b, 0))
                if not isinstance(b, int) or b > 0:
                    act.wait_ge(s_vp.sem, s_vp.at(b, -1))
                    act.wait_ge(s_ctall.sem, s_ctall.at(b, -1))
                act.copy(c_t[:], banks[7][0:CTX, 0:SK]).then_inc(s_ct.sem, 1)

            def copy_x(b):
                for g in range(G):
                    act.wait_ge(s_xturn.sem, s_xturn.at(b, g))
                    act.copy(x_t[:, g, :], banks[2 + g]).then_inc(s_xt.sem, 1)

            def copy_queries(b):
                for g in range(G):
                    act.wait_ge(s_qp.sem, s_qp.at(b, g))
                    act.activation(q_t[:, g, :], banks[2 + g], ACT.Copy, scale=SCALE0).then_inc(s_q.sem, 1)

            copy_context(0)
            copy_x(0)
            copy_queries(0)

            def batch(b, more):
                def exp1(h):
                    act.wait_ge(s_max1.sem, s_max1.at(b, h))
                    act.wait_ge(s_turn1.sem, s_turn1.at(b, h - N1))
                    act.activation(probs1[:, h % N1, :], banks[h % 2][0:CTX, :], ACT.Exp, bias=negmax1[:, h % N1:h % N1 + 1],
                                   accum_out=total1[:, h % N1:h % N1 + 1]).then_inc(s_exp1.sem, 1)

                def exp(u):
                    q, g = divmod(u, G)
                    act.wait_ge(s_sub.sem, s_sub.at(b, u))
                    p = probs[:, q, g, :, :].rearrange("p h k -> p (h k)")
                    act.activation(p, p, ACT.Exp).then_inc(s_exp.sem, 1)

                def copy_turned1(h):
                    act.wait_ge(s_turn1.sem, s_turn1.at(b, h))
                    act.wait_ge(s_pv1.sem, s_pv1.at(b, h - 2))
                    act.copy(turned1[:, h % 2, :, :].rearrange("p k c -> p (k c)"), banks[2 + h % 2][:, 0:QT * CTX]).then_inc(s_evac1.sem, 1)

                for i in range(H0 + 3):
                    if i < H0:
                        exp1(i)
                        exp(i)
                    if i >= 3:
                        copy_turned1(i - 3)
                act.wait_ge(s_pv1.sem, s_pv1.at(b, H0 - 1))
                act.copy(flat(hs1[:]), banks[7][:, 0:G * CTX]).then_inc(s_hs1.sem, 1)

                for h in range(0, H0, 2):
                    act.wait_ge(s_turn.sem, s_turn.at(b, h))
                    act.wait_ge(s_pv.sem, s_pv.at(b, h - 2))
                    act.copy(turned[:, h % 2, :], banks[2 + h % 2][0:SE, :]).then_inc(s_evac[0].sem, 1)
                    if h == 0:
                        act.wait_ge(s_q2p.sem, s_q2p.at(b, 0))
                        act.activation(flat(q2[:]), banks[7][:, 0:G * CTX], ACT.Copy, scale=SCALE0).then_inc(s_q2.sem, 1)
                    if h == 2:
                        act.wait_ge(s_soft2.sem, s_soft2.at(b, 1))
                        act.activation(flat(probs2[:]), flat(probs2[:]), ACT.Exp).then_inc(s_soft2.sem, 1)
                act.wait_ge(s_px.sem, s_px.at(b, 0))
                act.wait_ge(s_add2.sem, s_add2.at(b, -1))
                act.copy(probs2x[:], banks[4][0:H0 * NCA, :]).then_inc(s_p2x.sem, 1)
                if more:
                    copy_context(b + 1)
                    copy_x(b + 1)
                act.wait_ge(s_o.sem, s_o.at(b, -1))
                for g in range(G):
                    act.wait_ge(s_add2.sem, s_add2.at(b, g))
                    act.copy(heads[:, g, :], banks[g]).then_inc(s_heads.sem, 1)
                if more:
                    copy_queries(b + 1)
                act.wait_ge(s_raw, 16 * Split.LOADS * len(splits))
                for (_, parts), raw in zip(splits, raws):
                    parts.round(act, raw, columns(b), s_rounded.sem)

            over_batches(act, batch)

        @block.vector
        def _(dve):
            dve.sem_inc(s_x.sem, s_x.credit)
            dve.sem_inc(s_evac[1].sem, s_evac[1].credit)
            for tile in (q1_diag, k_diag, k2_diag):
                dve.memset(tile[:], 0.0).then_inc(s_zero, 1)
            dve.wait_ge(s_zero, 11)
            dve.wait_ge(s_in, 32)

            def pad_x(b):
                xb = x[:, bass.ds(b * QT, QT), :]
                dve.wait_ge(s_pv1.sem, s_pv1.at(b, -1))
                dve.sem_inc(s_noted_dve, 1)
                dve.tensor_copy(x_pad[:, :, :, 0:HD0].rearrange("p q h c -> p (q h) c"),
                                xb.rearrange("p q (h c) -> p (q h) c", h=H0)).then_inc(s_pad.sem, 1)

            def repeat_context(b):
                dve.wait_ge(s_ct.sem, s_ct.at(b, 0))
                dve.tensor_copy(c_rep[:], c_t[:, SE:SK].unsqueeze(1).broadcast_to([CTX, H0, NCA])).then_inc(s_crep.sem, 1)

            def place_context(b):
                dve.wait_ge(s_kp.sem, s_kp.at(b, 0))
                for j in range(HG):
                    rows = slice(j * HP, (j + 1) * HP)
                    dve.tensor_scalar(q1_diag[rows, j::HG, :], b_q1[rows, :].rearrange("p (g c) -> p g c", g=G),
                                      SCALE0, None, ALU.mult).then_inc(s_q1.sem, 1)
                for j in range(HG):
                    rows = slice(j * HP, (j + 1) * HP)
                    dve.tensor_copy(k_diag[rows, :, j, :], b_k[rows, 0:G * SE].rearrange("p (g k) -> p g k", g=G)).then_inc(s_kd.sem, 1)
                    dve.tensor_copy(k2_diag[rows, :, j, :], b_k[rows, G * SE:G * (SE + NCA)].rearrange("p (g k) -> p g k", g=G)).then_inc(s_kd.sem, 1)
                dve.wait_ge(s_vp.sem, s_vp.at(b, 0))
                dve.wait_ge(s_add2.sem, s_add2.at(b, -1))
                dve.wait_ge(s_w, 16 * N_W)
                dve.tensor_copy(v[:], banks[4][0:SE, 0:HC]).then_inc(s_vd.sem, 1)
                dve.tensor_tensor(v2[:], banks[4][0:H0 * NCA, HC:2 * HC], own[:], ALU.mult).then_inc(s_vd.sem, 1)

            pad_x(0)
            repeat_context(0)
            place_context(0)

            def batch(b, more):
                def max1(h):
                    dve.wait_ge(s_s1.sem, s_s1.at(b, h))
                    dve.tensor_reduce(negmax1[:, h % N1:h % N1 + 1], banks[h % 2][0:CTX, :], AX_X, ALU.max, negate=True).then_inc(s_max1.sem, 1)

                def inverses1(h):
                    dve.wait_ge(s_exp1.sem, s_exp1.at(b, h))
                    dve.reciprocal(inverse1[:, h % N1:h % N1 + 1], total1[:, h % N1:h % N1 + 1]).then_inc(s_inv1.sem, 1)

                def shift(u):
                    q, g = divmod(u, G)
                    s3 = banks[5 + g][:, 0:HG * SE].rearrange("p (h k) -> p h k", h=HG)
                    dve.wait_ge(s_s.sem, s_s.at(b, u))
                    dve.tensor_reduce(top[:, u, :], s3, AX_X, ALU.max).then_inc(s_max.sem, 1)
                    dve.wait_ge(s_max.sem, s_max.at(b, u))
                    if u == 0:
                        dve.wait_ge(s_turn.sem, s_turn.at(b, -1))
                    dve.tensor_tensor(probs[:, q, g, :, :], s3, top[:, u, :].unsqueeze(2).broadcast_to([P, HG, SE]), ALU.subtract).then_inc(s_sub.sem, 1)

                def inverses(u):
                    q, g = divmod(u, G)
                    dve.wait_ge(s_exp.sem, s_exp.at(b, u))
                    dve.tensor_reduce(total[:, u, :], probs[:, q, g, :, :], AX_X, ALU.add).then_inc(s_sum.sem, 1)
                    dve.wait_ge(s_sum.sem, s_sum.at(b, u))
                    dve.reciprocal(inverse[:, u, :], total[:, u, :]).then_inc(s_inv.sem, 1)

                def copy_turned(h):
                    dve.wait_ge(s_turn.sem, s_turn.at(b, h))
                    dve.wait_ge(s_pv.sem, s_pv.at(b, h - 2))
                    dve.tensor_copy(turned[:, h % 2, :], banks[2 + h % 2][0:SE, :]).then_inc(s_evac[1].sem, 1)

                for i in range(H0 + 1):
                    if i < H0:
                        max1(i)
                        shift(i)
                    if i >= 1:
                        inverses1(i - 1)
                        inverses(i - 1)
                s3 = banks[7][0:CTX, 0:H0 * NCA].rearrange("p (h k) -> p h k", h=H0)
                spread = lambda tile: tile[:].unsqueeze(2).broadcast_to([CTX, H0, NCA])
                copy_turned(1)
                dve.wait_ge(s_s2.sem, s_s2.at(b, 0))
                dve.tensor_reduce(top2[:], s3, AX_X, ALU.max).then_inc(s_soft2.sem, 1)
                dve.wait_ge(s_soft2.sem, s_soft2.at(b, 0))
                dve.tensor_tensor(probs2[:], s3, spread(top2), ALU.subtract).then_inc(s_soft2.sem, 1)
                copy_turned(3)
                dve.wait_ge(s_soft2.sem, s_soft2.at(b, 2))
                dve.tensor_reduce(total2[:], probs2[:], AX_X, ALU.add).then_inc(s_soft2.sem, 1)
                dve.wait_ge(s_soft2.sem, s_soft2.at(b, 3))
                dve.reciprocal(inverse2[:], total2[:]).then_inc(s_soft2.sem, 1)
                dve.wait_ge(s_soft2.sem, s_soft2.at(b, 4))
                dve.tensor_tensor(probs2[:], probs2[:], spread(inverse2), ALU.mult).then_inc(s_soft2.sem, 1)
                copy_turned(5)
                if more:
                    pad_x(b + 1)
                copy_turned(7)
                if more:
                    repeat_context(b + 1)
                    place_context(b + 1)
                dve.wait_ge(s_bias.sem, s_bias.at(b, 0))
                for half in range(2):
                    dve.wait_ge(s_o.sem, s_o.at(b, half))
                    for i in range(2):
                        xt = x[:, bass.ds(b * QT + 2 * half + i, 1), :].rearrange("p a d -> p (a d)")
                        dve.tensor_tensor(xt, banks[5 + half][:, i * D:(i + 1) * D], xt, ALU.add).then_inc(s_x.sem, 1)
                for i, ((_, parts), raw) in enumerate(zip(splits, raws)):
                    dve.wait_ge(s_rounded.sem, s_rounded.at(b, Split.ROUNDED * (i + 1) - 1))
                    parts.rest(dve, raw, columns(b), s_rest.sem)

            over_batches(dve, batch)

        @block.gpsimd
        def _(pool):
            for tile in (x_pad, wq_ca, wk, wk_ca, wv, wv_ca, wq, wo):
                pool.memset(tile[:], 0.0).then_inc(s_zero, 1)
            pool.wait_ge(s_zero, 11)
            pool.wait_ge(s_in, 32)
            pool.wait_ge(s_wo, 16 * N_WO)

            def batch(b, _):
                xb = x[:, bass.ds(b * QT, QT), :]
                pool.wait_ge(s_pad.sem, s_pad.at(b, 0))
                pool.tensor_tensor(xb, xb, b_o[:].unsqueeze(1).broadcast_to([P, QT, D]), ALU.add).then_inc(s_bias.sem, 1)
                pool.wait_ge(s_ct.sem, s_ct.at(b, 0))
                pool.sem_inc(s_noted_pool, 1)
                pool.tensor_copy(ctx_t[:, bass.ds(b, 1), :].rearrange("p a k -> p (a k)"), c_t[:]).then_inc(s_ctall.sem, 1)
                for h in range(H0):
                    pool.wait_ge(s_inv1.sem, s_inv1.at(b, h))
                    pool.sem_inc(s_noted_pool, 1)
                    pool.tensor_scalar(probs1[:, h % N1, :], probs1[:, h % N1, :], inverse1[:, h % N1:h % N1 + 1], 1.0, ALU.mult, ALU.mult).then_inc(s_norm1.sem, 1)
                    q, g = divmod(h, G)
                    pool.wait_ge(s_inv.sem, s_inv.at(b, h))
                    pool.tensor_tensor(probs[:, q, g, :, :], probs[:, q, g, :, :], inverse[:, h, :].unsqueeze(2).broadcast_to([P, HG, SE]),
                                       ALU.mult).then_inc(s_norm.sem, 1)

            over_batches(pool, batch, peel=False)


def crossattn(nc, x, ident, norm_args, ctx_t, w_q, w_k, w_v, w_o, bias_o, banks, next_w, next_parts, raw, later):
    BUFS = 5
    LN_AT = 3
    with ExitStack() as ctx:
        sb = lambda n, s, d=F32: ctx.enter_context(nc.sbuf_tensor("ca_" + n, s, d))
        sig = lambda n, per, credit=0, step=1: Signal(ctx, nc, "ca_" + n, per, credit, step)
        ctx_b = sb("ctx_b", [CTX, SK])
        q_sb = sb("q", [P, BUFS, S])
        k_diag = sb("k_diag", [P, BUFS, 2, SK])
        v_sb = sb("v", [SK, BUFS, P])
        probs = sb("probs", [P, BUFS, QT, 2, SK])
        turned = sb("turned", [SK, 2, S])
        att = sb("att", [P, NPAIR, S])
        hat = sb("hat", [P, QT, D])
        full = sb("full", [P, S])
        full_tail = sb("full_tail", [DT, S])
        hi, lo, tail = sb("y_hi", [P, S], F32R), sb("y_lo", [P, S], F32R), sb("y_tail", [3 * DT, S], F32R)
        top = sb("top", [P, BUFS, 2 * QT])
        total = sb("total", [P, BUFS, 2 * QT])
        inverse = sb("inverse", [P, BUFS, 2 * QT])

        b_proj, b_kv, b_turn, b_out = banks[0], banks[1], banks[2:4], banks[4:6]
        b_scores = banks.pair(6)
        used = 2 * 2 * SK
        scores_ap = b_scores[:, :, 0:used]
        ln = Norm(ctx, nc, "ca_ln_", x, hat, hi, lo, tail, full, full_tail, *norm_args, [b_proj, b_kv])

        s_zero = sig("diag_cleared", 1)
        s_ctx = sig("ctx_copied", 1)
        s_noted = ctx.enter_context(nc.semaphore("ca_use_noted"))
        s_q = sig("q_projected", NPAIR, 2)
        s_kv = sig("kv_projected", NPAIR, 2)
        s_qsb = sig("q_copied", NPAIR, 2)
        s_ksb = sig("k_copied", 3 * NPAIR, 6)
        s_scores = sig("scores_made", NPAIR, BUFS)
        s_max = sig("max_made", NPAIR)
        s_sub = sig("shifted", NPAIR, 2)
        s_exp = sig("exp_made", NPAIR)
        s_sum = sig("sum_made", NPAIR)
        s_inv = sig("inverse_made", NPAIR)
        s_norm = sig("probs_scaled", NPAIR)
        s_turn = sig("turned_made", 2 * NPAIR, 2 * BUFS)
        s_evac0 = sig("turned_copied_even", NPAIR, 1)
        s_evac1 = sig("turned_copied_odd", NPAIR, 1)
        s_pv = sig("pv_made", 2 * NPAIR, 2 * BUFS)
        s_att = sig("att_copied", NPAIR, 2)
        s_o = sig("out_projected", 2, 2)
        s_bias = sig("bias_added", 1)
        s_x = sig("x_updated", QT, QT)

        s_raw, s_later = (ctx.enter_context(nc.semaphore(f"ca_{n}_loaded")) for n in ("raw", "later"))
        s_rounded = sig("next_rounded", Split.ROUNDED)
        s_rest = sig("next_rest", Split.REST)
        columns = lambda b: bass.ds(b * (INNER // B), INNER // B)

        def ahead(step, b, j, more):
            if j < NPAIR:
                step(b, j)
            elif more:
                step(b + 1, j - NPAIR)

        block = ctx.enter_context(nc.Block())

        @block.sync
        def _(sp):
            next_parts.load(sp, next_w, raw, s_raw)
            for tile, src in later:
                sp.dma_start(tile, src).then_inc(s_later, 16)
            sp.wait_ge(s_later, 16 * len(later))

        @block.tensor
        def _(pe):
            ln.start_tensor(pe)
            for s in (s_q, s_kv, s_scores, s_turn, s_pv, s_o):
                pe.sem_inc(s.sem, s.credit)

            def turn_norm(b):
                def bank_free(i):
                    if i == 0:
                        pe.wait_ge(s_qsb.sem, s_qsb.at(b, -1))
                    else:
                        pe.wait_ge(s_ksb.sem, s_ksb.at(b, -1))
                ln.turn(pe, b, ident, bank_free)

            def project(b, j):
                if j == 0:
                    ln.ready(pe, b)
                    pe.wait_ge(s_ctx.sem, s_ctx.at(b, 0))
                pe.wait_ge(s_qsb.sem, s_qsb.at(b, j - 1))
                ln.project(pe, b_proj, w_q, j * P).then_inc(s_q.sem, 1)
                pe.wait_ge(s_ksb.sem, s_ksb.at(b, 3 * j - 1))
                pe.matmul(b_kv[:, 0:SK], w_k[:, j * P:(j + 1) * P], ctx_b[:], start=True, stop=True)
                pe.matmul(b_kv[0:SK, P:2 * P], ctx_b[:], w_v[:, j * P:(j + 1) * P], start=True, stop=True).then_inc(s_kv.sem, 1)

            def scores(b, j):
                pe.wait_ge(s_qsb.sem, s_qsb.at(b, j))
                pe.wait_ge(s_ksb.sem, s_ksb.at(b, 3 * j + 2))
                pe.wait_ge(s_sub.sem, s_sub.at(b, j - 1))
                for q in range(QT):
                    last = pe.matmul(b_scores[:, q // 2, (q % 2) * 2 * SK:(q % 2 + 1) * 2 * SK], q_sb[:, j % BUFS, q * P:(q + 1) * P],
                                     k_diag[:, j % BUFS, :, :], start=True, stop=True)
                last.then_inc(s_scores.sem, 1)

            def turns(b, j):
                pe.wait_ge(s_norm.sem, s_norm.at(b, j))
                for e in range(2):
                    s = (s_evac0, s_evac1)[e]
                    pe.wait_ge(s.sem, s.at(b, j - 1))
                    for q in range(QT):
                        last = pe.transpose(b_turn[e][0:SK, q * P:(q + 1) * P], probs[:, j % BUFS, q, e, :], ident[:])
                    last.then_inc(s_turn.sem, 1)

            def pv(b, j):
                if j >= 2:
                    pe.wait_ge(s_att.sem, s_att.at(b, j - 2))
                else:
                    pe.wait_ge(s_x.sem, s_x.at(b, 2 * j + 1 - QT))
                for e in range(2):
                    s = (s_evac0, s_evac1)[e]
                    pe.wait_ge(s.sem, s.at(b, j))
                    pe.matmul(b_out[j % 2][e * HD:(e + 1) * HD, :], v_sb[:, j % BUFS, e * HD:(e + 1) * HD],
                              turned[:, e, :], start=True, stop=True).then_inc(s_pv.sem, 1)

            def project_out(b):
                for half in range(2):
                    for t in range(2):
                        q = 2 * half + t
                        for j in range(NPAIR):
                            if q == 0:
                                pe.wait_ge(s_att.sem, s_att.at(b, NPAIR - 2 if j < NPAIR - 1 else NPAIR - 1))
                            last = pe.matmul(b_out[half][:, t * D:(t + 1) * D], att[:, j, q * P:(q + 1) * P],
                                             w_o[:, j, :], start=(j == 0), stop=(j == NPAIR - 1))
                    last.then_inc(s_o.sem, 1)

            pe.wait_ge(s_zero.sem, 1)
            turn_norm(0)
            project(0, 0)
            project(0, 1)
            scores(0, 0)
            project(0, 2)
            scores(0, 1)

            def batch(b, more):
                for j in range(NPAIR):
                    ahead(scores, b, j + 2, more)
                    turns(b, j)
                    ahead(project, b, j + 3, more)
                    if more and j == NPAIR - 4:
                        turn_norm(b + 1)
                    pv(b, j)
                project_out(b)

            over_batches(pe, batch)

        @block.scalar
        def _(act):
            ln.start_scalar(act)
            for s in (s_qsb, s_evac0, s_att):
                act.sem_inc(s.sem, s.credit)

            def operands_free(b):
                def wait(eng):
                    eng.wait_ge(s_q.sem, s_q.at(b, -1))
                return wait

            def copy_q(b, j):
                act.wait_ge(s_q.sem, s_q.at(b, j))
                act.wait_ge(s_scores.sem, s_scores.at(b, j - BUFS))
                act.activation(q_sb[:, j % BUFS, :], b_proj, ACT.Copy, scale=SCALE1).then_inc(s_qsb.sem, 1)

            def exps(b, j):
                act.wait_ge(s_sub.sem, s_sub.at(b, j))
                p = probs[:, j % BUFS, :, :, :].rearrange("p a b c -> p (a b c)")
                act.activation(p, p, ACT.Exp).then_inc(s_exp.sem, 1)

            def copy_turned(b, j):
                act.wait_ge(s_turn.sem, s_turn.at(b, 2 * j))
                act.wait_ge(s_pv.sem, s_pv.at(b, 2 * j - 2))
                act.copy(turned[:, 0, :], b_turn[0][0:SK, :]).then_inc(s_evac0.sem, 1)

            def copy_att(b, j):
                act.wait_ge(s_pv.sem, s_pv.at(b, 2 * j + 1))
                act.wait_ge(s_o.sem, s_o.at(b, -1))
                act.copy(att[:, j, :], b_out[j % 2]).then_inc(s_att.sem, 1)

            ln.scale_and_round(act, 0, operands_free(0))
            copy_q(0, 0)
            copy_q(0, 1)
            exps(0, 0)
            copy_q(0, 2)
            exps(0, 1)

            def batch(b, more):
                for j in range(NPAIR):
                    if j >= 1:
                        copy_att(b, j - 1)
                    copy_turned(b, j)
                    ahead(exps, b, j + 2, more)
                    ahead(copy_q, b, j + 3, more)
                    if more and j == NPAIR - 4:
                        ln.scale_and_round(act, b + 1, operands_free(b + 1))
                    if j == 2:
                        act.wait_ge(s_raw, 16 * Split.LOADS)
                        next_parts.round(act, raw, columns(b), s_rounded.sem)
                copy_att(b, NPAIR - 1)

            over_batches(act, batch)

        @block.vector
        def _(dve):
            ln.start_vector(dve)
            for s in (s_ksb, s_sub, s_evac1, s_x):
                dve.sem_inc(s.sem, s.credit)
            dve.memset(k_diag[:], 0.0).then_inc(s_zero.sem, 1)
            dve.wait_ge(s_zero.sem, 1)

            def operands_free(b):
                def wait(eng):
                    eng.wait_ge(s_q.sem, s_q.at(b, -1))
                return wait

            def copy_kv(b, j):
                dve.wait_ge(s_kv.sem, s_kv.at(b, j))
                dve.wait_ge(s_scores.sem, s_scores.at(b, j - BUFS))
                for e in range(2):
                    rows = slice(e * HD, (e + 1) * HD)
                    dve.tensor_copy(k_diag[rows, j % BUFS, e, :], b_kv[rows, 0:SK]).then_inc(s_ksb.sem, 1)
                dve.wait_ge(s_pv.sem, s_pv.at(b, 2 * (j - BUFS) + 1))
                dve.tensor_copy(v_sb[:, j % BUFS, :], b_kv[0:SK, P:2 * P]).then_inc(s_ksb.sem, 1)

            def shift(b, j):
                s4 = scores_ap.rearrange("p a (c k) -> p a c k", k=SK)
                p = probs[:, j % BUFS, :, :, :].rearrange("p (a q) e k -> p a (q e) k", a=2)
                m = top[:, j % BUFS, :]
                dve.wait_ge(s_scores.sem, s_scores.at(b, j))
                dve.tensor_reduce(m, s4, AX_X, ALU.max).then_inc(s_max.sem, 1)
                dve.wait_ge(s_max.sem, s_max.at(b, j))
                dve.wait_ge(s_turn.sem, s_turn.at(b, 2 * (j - BUFS) + 1))
                dve.tensor_tensor(p, s4, m.rearrange("p (a c) -> p a c", a=2).unsqueeze(3).broadcast_to([P, 2, QT, SK]),
                                  ALU.subtract).then_inc(s_sub.sem, 1)

            def invert(b, j):
                p = probs[:, j % BUFS, :, :, :].rearrange("p q e k -> p (q e) k")
                dve.wait_ge(s_exp.sem, s_exp.at(b, j))
                dve.tensor_reduce(total[:, j % BUFS, :], p, AX_X, ALU.add).then_inc(s_sum.sem, 1)
                dve.wait_ge(s_sum.sem, s_sum.at(b, j))
                dve.reciprocal(inverse[:, j % BUFS, :], total[:, j % BUFS, :]).then_inc(s_inv.sem, 1)

            def copy_turned(b, j):
                dve.wait_ge(s_turn.sem, s_turn.at(b, 2 * j + 1))
                dve.wait_ge(s_pv.sem, s_pv.at(b, 2 * j - 1))
                dve.tensor_copy(turned[:, 1, :], b_turn[1][0:SK, :]).then_inc(s_evac1.sem, 1)

            def update(b):
                dve.wait_ge(s_bias.sem, s_bias.at(b, 0))
                for half in range(2):
                    dve.wait_ge(s_o.sem, s_o.at(b, half))
                    for t in range(2):
                        xt = x[:, bass.ds(b * QT + 2 * half + t, 1), :].rearrange("p a d -> p (a d)")
                        dve.tensor_tensor(xt, b_out[half][:, t * D:(t + 1) * D], xt, ALU.add).then_inc(s_x.sem, 1)

            ln.statistics(dve, 0)
            ln.standardize(dve, 0)
            ln.remainder(dve, 0, operands_free(0))
            copy_kv(0, 0)
            copy_kv(0, 1)
            shift(0, 0)
            copy_kv(0, 2)
            invert(0, 0)
            shift(0, 1)

            def batch(b, more):
                for j in range(NPAIR):
                    ahead(invert, b, j + 1, more)
                    ahead(shift, b, j + 2, more)
                    copy_turned(b, j)
                    ahead(copy_kv, b, j + 3, more)
                    if j == 3:
                        dve.wait_ge(s_rounded.sem, s_rounded.at(b, Split.ROUNDED - 1))
                        next_parts.rest(dve, raw, columns(b), s_rest.sem)
                    if more and j == LN_AT:
                        ln.statistics(dve, b + 1)
                    if more and j == LN_AT + 1:
                        ln.standardize(dve, b + 1)
                    if more and j == NPAIR - 4:
                        ln.remainder(dve, b + 1, operands_free(b + 1))
                update(b)

            over_batches(dve, batch)

        @block.gpsimd
        def _(pool):
            ln.start_gpsimd(pool)

            def add_bias(b):
                ln.deviations(pool, b)
                pool.wait_ge(ln.s_hat.sem, ln.s_hat.at(b, QT - 1))
                xt = x[:, bass.ds(b * QT, QT), :]
                pool.tensor_tensor(xt, xt, bias_o[:].unsqueeze(1).broadcast_to([P, QT, D]), ALU.add).then_inc(s_bias.sem, 1)

            def copy_context(b):
                pool.wait_ge(s_kv.sem, s_kv.at(b, -1))
                pool.sem_inc(s_noted, 1)
                pool.tensor_copy(ctx_b[:], ctx_t[:, bass.ds(b, 1), :].rearrange("p a k -> p (a k)")).then_inc(s_ctx.sem, 1)

            def scale(b, j):
                p = probs[:, j % BUFS, :, :, :].rearrange("p q e k -> p (q e) k")
                pool.wait_ge(s_inv.sem, s_inv.at(b, j))
                pool.tensor_tensor(p, p, inverse[:, j % BUFS, :].unsqueeze(2).broadcast_to([P, 2 * QT, SK]), ALU.mult).then_inc(s_norm.sem, 1)

            add_bias(0)
            copy_context(0)
            scale(0, 0)

            def batch(b, more):
                for j in range(NPAIR):
                    ahead(scale, b, j + 1, more)
                    if more and j == LN_AT + 1:
                        add_bias(b + 1)
                    if more and j == NPAIR - 4:
                        copy_context(b + 1)

            over_batches(pool, batch)


def feedfwd(nc, x, ident, norm_args, w_1, b_1, w_2, bias_o, banks, out):
    with ExitStack() as ctx:
        sb = lambda n, s, d=F32: ctx.enter_context(nc.sbuf_tensor("ff_" + n, s, d))
        sig = lambda n, per, credit=0, step=1: Signal(ctx, nc, "ff_" + n, per, credit, step)
        gate = sb("gate", [P, 2, S])
        h = sb("h", [P, NF, S])
        hat = sb("hat", [P, QT, D])
        full = sb("full", [P, S])
        full_tail = sb("full_tail", [DT, S])
        hi, lo, tail = sb("y_hi", [P, S], F32R), sb("y_lo", [P, S], F32R), sb("y_tail", [3 * DT, S], F32R)

        b_gate, b_a, b_out, b_ln = banks[0:2], banks[2:4], banks[4:6], banks[6:8]
        ln = Norm(ctx, nc, "ff_ln_", x, hat, hi, lo, tail, full, full_tail, *norm_args, b_ln)

        s_g = sig("gate_projected", NF)
        s_a = sig("a_projected", NF, 1)
        s_gelu = sig("gelu_made", NF, 1)
        s_h = sig("h_made", NF, 2)
        s_o = sig("out_projected", 2, 1)
        s_bias = sig("bias_added", 1)
        s_x = sig("x_updated", QT, QT)
        s_out = sig("out_stored", 1, 0, 16)
        s_noted = ctx.enter_context(nc.semaphore("ff_x_noted"))

        block = ctx.enter_context(nc.Block())

        @block.tensor
        def _(pe):
            ln.start_tensor(pe)
            for s in (s_a, s_o):
                pe.sem_inc(s.sem, s.credit)

            def turn_norm(b):
                ln.turn(pe, b, ident, lambda i: pe.wait_ge(ln.s_full.sem, ln.s_full.at(b, i - 2)))

            turn_norm(0)

            def batch(b, more):
                ln.ready(pe, b)
                for m in range(NF):
                    before = max(m - 2, -1)
                    pe.wait_ge(s_gelu.sem, s_gelu.at(b, before))
                    ln.project(pe, b_gate[m % 2], w_1, DFF + m * P).then_inc(s_g.sem, 1)
                    pe.wait_ge(s_h.sem, s_h.at(b, before))
                    ln.project(pe, b_a[m % 2], w_1, m * P).then_inc(s_a.sem, 1)
                if more:
                    turn_norm(b + 1)
                for half in range(2):
                    pe.wait_ge(s_x.sem, s_x.at(b, 2 * half + 1 - QT))
                    for t in range(2):
                        q = 2 * half + t
                        for m in range(NF):
                            if q == 0:
                                pe.wait_ge(s_h.sem, s_h.at(b, m))
                            last = pe.matmul(b_out[half][:, t * D:(t + 1) * D], h[:, m, q * P:(q + 1) * P],
                                             w_2[:, m, :], start=(m == 0), stop=(m == NF - 1))
                    last.then_inc(s_o.sem, 1)

            over_batches(pe, batch)

        @block.scalar
        def _(act):
            ln.start_scalar(act)
            act.sem_inc(s_gelu.sem, 1)

            def operands_free(b):
                return lambda eng: eng.wait_ge(s_a.sem, s_a.at(b, -1))

            ln.scale_and_round(act, 0, operands_free(0))

            def batch(b, more):
                for m in range(NF):
                    act.wait_ge(s_g.sem, s_g.at(b, m))
                    act.wait_ge(s_h.sem, s_h.at(b, max(m - 2, -1)))
                    act.activation(gate[:, m % 2, :], b_gate[m % 2], ACT.Gelu_apprx_tanh, bias=b_1[:, NF + m:NF + m + 1]).then_inc(s_gelu.sem, 1)
                if more:
                    ln.scale_and_round(act, b + 1, operands_free(b + 1))

            over_batches(act, batch)

        @block.vector
        def _(dve):
            ln.start_vector(dve)
            for s in (s_h, s_x):
                dve.sem_inc(s.sem, s.credit)

            def operands_free(b):
                return lambda eng: eng.wait_ge(s_a.sem, s_a.at(b, -1))

            ln.statistics(dve, 0)
            ln.standardize(dve, 0)
            ln.remainder(dve, 0, operands_free(0))

            def batch(b, more):
                if more:
                    ln.statistics(dve, b + 1)
                    ln.standardize(dve, b + 1)
                for m in range(NF):
                    dve.wait_ge(s_a.sem, s_a.at(b, m))
                    dve.wait_ge(s_gelu.sem, s_gelu.at(b, m))
                    dve.wait_ge(s_o.sem, s_o.at(b, -1))
                    dve.scalar_tensor_tensor(out=h[:, m, :], in0=b_a[m % 2], scalar=b_1[:, m:m + 1], in1=gate[:, m % 2, :],
                                             op0=ALU.add, op1=ALU.mult).then_inc(s_h.sem, 1)
                if more:
                    ln.remainder(dve, b + 1, operands_free(b + 1))
                dve.wait_ge(s_bias.sem, s_bias.at(b, 0))
                for half in range(2):
                    dve.wait_ge(s_o.sem, s_o.at(b, half))
                    for t in range(2):
                        xt = x[:, bass.ds(b * QT + 2 * half + t, 1), :].rearrange("p a d -> p (a d)")
                        dve.tensor_tensor(xt, b_out[half][:, t * D:(t + 1) * D], xt, ALU.add).then_inc(s_x.sem, 1)

            over_batches(dve, batch)

        @block.gpsimd
        def _(pool):
            ln.start_gpsimd(pool)

            with pool.Fori(0, B) as b:
                ln.deviations(pool, b)
                pool.wait_ge(ln.s_hat.sem, ln.s_hat.at(b, QT - 1))
                xt = x[:, bass.ds(b * QT, QT), :]
                pool.tensor_tensor(xt, xt, bias_o[:].unsqueeze(1).broadcast_to([P, QT, D]), ALU.add).then_inc(s_bias.sem, 1)

        @block.sync
        def _(sp):
            tiles = out.rearrange("b (q p) d -> p (b q) d", p=P)
            with sp.Fori(0, B) as b:
                sp.wait_ge(s_x.sem, s_x.at(b, QT - 1))
                sp.sem_inc(s_noted, 1)
                sp.dma_start(tiles[:, bass.ds(b * QT, QT), :], x[:, bass.ds(b * QT, QT), :]).then_inc(s_out.sem, 16)
            sp.wait_ge(s_out.sem, s_out.at(B - 1, 0))


class Banks:

    def __init__(self, psum):
        self.psum = psum

    def __getitem__(self, i):
        if isinstance(i, slice):
            return [self.psum[:, k, :] for k in range(*i.indices(8))]
        return self.psum[:, i, :]

    def pair(self, i):
        return self.psum[:, i:i + 2, :]


def build(nc, t, out):
    w = lambda n: t["L1_xattn_" + n]
    with ExitStack() as ctx:
        psum = ctx.enter_context(nc.psum_tensor("banks", [P, 8, 512], F32))
        banks = Banks(psum)
        keep = lambda n, s, d=F32: ctx.enter_context(nc.sbuf_tensor(n, s, d))
        x = keep("x", [P, B * QT, D])
        ident = keep("ident", [P, P])
        ctx_t = keep("ctx_t", [CTX, B, SK])
        bias = {n: keep(n, [P, D]) for n in ("bo1", "bo2")}
        gains = {n: keep(n, [P, 2]) for n in ("g1", "be1", "g2", "be2", "g3", "be3")}
        b_1 = keep("b_1", [P, 2 * NF])
        wa, wb, wc = (Split(ctx, nc, f"w{c}_") for c in "abc")
        raw = Raw(ctx, nc, "raw_")
        w_o1, w_o2 = keep("w_o1", [P, NPAIR, D]), keep("w_o2", [P, NPAIR, D])
        w_k2, w_v2 = keep("w_k2", [CTX, INNER]), keep("w_v2", [CTX, INNER])

        pairs = lambda ap: ap.rearrange("(j p) d -> p j d", p=P)
        later = [(b_1[:, m:m + 1], w("b_ff1")[m * P:(m + 1) * P].unsqueeze(1)) for m in range(2 * NF)]
        later += [(to[:], w(name).unsqueeze(0).broadcast_to([P, D])) for name, to in bias.items()]
        for name, to in gains.items():
            later += [(to[:, 0:1], w(name)[0:P].unsqueeze(1)), (to[0:DT, 1:2], w(name)[P:D].unsqueeze(1))]
        later += [(w_o1[:], pairs(w("wo1"))), (w_o2[:], pairs(w("wo2"))), (w_k2[:], w("wk2")), (w_v2[:], w("wv2"))]

        adapter(nc, t, x, ident, ctx_t, banks, [(w("wq1"), wa), (w("wk1"), wb), (w("wv1"), wc)], later)
        selfattn(nc, x, ident, (gains["g1"], gains["be1"]), wa, wb, wc, w_o1, bias["bo1"], banks, w("wq2"), raw)
        w_2, b_2 = keep("w_2", [P, NF, D]), keep("b_2", [P, D])
        crossattn(nc, x, ident, (gains["g2"], gains["be2"]), ctx_t, wa, w_k2, w_v2, w_o2, bias["bo2"], banks, w("w_ff1"), wb, raw,
                  [(w_2[:], pairs(w("w_ff2"))), (b_2[:], w("b_ff2").unsqueeze(0).broadcast_to([P, D]))])
        feedfwd(nc, x, ident, (gains["g3"], gains["be3"]), wb, b_1, w_2, b_2, banks, out)


def kernel(**inputs):
    import concourse.bacc as bacc
    from concourse.bass_utils import run_bass_kernel_spmd

    nc = bacc.Bacc("TRN2", target_bir_lowering=False, num_devices=1)
    arrays = {"in_" + n: np.ascontiguousarray(a) for n, a in inputs.items()}
    arrays["in_ident"] = np.eye(P, dtype=np.float32)
    repeated = np.linspace(0, CTX - 1, S).astype(np.int64)
    arrays["in_expand"] = (np.arange(CTX)[:, None] == repeated[None, :]).astype(np.float32)
    arrays["in_own"] = (np.arange(H0 * NCA)[:, None] // NCA == np.arange(H0 * HP)[None, :] // HP).astype(np.float32)
    t = {n[3:]: nc.dram_tensor(n, a.shape, F32, kind="ExternalInput").ap() for n, a in arrays.items()}
    out = nc.dram_tensor("out", (B, S, D), F32, kind="ExternalOutput").ap()
    build(nc, t, out)
    r = run_bass_kernel_spmd(nc, [arrays], core_ids=[0])
    return r.results[0]["out"]
```

```python
from contextlib import ExitStack

import numpy as np

import concourse.bass as bass
from concourse import mybir

F32 = mybir.dt.float32
F32R = mybir.dt.float32r
ALU = mybir.AluOpType
ACT = mybir.ActivationFunctionType
AX_X = mybir.AxisListType.X

B, S, D = 4, 512, 160
P = 128
QT = S // P
DT = D - P
SK, CTX = 77, 96
NCA = 4
SE = SK - NCA
H0, HD0, HP = 8, 20, 32
G = H0 * HP // P
HG = H0 // G
H1, HD = 20, 64
INNER = H1 * HD
NPAIR = H1 // 2
DFF = 640
NF = DFF // P
EPS = 1e-5
SCALE0 = float(HD0) ** -0.5
SCALE1 = float(HD) ** -0.5


class Signal:

    def __init__(self, ctx, nc, name, per, credit=0, step=1):
        self.sem = ctx.enter_context(nc.semaphore(name))
        self.per, self.credit, self.step = per, credit, step

    def at(self, b, k):
        return (b * self.per + (k + 1) + self.credit) * self.step


def over_batches(eng, body):
    with eng.Fori(0, B - 1) as b:
        body(b, True)
    body(B - 1, False)


class NormStore:

    def __init__(self, ctx, nc, x):
        self.x = x
        name = "ln_"
        sb = lambda n, s, d=F32: ctx.enter_context(nc.sbuf_tensor(name + n, s, d))
        self.hat = sb("hat", [P, QT, D])
        self.full = sb("full", [P, S])
        self.full_tail = sb("full_tail", [DT, S])
        self.hi, self.lo, self.tail = sb("y_hi", [P, S], F32R), sb("y_lo", [P, S], F32R), sb("y_tail", [3 * DT, S], F32R)
        self.stats = sb("stats", [P, QT, 6])
        self.moments = sb("moments", [P, QT, 2])
        self.veps = sb("veps", [P, QT])
        self.half = sb("half", [P, QT])
        self.eps = sb("eps", [P, QT])
        self.rstd = sb("rstd", [P, QT])
        sig = lambda n, per, credit=0: Signal(ctx, nc, name + n, per, credit)
        self.s_stats = sig("stats_made", QT)
        self.s_noted = ctx.enter_context(nc.semaphore(name + "stats_noted"))
        self.s_moments = sig("moments_made", QT)
        self.s_half = sig("constants_set", 2)
        self.s_veps = sig("veps_made", 1)
        self.s_rstd = sig("rstd_made", 1)
        self.s_hat = sig("hat_made", QT)
        self.s_turned = sig("turned", 2, 2)
        self.s_full = sig("full_made", 2, 2)
        self.s_hi = sig("hi_made", 3, 3)
        self.s_lo = sig("lo_made", 2, 2)


class Norm:

    def __init__(self, store, i, gain, shift):
        self.before, self.gain, self.shift = i * B, gain, shift
        self.x, self.hat, self.full, self.full_tail = store.x, store.hat, store.full, store.full_tail
        self.hi, self.lo, self.tail, self.stats = store.hi, store.lo, store.tail, store.stats
        self.moments, self.veps, self.half, self.eps = store.moments, store.veps, store.half, store.eps
        self.rstd, self.s_stats, self.s_noted, self.s_moments = store.rstd, store.s_stats, store.s_noted, store.s_moments
        self.s_half, self.s_veps, self.s_rstd, self.s_hat = store.s_half, store.s_veps, store.s_rstd, store.s_hat
        self.s_turned, self.s_full, self.s_hi, self.s_lo = store.s_turned, store.s_full, store.s_hi, store.s_lo

    def start_gpsimd(self, pool):
        pool.memset(self.half[:], -0.5).then_inc(self.s_half.sem, 1)
        pool.memset(self.eps[:], EPS).then_inc(self.s_half.sem, 1)
        pool.wait_ge(self.s_half.sem, 2)

    def start_tensor(self, pe):
        pe.sem_inc(self.s_turned.sem, 2)

    def start_scalar(self, act):
        act.sem_inc(self.s_full.sem, 2)
        act.sem_inc(self.s_hi.sem, 3)

    def start_vector(self, dve):
        dve.sem_inc(self.s_lo.sem, 2)

    def statistics(self, dve, b):
        for q in range(QT):
            dve.bn_stats(self.stats[:, q, :], self.x[:, bass.ds(b * QT + q, 1), :].rearrange("p a d -> p (a d)")).then_inc(self.s_stats.sem, 1)
        dve.wait_ge(self.s_stats.sem, self.s_stats.at(self.before + b, QT - 1))
        dve.sem_inc(self.s_noted, 1)
        for q in range(QT):
            dve.bn_aggr(self.moments[:, q, :], self.stats[:, q, :]).then_inc(self.s_moments.sem, 1)

    def deviations(self, pool, b):
        pool.wait_ge(self.s_moments.sem, self.s_moments.at(self.before + b, QT - 1))
        pool.tensor_tensor(self.veps[:], self.moments[:, :, 1], self.eps[:], ALU.add).then_inc(self.s_veps.sem, 1)
        pool.wait_ge(self.s_veps.sem, self.s_veps.at(self.before + b, 0))
        pool.tensor_tensor(self.rstd[:], self.veps[:], self.half[:], ALU.pow).then_inc(self.s_rstd.sem, 1)

    def standardize(self, dve, b):
        dve.wait_ge(self.s_rstd.sem, self.s_rstd.at(self.before + b, 0))
        dve.wait_ge(self.s_turned.sem, self.s_turned.at(self.before + b, -1))
        for q in range(QT):
            dve.tensor_scalar(self.hat[:, q, :], self.x[:, bass.ds(b * QT + q, 1), :].rearrange("p a d -> p (a d)"),
                              self.moments[:, q, 0:1], self.rstd[:, q:q + 1], ALU.subtract, ALU.mult).then_inc(self.s_hat.sem, 1)

    def turn(self, pe, b, ident, banks, bank_free):
        pe.wait_ge(self.s_hat.sem, self.s_hat.at(self.before + b, QT - 1))
        bank_free(0)
        for q in range(QT):
            last = pe.transpose(banks[0][:, q * P:(q + 1) * P], self.hat[:, q, 0:P], ident[:])
        last.then_inc(self.s_turned.sem, 1)
        bank_free(1)
        for q in range(QT):
            last = pe.transpose(banks[1][0:DT, q * P:(q + 1) * P], self.hat[:, q, P:D], ident[:])
        last.then_inc(self.s_turned.sem, 1)

    def scale(self, act, b, banks):
        act.wait_ge(self.s_turned.sem, self.s_turned.at(self.before + b, 0))
        act.wait_ge(self.s_lo.sem, self.s_lo.at(self.before + b, -1))
        act.wait_ge(self.s_hi.sem, self.s_hi.at(self.before + b, -1))
        act.activation(self.full[:], banks[0], ACT.Identity, bias=self.shift[:, 0:1], scale=self.gain[:, 0:1]).then_inc(self.s_full.sem, 1)
        act.wait_ge(self.s_turned.sem, self.s_turned.at(self.before + b, 1))
        act.activation(self.full_tail[:], banks[1][0:DT, :], ACT.Identity, bias=self.shift[0:DT, 1:2], scale=self.gain[0:DT, 1:2]).then_inc(self.s_full.sem, 1)

    def round(self, act, b, operands_free):
        operands_free(act)
        act.wait_ge(self.s_full.sem, self.s_full.at(self.before + b, 0))
        act.copy(self.hi[:], self.full[:]).then_inc(self.s_hi.sem, 1)
        act.wait_ge(self.s_full.sem, self.s_full.at(self.before + b, 1))
        act.copy(self.tail[0:DT, :], self.full_tail[:]).then_inc(self.s_hi.sem, 1)
        act.copy(self.tail[2 * DT:3 * DT, :], self.full_tail[:]).then_inc(self.s_hi.sem, 1)

    def scale_and_round(self, act, b, banks, operands_free):
        self.scale(act, b, banks)
        self.round(act, b, operands_free)

    def remainder(self, dve, b, operands_free):
        operands_free(dve)
        dve.wait_ge(self.s_hi.sem, self.s_hi.at(self.before + b, 0))
        dve.tensor_tensor(self.lo[:], self.full[:], self.hi[:].bitcast(F32), ALU.subtract).then_inc(self.s_lo.sem, 1)
        dve.wait_ge(self.s_hi.sem, self.s_hi.at(self.before + b, 1))
        dve.tensor_tensor(self.tail[DT:2 * DT, :], self.full_tail[:], self.tail[0:DT, :].bitcast(F32), ALU.subtract).then_inc(self.s_lo.sem, 1)

    def ready(self, pe, b):
        pe.wait_ge(self.s_hi.sem, self.s_hi.at(self.before + b, 2))
        pe.wait_ge(self.s_lo.sem, self.s_lo.at(self.before + b, 1))

    def project(self, pe, bank, w, c0, n=P):
        c = slice(c0, c0 + n)
        pe.matmul(bank, w.hi[:, c], self.hi[:], start=True, stop=False)
        pe.matmul(bank, w.hi[:, c], self.lo[:], start=False, stop=False)
        pe.matmul(bank, w.lo[:, c], self.hi[:], start=False, stop=False)
        return pe.matmul(bank, w.tail[:, c], self.tail[:], start=False, stop=True)

    def project_tokens(self, pe, bank, w, c0, q, n=P):
        c, t = slice(c0, c0 + n), slice(q * P, (q + 1) * P)
        pe.matmul(bank, self.hi[:, t], w.hi[:, c], start=True, stop=False)
        pe.matmul(bank, self.lo[:, t], w.hi[:, c], start=False, stop=False)
        pe.matmul(bank, self.hi[:, t], w.lo[:, c], start=False, stop=False)
        return pe.matmul(bank, self.tail[:, t], w.tail[:, c], start=False, stop=True)


class Raw:

    def __init__(self, ctx, nc, name):
        self.main = ctx.enter_context(nc.sbuf_tensor(name + "main", [P, INNER], F32))
        self.tail = ctx.enter_context(nc.sbuf_tensor(name + "tail", [3 * DT, INNER], F32))


class Split:

    LOADS, ROUNDED, REST = 4, 2, 2

    def __init__(self, ctx, nc, name):
        sb = lambda n, s: ctx.enter_context(nc.sbuf_tensor(name + n, s, F32R))
        self.hi, self.lo, self.tail = sb("hi", [P, INNER]), sb("lo", [P, INNER]), sb("tail", [3 * DT, INNER])

    @staticmethod
    def load(sp, w, raw, loaded):
        sp.dma_start(raw.main[:], w[0:P, :]).then_inc(loaded, 16)
        for r in range(3):
            sp.dma_start(raw.tail[r * DT:(r + 1) * DT, :], w[P:D, :]).then_inc(loaded, 16)

    def round(self, act, raw, c, rounded):
        act.copy(self.hi[:, c], raw.main[:, c]).then_inc(rounded, 1)
        act.copy(self.tail[:, c], raw.tail[:, c]).then_inc(rounded, 1)

    def rest(self, dve, raw, c, made):
        low = slice(2 * DT, 3 * DT)
        dve.tensor_tensor(self.lo[:, c], raw.main[:, c], self.hi[:, c].bitcast(F32), ALU.subtract).then_inc(made, 1)
        dve.tensor_tensor(self.tail[low, c], raw.tail[low, c], self.tail[low, c].bitcast(F32), ALU.subtract).then_inc(made, 1)


def selfattn(nc, x, ident, ln, next_ln, w_q, w_k, w_v, w_o, bias_o, banks, next_w_q, raw):
    LEAD, LAG = 10, 2
    NB = H1 * QT
    PAIRB = 2 * QT
    V_BUF = (0, 1, 2, 0, 1)
    V_BEFORE = (3 - 5, 4 - 5, 2 - 5, 0, 1)
    PS = 4
    TS = 4
    LN_AT = 37
    TURN_AT = (NPAIR - 3) * PAIRB + 1
    PROJECT, ROUND, REST = (20, 19, 16), (19, 18, 15), (18, 17)
    START = {1: (1, 0), 2: (1, 1), 3: (1, 2), 8: (2, 0), 9: (2, 1)}

    def step_at(n, ahead):
        for what, a in enumerate(ahead):
            j, off = divmod(n + a, PAIRB)
            if off == 0:
                return j, what
        return None

    def product_of(n):
        return n // 2

    with ExitStack() as ctx:
        sb = lambda n, s, d=F32: ctx.enter_context(nc.sbuf_tensor("sa_" + n, s, d))
        sig = lambda n, per, credit=0, step=1: Signal(ctx, nc, "sa_" + n, per, credit, step)
        q_stack = sb("q_stack", [P, 2, 2, S], F32R)
        k_stack = sb("k_stack", [P, 2, 2, 2, S], F32R)
        q_parts = sb("q_parts", [P, 2, S], F32R)
        k_parts = sb("k_parts", [P, 2, S], F32R)
        v = sb("v", [P, 3, QT, 2 * P])
        probs = sb("probs", [P, PS, QT, S])
        turned = sb("turned", [P, TS, S])
        att = sb("att", [P, NPAIR, S])
        negmax = sb("negmax", [P, 4 * QT])
        total = sb("total", [P, 4 * QT])
        inverse = sb("inverse", [P, 4 * QT])

        b_scores, b_turn, b_out, b_proj = banks[0:2], banks[2:4], banks[4:6], banks[6:8]

        s_q = sig("q_projected", NPAIR, 2)
        s_k = sig("k_projected", NPAIR, 2)
        s_v = sig("v_projected", NPAIR, 2)
        s_qhi = sig("q_rounded", NPAIR)
        s_khi = sig("k_rounded", NPAIR)
        s_qlo = sig("q_rest", NPAIR, 2)
        s_klo = sig("k_rest", NPAIR, 2)
        s_vsb = sig("v_copied", NPAIR, 2)
        s_stack = [sig(f"stacked{i}", NPAIR // 2, 0, 8 * 16) for i in range(2)]
        s_scores = sig("scores_made", NB, 8 * QT)
        s_max = sig("max_made", NB)
        s_exp = sig("exp_made", NB, 4 * QT)
        s_inv = sig("inverse_made", NB)
        s_norm = sig("probs_scaled", NB)
        s_noted = ctx.enter_context(nc.semaphore("sa_inverse_noted"))
        s_noted_sp = ctx.enter_context(nc.semaphore("sa_parts_noted"))
        s_turn = sig("turned_made", NB, 4 * QT)
        s_evac = sig("turned_copied", NB * 3 // 4, 3)
        s_evac_act = sig("turned_copied_act", NB // 4, 1)
        s_pv = sig("pv_made", NB // 2, 6 * QT)
        s_att = sig("att_copied", NPAIR, 2)
        s_o = sig("out_projected", 2, 2)
        s_bias = sig("bias_added", 1)
        s_x = sig("x_updated", QT, QT)
        s_next, s_rounded, s_rest = (ctx.enter_context(nc.semaphore("sa_next_w_q_" + n)) for n in ("loaded", "rounded", "rest"))
        every = slice(0, INNER)

        def following(b, more):
            return (ln, b + 1, b + 1) if more else (next_ln, b + 1, 0)

        def wait_turned_copied(eng, b, n):
            g, k = divmod(n, 4)
            if k == 3:
                eng.wait_ge(s_evac_act.sem, s_evac_act.at(b, g))
            else:
                eng.wait_ge(s_evac.sem, s_evac.at(b, 3 * g + k))

        block = ctx.enter_context(nc.Block())

        @block.sync
        def _(sp):
            def stack(b, j):
                s = j % 2
                places = [(e, slice(e * HD, (e + 1) * HD), half, slice(half * HD, (half + 1) * HD)) for e in range(2) for half in range(2)]
                sp.wait_ge(s_scores.sem, s_scores.at(b, PAIRB * (j - 1) - 1))
                sp.sem_inc(s_noted_sp, 1)
                sp.wait_ge(s_qlo.sem, s_qlo.at(b, j))
                for e, rows, half, to in places:
                    sp.dma_start(q_stack[to, s, e, :].bitcast(F32), q_parts[rows, half, :].bitcast(F32)).then_inc(s_stack[s].sem, 16)
                sp.sem_inc(s_noted_sp, 1)
                sp.wait_ge(s_klo.sem, s_klo.at(b, j))
                for e, rows, half, to in places:
                    sp.dma_start(k_stack[to, s, e, :, :].bitcast(F32), k_parts[rows, :, :].bitcast(F32)).then_inc(s_stack[s].sem, 16)

            for j in range(3):
                stack(0, j)

            def batch(b, more):
                for j in range(3, NPAIR):
                    stack(b, j)
                if more:
                    for j in range(3):
                        stack(b + 1, j)
                else:
                    sp.wait_ge(s_q.sem, s_q.at(b, NPAIR - 1))
                    w_q.load(sp, next_w_q, raw, s_next)

            over_batches(sp, batch)

        @block.tensor
        def _(pe):
            for s in (s_q, s_k, s_v, s_scores, s_turn, s_pv, s_o):
                pe.sem_inc(s.sem, s.credit)

            def turn_norm(norm, b, nb):
                def bank_free(i):
                    if i == 0:
                        pe.wait_ge(s_vsb.sem, s_vsb.at(b, -1))
                    else:
                        pe.wait_ge(s_klo.sem, s_klo.at(b, -1))
                norm.turn(pe, nb, ident, b_proj, bank_free)

            def project(b, j, what):
                if j == 0 and what == 0:
                    ln.ready(pe, b)
                if what == 0:
                    if j > 0:
                        pe.wait_ge(s_vsb.sem, s_vsb.at(b, j - 1))
                    ln.project(pe, b_proj[0], w_q, j * P).then_inc(s_q.sem, 1)
                elif what == 1:
                    if j > 0:
                        pe.wait_ge(s_klo.sem, s_klo.at(b, j - 1))
                    ln.project(pe, b_proj[1], w_k, j * P).then_inc(s_k.sem, 1)
                else:
                    pe.wait_ge(s_qlo.sem, s_qlo.at(b, j))
                    for t in range(2):
                        last = ln.project_tokens(pe, b_proj[0][:, t * 2 * P:(t + 1) * 2 * P], w_v, j // 2 * 2 * P, j % 2 * 2 + t, 2 * P)
                    last.then_inc(s_v.sem, 1)

            def scores(b, n):
                h, q = divmod(n, QT)
                j, e = divmod(h, 2)
                if n % PAIRB == 0:
                    pe.wait_ge(s_stack[j % 2].sem, s_stack[j % 2].at(b, j // 2))
                pe.wait_ge(s_exp.sem, s_exp.at(b, n - 2))
                lhs = q_stack[:, j % 2, e, q * P:(q + 1) * P]
                bank = b_scores[n % 2]
                pe.matmul(bank, lhs, k_stack[:, j % 2, e, 0, :], start=True, stop=False)
                pe.matmul(bank, lhs, k_stack[:, j % 2, e, 1, :], start=False, stop=True).then_inc(s_scores.sem, 1)

            def turns(b, n):
                j, i = divmod(n, PAIRB)
                k, e = divmod(i, 2)
                h = 2 * j + e
                if k == 0:
                    pe.wait_ge(s_norm.sem, s_norm.at(b, QT * h + QT - 1))
                wait_turned_copied(pe, b, n - 2)
                for q in range(QT):
                    last = pe.transpose(b_turn[n % 2][:, q * P:(q + 1) * P], probs[:, h % PS, q, k * P:(k + 1) * P], ident[:])
                last.then_inc(s_turn.sem, 1)

            def pv(b, n):
                j, i = divmod(n, PAIRB)
                k, e = divmod(i, 2)
                if e == 0:
                    return
                wait_turned_copied(pe, b, n - 1)
                wait_turned_copied(pe, b, n)
                if k == 0:
                    pe.wait_ge(s_vsb.sem, s_vsb.at(b, j | 1))
                    if j >= 2:
                        pe.wait_ge(s_att.sem, s_att.at(b, j - 2))
                    else:
                        pe.wait_ge(s_x.sem, s_x.at(b, 2 * j - 1 - QT + 2))
                for e in range(2):
                    c = j % 2 * P + e * HD
                    last = pe.matmul(b_out[j % 2][e * HD:(e + 1) * HD, :], v[:, V_BUF[j // 2], k, c:c + HD],
                                     turned[:, (n - 1 + e) % TS, :], start=(k == 0), stop=(k == QT - 1))
                last.then_inc(s_pv.sem, 1)

            def project_out(b, q, first, end):
                for j in range(first, end):
                    pe.wait_ge(s_att.sem, s_att.at(b, max(j, NPAIR - 2)))
                    last = pe.matmul(b_out[q // 2][:, q % 2 * D:(q % 2 + 1) * D], att[:, j, q * P:(q + 1) * P],
                                     w_o[:, j, :], start=(j == 0), stop=(j == NPAIR - 1))
                if q % 2 == 1:
                    last.then_inc(s_o.sem, 1)

            for what in range(3):
                project(0, 0, what)
            for n in range(LEAD):
                if n in START:
                    project(0, *START[n])
                scores(0, n)

            def batch(b, more):
                for n in range(NB):
                    m = n + LEAD
                    if m < NB:
                        scores(b, m)
                    elif more:
                        scores(b + 1, m - NB)
                    if n >= LAG:
                        pv(b, n - LAG)
                    turns(b, n)
                    if step_at(n, PROJECT):
                        j, what = step_at(n, PROJECT)
                        if j < NPAIR:
                            project(b, j, what)
                        elif more:
                            project(b + 1, j - NPAIR, what)
                    if n == TURN_AT:
                        turn_norm(*following(b, more))
                project_out(b, 0, 0, 4)
                for n in range(NB - LAG, NB):
                    pv(b, n)
                project_out(b, 0, 4, NPAIR)
                for q in range(1, QT):
                    project_out(b, q, 0, NPAIR)

            over_batches(pe, batch)

        @block.scalar
        def _(act):
            for s in (s_vsb, s_exp, s_att, s_evac_act):
                act.sem_inc(s.sem, s.credit)

            def operands_free(b):
                def wait(eng):
                    eng.wait_ge(s_v.sem, s_v.at(b, -1))
                return wait

            def round_part(b, j, what, first=False):
                if what == 0:
                    act.wait_ge(s_q.sem, s_q.at(b, j))
                    if j >= 1 or not first:
                        act.wait_ge(s_stack[(j - 1) % 2].sem, s_stack[(j - 1) % 2].at(b, (j - 1) // 2))
                    act.activation(q_parts[:, 0, :], b_proj[0], ACT.Copy, scale=SCALE1).then_inc(s_qhi.sem, 1)
                elif what == 1:
                    act.wait_ge(s_k.sem, s_k.at(b, j))
                    act.copy(k_parts[:, 0, :], b_proj[1]).then_inc(s_khi.sem, 1)
                else:
                    act.wait_ge(s_v.sem, s_v.at(b, j))
                    act.wait_ge(s_pv.sem, s_pv.at(b, 2 * QT * (V_BEFORE[j // 2] + 1) - 1))
                    act.copy(v[:, V_BUF[j // 2], j % 2 * 2:j % 2 * 2 + 2, :].rearrange("p a c -> p (a c)"), b_proj[0]).then_inc(s_vsb.sem, 1)

            def exps(b, n):
                h, q = divmod(n, QT)
                c = n % (4 * QT)
                act.wait_ge(s_max.sem, s_max.at(b, n))
                if q == 0:
                    act.wait_ge(s_turn.sem, s_turn.at(b, (h - PS) // 2 * PAIRB + PAIRB - 2 + h % 2))
                act.activation(probs[:, h % PS, q, :], b_scores[n % 2], ACT.Exp, bias=negmax[:, c:c + 1],
                               accum_out=total[:, c:c + 1]).then_inc(s_exp.sem, 1)

            def copy_att(b, j):
                act.wait_ge(s_pv.sem, s_pv.at(b, QT * j + QT - 1))
                act.wait_ge(s_o.sem, s_o.at(b, -1))
                act.copy(att[:, j, :], b_out[j % 2]).then_inc(s_att.sem, 1)

            def copy_turned(b, n):
                act.wait_ge(s_turn.sem, s_turn.at(b, n))
                act.wait_ge(s_pv.sem, s_pv.at(b, product_of(n - TS)))
                act.copy(turned[:, n % TS, :], b_turn[n % 2]).then_inc(s_evac_act.sem, 1)

            for what in range(3):
                round_part(0, 0, what, first=True)
            for n in range(LEAD):
                if n in START:
                    round_part(0, *START[n])
                exps(0, n)

            def batch(b, more):
                for n in range(NB):
                    m = n + LEAD
                    if m < NB:
                        exps(b, m)
                    elif more:
                        exps(b + 1, m - NB)
                    if n % 4 == 3:
                        copy_turned(b, n)
                    if step_at(n, ROUND):
                        j, what = step_at(n, ROUND)
                        if j < NPAIR:
                            round_part(b, j, what)
                        elif more:
                            round_part(b + 1, j - NPAIR, what)
                    if n % PAIRB == LAG + 1 and n > PAIRB:
                        copy_att(b, n // PAIRB - 1)
                    norm, _, nb = following(b, more)
                    if n == TURN_AT:
                        norm.scale(act, nb, b_proj)
                    if n == TURN_AT + 1:
                        norm.round(act, nb, operands_free(b + 1))
                    if not more and n == NB - 10:
                        act.wait_ge(s_next, 16 * Split.LOADS)
                        w_q.round(act, raw, every, s_rounded)
                copy_att(b, NPAIR - 1)

            over_batches(act, batch)

        @block.vector
        def _(dve):
            for s in (s_qlo, s_klo, s_evac, s_x):
                dve.sem_inc(s.sem, s.credit)

            def operands_free(b):
                def wait(eng):
                    eng.wait_ge(s_v.sem, s_v.at(b, -1))
                return wait

            def rest(b, j, what):
                if what == 0:
                    dve.wait_ge(s_qhi.sem, s_qhi.at(b, j))
                    dve.scalar_tensor_tensor(out=q_parts[:, 1, :], in0=b_proj[0], scalar=SCALE1, in1=q_parts[:, 0, :].bitcast(F32),
                                             op0=ALU.mult, op1=ALU.subtract).then_inc(s_qlo.sem, 1)
                else:
                    dve.wait_ge(s_khi.sem, s_khi.at(b, j))
                    dve.tensor_tensor(k_parts[:, 1, :], b_proj[1], k_parts[:, 0, :].bitcast(F32), ALU.subtract).then_inc(s_klo.sem, 1)

            def maxima(b, n):
                c = n % (4 * QT)
                dve.wait_ge(s_scores.sem, s_scores.at(b, n))
                dve.tensor_reduce(negmax[:, c:c + 1], b_scores[n % 2], AX_X, ALU.max, negate=True).then_inc(s_max.sem, 1)

            def inverses(b, n):
                c = n % (4 * QT)
                dve.wait_ge(s_exp.sem, s_exp.at(b, n))
                dve.reciprocal(inverse[:, c:c + 1], total[:, c:c + 1]).then_inc(s_inv.sem, 1)

            def copy_turned(b, n):
                dve.wait_ge(s_turn.sem, s_turn.at(b, n))
                dve.wait_ge(s_pv.sem, s_pv.at(b, product_of(n - TS)))
                dve.tensor_copy(turned[:, n % TS, :], b_turn[n % 2]).then_inc(s_evac.sem, 1)

            def update(b):
                for half in range(2):
                    dve.wait_ge(s_o.sem, s_o.at(b, half))
                    if half == 0:
                        dve.wait_ge(s_bias.sem, s_bias.at(b, 0))
                    for t in range(2):
                        xt = x[:, bass.ds(b * QT + 2 * half + t, 1), :].rearrange("p a d -> p (a d)")
                        dve.tensor_tensor(xt, b_out[half][:, t * D:(t + 1) * D], xt, ALU.add).then_inc(s_x.sem, 1)

            for what in range(2):
                rest(0, 0, what)
            for n in range(LEAD):
                if n in START and START[n][1] < 2:
                    rest(0, *START[n])
                maxima(0, n)
                if n >= 1:
                    inverses(0, n - 1)

            def batch(b, more):
                for n in range(NB):
                    m = n + LEAD
                    if m < NB:
                        maxima(b, m)
                    elif more:
                        maxima(b + 1, m - NB)
                    if m - 1 < NB:
                        inverses(b, m - 1)
                    elif more:
                        inverses(b + 1, m - 1 - NB)
                    if n % 4 != 3:
                        copy_turned(b, n)
                    if step_at(n, REST):
                        j, what = step_at(n, REST)
                        if j < NPAIR:
                            rest(b, j, what)
                        elif more:
                            rest(b + 1, j - NPAIR, what)
                    norm, _, nb = following(b, more)
                    if n == LN_AT:
                        norm.statistics(dve, nb)
                    if n == LN_AT + 4:
                        norm.standardize(dve, nb)
                    if n == TURN_AT + 2:
                        norm.remainder(dve, nb, operands_free(b + 1))
                if not more:
                    dve.wait_ge(s_rounded, Split.ROUNDED)
                    w_q.rest(dve, raw, every, s_rest)
                update(b)

            over_batches(dve, batch)

        @block.gpsimd
        def _(pool):
            def scale(b, n):
                h, q = divmod(n, QT)
                c = n % (4 * QT)
                pool.wait_ge(s_inv.sem, s_inv.at(b, n))
                pool.sem_inc(s_noted, 1)
                pool.tensor_scalar(probs[:, h % PS, q, :], probs[:, h % PS, q, :], inverse[:, c:c + 1], 1.0,
                                   ALU.mult, ALU.mult).then_inc(s_norm.sem, 1)

            def add_bias(b):
                pool.wait_ge(ln.s_hat.sem, ln.s_hat.at(ln.before + b, QT - 1))
                xt = x[:, bass.ds(b * QT, QT), :]
                pool.tensor_tensor(xt, xt, bias_o[:].unsqueeze(1).broadcast_to([P, QT, D]), ALU.add).then_inc(s_bias.sem, 1)

            add_bias(0)
            for n in range(LEAD - 1):
                scale(0, n)

            def batch(b, more):
                for n in range(NB):
                    m = n + LEAD - 1
                    if m < NB:
                        scale(b, m)
                    elif more:
                        scale(b + 1, m - NB)
                    if n == LN_AT + 2:
                        norm, _, nb = following(b, more)
                        norm.deviations(pool, nb)
                    if more and n == LN_AT + 8:
                        add_bias(b + 1)

            over_batches(pool, batch)


def adapter(nc, t, x, ident, ctx_t, banks, splits, later, next_ln):
    w = lambda n: t["L0_xattn_" + n]
    with ExitStack() as ctx:
        sb = lambda n, s, d=F32: ctx.enter_context(nc.sbuf_tensor("ad_" + n, s, d))
        sig = lambda n, per, credit=0, step=1: Signal(ctx, nc, "ad_" + n, per, credit, step)
        N1 = 4
        HC = H0 * HP
        wq = sb("wq", [P, G, H0, HP])
        wo = sb("wo", [P, G, D])
        wk, wv, wk_ca, wv_ca = (sb(n, [CTX, H0, HP]) for n in ("wk", "wv", "wk_ca", "wv_ca"))
        wq_ca = sb("wq_ca", [NCA, H0, HP])
        b_o = sb("b_out", [P, D])
        expand = sb("expand", [CTX, S])
        own = sb("own", [H0 * NCA, HC])
        context = sb("context", [SK, CTX])
        tokens = sb("tokens", [NCA, CTX])
        x_pad = sb("x_pad", [P, QT, H0, HP])
        x_t = sb("x_t", [P, G, S])
        c_t = sb("c_t", [CTX, SK])
        c_rep = sb("c_rep", [CTX, H0, NCA])
        q_t = sb("q_t", [P, G, S])
        q1_diag = sb("q1_diag", [P, H0, CTX])
        k_diag = sb("k_diag", [P, G, HG, SE])
        k2_diag = sb("k2_diag", [P, G, HG, NCA])
        v = sb("v", [SE, HC])
        v2 = sb("v2", [H0 * NCA, HC])
        probs = sb("probs", [P, QT, G, HG, SE])
        turned = sb("turned", [SE, 2, S])
        probs1 = sb("probs1", [CTX, N1, S])
        turned1 = sb("turned1", [P, 2, QT, CTX])
        hs1 = sb("hs1", [P, G, CTX])
        q2 = sb("q2", [P, G, CTX])
        probs2 = sb("probs2", [CTX, H0, NCA])
        probs2x = sb("probs2x", [H0 * NCA, S])
        heads = sb("heads", [P, G, S])
        negmax1, total1, inverse1 = (sb(n, [CTX, N1]) for n in ("negmax1", "total1", "inverse1"))
        top, total, inverse = (sb(n, [P, QT, H0]) for n in ("top", "total", "inverse"))
        top2, total2, inverse2 = (sb(n, [CTX, H0]) for n in ("top2", "total2", "inverse2"))
        raws = [Raw(ctx, nc, f"ad_raw{i}_") for i in range(len(splits))]
        columns = lambda b: bass.ds(b * (INNER // B), INNER // B)
        SCORES_AT, INVERSES_AT = (0, 1, 3, 5), (2, 4, 6, 7)
        flat = lambda tile: tile.rearrange("p a b -> p (a b)")

        b_q1, b_k = banks[7][:, P:P + G * CTX], banks[7][:, P + G * CTX:P + G * CTX + G * SK]
        s_in, s_xrest, s_w, s_wq, s_wo, s_raw, s_later = (ctx.enter_context(nc.semaphore(f"ad_{n}_loaded")) for n in
                                                          ("first_x", "other_x", "weights", "wq", "out_weights", "raw", "later"))
        s_rounded = sig("weights_rounded", Split.ROUNDED * len(splits))
        s_rest = sig("weights_rest", Split.REST * len(splits))
        s_zero = ctx.enter_context(nc.semaphore("ad_cleared"))
        s_zero_diag = ctx.enter_context(nc.semaphore("ad_diagonals_cleared"))
        s_ctx = sig("context_loaded", 2, 0, 16)
        s_noted = ctx.enter_context(nc.semaphore("ad_noted"))
        s_noted_pool = ctx.enter_context(nc.semaphore("ad_noted_pool"))
        s_noted_dve = ctx.enter_context(nc.semaphore("ad_noted_dve"))
        s_pad = sig("x_padded", 1)
        s_bias = sig("bias_added", 1)
        s_xturn = sig("x_turned", G)
        s_xt = sig("x_t_copied", G)
        s_cturn = sig("c_turned", 1)
        s_ct = sig("c_t_copied", 1)
        s_ctall = sig("c_t_kept", 1)
        s_crep = sig("c_rep_made", 1)
        s_q1p = sig("q1_projected", 1)
        s_q1 = sig("q1_placed", HG)
        s_kp = sig("k_projected", 1)
        s_kd = sig("k_placed", 2 * HG)
        s_vp = sig("v_projected", 1)
        s_vd = sig("v_placed", 2)
        s_qp = sig("q_projected", G)
        s_q = sig("q_copied", G)
        s_s1 = sig("scores1_made", H0)
        s_max1 = sig("max1_made", H0)
        s_exp1 = sig("exp1_made", H0)
        s_inv1 = sig("inverse1_made", H0)
        s_norm1 = sig("probs1_scaled", H0)
        s_turn1 = sig("turned1_made", H0, N1)
        s_evac1 = sig("turned1_copied", H0, 2)
        s_pv1 = sig("pv1_made", H0, 2)
        s_s = sig("scores_made", QT)
        s_max = sig("max_made", QT)
        s_sub = sig("shifted", QT)
        s_exp = sig("exp_made", QT)
        s_sum = sig("sum_made", QT)
        s_inv = sig("inverse_made", QT)
        s_norm = sig("probs_scaled", QT)
        s_hs1 = sig("hs1_copied", 1)
        s_q2p = sig("q2_projected", 1)
        s_q2 = sig("q2_copied", 1)
        s_s2 = sig("scores2_made", 1)
        s_soft2 = sig("softmax2_steps", 6)
        s_px = sig("probs2_expanded", 1)
        s_p2x = sig("probs2x_copied", 1)
        s_turn = sig("turned_made", H0, 1)
        s_evac = [sig(f"turned_copied{i}", H0 // 2, 1) for i in range(2)]
        s_pv = sig("pv_made", H0, 2)
        s_add2 = sig("adapter_added", G, G)
        s_heads = sig("heads_copied", G)
        s_o = sig("out_projected", 2, 1)
        s_x = sig("x_updated", QT, QT)
        N_W, N_WO = 6, H0 + 2

        block = ctx.enter_context(nc.Block())

        @block.sync
        def _(sp):
            rows = t["ctx_768"]

            def load_context(b):
                sp.dma_start(context[:], rows[bass.ds(b, 1), :, :].rearrange("a k c -> (a k) c")).then_inc(s_ctx.sem, 16)
                sp.dma_start(tokens[:], rows[bass.ds(b, 1), SE:SK, :].rearrange("a k c -> (a k) c")).then_inc(s_ctx.sem, 16)

            tiles = t["x"].rearrange("b (q p) d -> p (b q) d", p=P)
            sp.dma_start(ident[:], t["ident"]).then_inc(s_in, 16)
            load_context(0)
            sp.dma_start(x[:, 0:QT, :], tiles[:, 0:QT, :]).then_inc(s_in, 16)
            sp.dma_start(own[:], t["own"]).then_inc(s_w, 16)
            sp.wait_ge(s_zero, 5)
            by_head = lambda ap: ap.rearrange("r (h c) -> r h c", h=H0)
            for tile, name in ((wq_ca, "Wq_ca"), (wk, "Wk"), (wk_ca, "Wk_ca"), (wv, "Wv"), (wv_ca, "Wv_ca")):
                sp.dma_start(tile[:, :, 0:HD0], by_head(w(name))).then_inc(s_w, 16)
            sp.wait_ge(s_zero, 8)
            to = lambda h: slice(HP * (h % HG), HP * (h % HG) + HD0)
            for h in range(H0):
                sp.dma_start(wq[to(h), h // HG, :, 0:HD0], by_head(w("Wq")[h * HD0:(h + 1) * HD0, :])).then_inc(s_wq, 16)
            sp.dma_start(x[:, QT:, :], tiles[:, QT:, :]).then_inc(s_xrest, 16)
            sp.dma_start(b_o[:], w("b_out").unsqueeze(0).broadcast_to([P, D])).then_inc(s_wo, 16)
            sp.dma_start(expand[:], t["expand"]).then_inc(s_wo, 16)
            for h in range(H0):
                sp.dma_start(wo[to(h), h // HG, :], w("Wout")[h * HD0:(h + 1) * HD0, :]).then_inc(s_wo, 16)
            for (weight, parts), raw in zip(splits, raws):
                parts.load(sp, weight, raw, s_raw)
            for tile, src in later:
                sp.dma_start(tile, src).then_inc(s_later, 16)
            with sp.Fori(1, B) as b:
                sp.wait_ge(s_vp.sem, s_vp.at(b, -1))
                sp.sem_inc(s_noted, 1)
                load_context(b)
            sp.wait_ge(s_later, 16 * len(later))

        @block.tensor
        def _(pe):
            for s in (s_turn1, s_pv1, s_turn, s_pv, s_add2, s_o):
                pe.sem_inc(s.sem, s.credit)
            next_ln.start_tensor(pe)
            pe.wait_ge(s_in, 32)

            def turn_inputs(b):
                pe.wait_ge(s_ctx.sem, s_ctx.at(b, 1))
                pe.transpose(banks[7][0:CTX, 0:SK], context[:], ident[0:SK, 0:SK]).then_inc(s_cturn.sem, 1)
                pe.wait_ge(s_pad.sem, s_pad.at(b, 0))
                for g in range(G):
                    for q in range(QT):
                        last = pe.transpose(banks[2 + g][:, q * P:(q + 1) * P], x_pad[:, q, g * HG:(g + 1) * HG, :].rearrange("p h c -> p (h c)"), ident[:])
                    last.then_inc(s_xturn.sem, 1)

            def project_context(b):
                pe.wait_ge(s_w, 16 * N_W)
                pe.wait_ge(s_ct.sem, s_ct.at(b, 0))
                for g in range(G):
                    pe.matmul(b_q1[:, g * CTX:(g + 1) * CTX], flat(wq_ca[:, g * HG:(g + 1) * HG, :]), tokens[:], start=True, stop=True)
                for g in range(G):
                    cols = slice(g * HG, (g + 1) * HG)
                    pe.matmul(b_k[:, g * SE:(g + 1) * SE], flat(wk[:, cols, :]), c_t[:, 0:SE], start=True, stop=True)
                    last = pe.matmul(b_k[:, G * SE + g * NCA:G * SE + (g + 1) * NCA], flat(wk_ca[:, cols, :]), c_t[:, SE:SK], start=True, stop=True)
                last.then_inc(s_kp.sem, 1)
                pe.wait_ge(s_crep.sem, s_crep.at(b, 0))
                pe.matmul(banks[4][0:SE, 0:HC], c_t[:, 0:SE], flat(wv[:]), start=True, stop=True)
                pe.matmul(banks[4][0:H0 * NCA, HC:2 * HC], flat(c_rep[:]), flat(wv_ca[:]), start=True, stop=True).then_inc(s_vp.sem, 1)

            def project_queries(b):
                pe.wait_ge(s_wq, 16 * H0)
                pe.wait_ge(s_xt.sem, s_xt.at(b, G - 1))
                for g in range(G):
                    for k in range(G):
                        last = pe.matmul(banks[2 + g], flat(wq[:, k, g * HG:(g + 1) * HG, :]), x_t[:, k, :], start=(k == 0), stop=(k == G - 1))
                    last.then_inc(s_qp.sem, 1)

            turn_inputs(0)
            project_context(0)
            project_queries(0)

            def batch(b, more):
                def scores1(h):
                    if h == 0:
                        pe.wait_ge(s_q1.sem, s_q1.at(b, HG - 1))
                    if h >= 2:
                        pe.wait_ge(s_exp1.sem, s_exp1.at(b, h - 2))
                    pe.matmul(banks[h % 2][0:CTX, :], q1_diag[:, h, :], x_t[:, h // HG, :], start=True, stop=True).then_inc(s_s1.sem, 1)

                def scores(q):
                    if q == 0:
                        pe.wait_ge(s_q.sem, s_q.at(b, G - 1))
                        pe.wait_ge(s_kd.sem, s_kd.at(b, 2 * HG - 1))
                        pe.wait_ge(s_x.sem, s_x.at(b, -1))
                    else:
                        pe.wait_ge(s_sub.sem, s_sub.at(b, q - 1))
                    for g in range(G):
                        last = pe.matmul(banks[5 + g][:, 0:HG * SE], q_t[:, g, q * P:(q + 1) * P], k_diag[:, g, :, :].rearrange("p h k -> p (h k)"),
                                         start=True, stop=True)
                    last.then_inc(s_s.sem, 1)

                def turns1(h):
                    pe.wait_ge(s_norm1.sem, s_norm1.at(b, h))
                    if h >= 2:
                        pe.wait_ge(s_evac1.sem, s_evac1.at(b, h - 2))
                    for k in range(QT):
                        last = pe.transpose(banks[2 + h % 2][:, k * CTX:(k + 1) * CTX], probs1[:, h % N1, k * P:(k + 1) * P], ident[0:CTX, 0:CTX])
                    last.then_inc(s_turn1.sem, 1)

                def pv1(h):
                    g, j = divmod(h, HG)
                    pe.wait_ge(s_evac1.sem, s_evac1.at(b, h))
                    for k in range(QT):
                        last = pe.matmul(banks[7][j * HP:(j + 1) * HP, g * CTX:(g + 1) * CTX], x_pad[:, k, h, :], turned1[:, h % 2, k, :],
                                         start=(k == 0), stop=(k == QT - 1))
                    last.then_inc(s_pv1.sem, 1)

                for i in range(H0 + 4):
                    if i < H0:
                        scores1(i)
                    if i in SCORES_AT:
                        scores(SCORES_AT.index(i))
                    if 3 <= i < H0 + 3:
                        turns1(i - 3)
                    if i >= 4:
                        pv1(i - 4)

                def turns(h):
                    if h == 0:
                        pe.wait_ge(s_norm.sem, s_norm.at(b, QT - 1))
                        pe.wait_ge(s_evac1.sem, s_evac1.at(b, H0 - 1))
                    elif h >= 2:
                        pe.wait_ge(s_evac[h % 2].sem, s_evac[h % 2].at(b, h // 2 - 1))
                    for q in range(QT):
                        last = pe.transpose(banks[2 + h % 2][0:SE, q * P:(q + 1) * P], probs[:, q, h // HG, h % HG, :], ident[:])
                    last.then_inc(s_turn.sem, 1)

                def pv(h):
                    g, j = divmod(h, HG)
                    pe.wait_ge(s_evac[h % 2].sem, s_evac[h % 2].at(b, h // 2))
                    pe.matmul(banks[g][j * HP:(j + 1) * HP, :], v[:, h * HP:(h + 1) * HP], turned[:, h % 2, :],
                              start=True, stop=False, skip_group_check=True).then_inc(s_pv.sem, 1)

                turns(0)
                pe.wait_ge(s_hs1.sem, s_hs1.at(b, 0))
                for g in range(G):
                    for k in range(G):
                        last = pe.matmul(banks[7][:, g * CTX:(g + 1) * CTX], flat(wq[:, k, g * HG:(g + 1) * HG, :]), hs1[:, k, :], start=(k == 0), stop=(k == G - 1))
                last.then_inc(s_q2p.sem, 1)
                turns(1)
                pv(0)
                pe.wait_ge(s_q2.sem, s_q2.at(b, 0))
                for g in range(G):
                    last = pe.matmul(banks[7][0:CTX, g * HG * NCA:(g + 1) * HG * NCA], q2[:, g, :], k2_diag[:, g, :, :].rearrange("p h k -> p (h k)"), start=True, stop=True)
                last.then_inc(s_s2.sem, 1)
                for h in range(2, H0):
                    turns(h)
                    pv(h - 1)
                pv(H0 - 1)
                pe.wait_ge(s_wo, 16 * N_WO)
                pe.wait_ge(s_soft2.sem, s_soft2.at(b, 5))
                pe.matmul(banks[4][0:H0 * NCA, :], flat(probs2[:]), expand[:], start=True, stop=True).then_inc(s_px.sem, 1)
                if more:
                    turn_inputs(b + 1)
                else:
                    next_ln.turn(pe, 0, ident, banks[2:4], lambda i: None)
                pe.wait_ge(s_p2x.sem, s_p2x.at(b, 0))
                for g in range(G):
                    pe.matmul(banks[g], v2[:, g * P:(g + 1) * P], probs2x[:], start=False, stop=True, skip_group_check=True).then_inc(s_add2.sem, 1)
                if more:
                    project_context(b + 1)
                for half in range(2):
                    for i in range(2):
                        q = 2 * half + i
                        for g in range(G):
                            if q == 0:
                                pe.wait_ge(s_heads.sem, s_heads.at(b, g))
                            last = pe.matmul(banks[5 + half][:, i * D:(i + 1) * D], heads[:, g, q * P:(q + 1) * P], wo[:, g, :], start=(g == 0), stop=(g == G - 1))
                    last.then_inc(s_o.sem, 1)
                if more:
                    project_queries(b + 1)

            over_batches(pe, batch)

        @block.scalar
        def _(act):
            act.sem_inc(s_evac1.sem, s_evac1.credit)
            act.sem_inc(s_evac[0].sem, s_evac[0].credit)
            next_ln.start_scalar(act)

            def copy_context(b, first=False):
                act.wait_ge(s_cturn.sem, s_cturn.at(b, 0))
                if not first:
                    act.wait_ge(s_vp.sem, s_vp.at(b, -1))
                    act.wait_ge(s_ctall.sem, s_ctall.at(b, -1))
                act.copy(c_t[:], banks[7][0:CTX, 0:SK]).then_inc(s_ct.sem, 1)

            def copy_x(b):
                for g in range(G):
                    act.wait_ge(s_xturn.sem, s_xturn.at(b, g))
                    act.copy(x_t[:, g, :], banks[2 + g]).then_inc(s_xt.sem, 1)

            def copy_queries(b):
                for g in range(G):
                    act.wait_ge(s_qp.sem, s_qp.at(b, g))
                    act.activation(q_t[:, g, :], banks[2 + g], ACT.Copy, scale=SCALE0).then_inc(s_q.sem, 1)

            copy_context(0, first=True)
            copy_x(0)
            copy_queries(0)

            def batch(b, more):
                def exp1(h):
                    act.wait_ge(s_max1.sem, s_max1.at(b, h))
                    act.wait_ge(s_turn1.sem, s_turn1.at(b, h - N1))
                    act.activation(probs1[:, h % N1, :], banks[h % 2][0:CTX, :], ACT.Exp, bias=negmax1[:, h % N1:h % N1 + 1],
                                   accum_out=total1[:, h % N1:h % N1 + 1]).then_inc(s_exp1.sem, 1)

                def exp(q):
                    act.wait_ge(s_sub.sem, s_sub.at(b, q))
                    p = probs[:, q, :, :, :].rearrange("p g h k -> p (g h k)")
                    act.activation(p, p, ACT.Exp).then_inc(s_exp.sem, 1)

                def copy_turned1(h):
                    act.wait_ge(s_turn1.sem, s_turn1.at(b, h))
                    act.wait_ge(s_pv1.sem, s_pv1.at(b, h - 2))
                    act.copy(turned1[:, h % 2, :, :].rearrange("p k c -> p (k c)"), banks[2 + h % 2][:, 0:QT * CTX]).then_inc(s_evac1.sem, 1)

                for i in range(H0 + 3):
                    if i < H0:
                        exp1(i)
                    if i >= 3:
                        copy_turned1(i - 3)
                    if i in SCORES_AT:
                        exp(SCORES_AT.index(i))
                act.wait_ge(s_pv1.sem, s_pv1.at(b, H0 - 1))
                act.copy(flat(hs1[:]), banks[7][:, 0:G * CTX]).then_inc(s_hs1.sem, 1)

                for h in range(0, H0, 2):
                    act.wait_ge(s_turn.sem, s_turn.at(b, h))
                    act.wait_ge(s_pv.sem, s_pv.at(b, h - 2))
                    act.copy(turned[:, h % 2, :], banks[2 + h % 2][0:SE, :]).then_inc(s_evac[0].sem, 1)
                    if h == 0:
                        act.wait_ge(s_q2p.sem, s_q2p.at(b, 0))
                        act.activation(flat(q2[:]), banks[7][:, 0:G * CTX], ACT.Copy, scale=SCALE0).then_inc(s_q2.sem, 1)
                    if h == 2:
                        act.wait_ge(s_soft2.sem, s_soft2.at(b, 1))
                        act.activation(flat(probs2[:]), flat(probs2[:]), ACT.Exp).then_inc(s_soft2.sem, 1)
                act.wait_ge(s_raw, 16 * Split.LOADS * len(splits))
                for (_, parts), raw in zip(splits, raws):
                    parts.round(act, raw, columns(b), s_rounded.sem)
                act.wait_ge(s_px.sem, s_px.at(b, 0))
                act.wait_ge(s_add2.sem, s_add2.at(b, -1))
                act.copy(probs2x[:], banks[4][0:H0 * NCA, :]).then_inc(s_p2x.sem, 1)
                if more:
                    copy_context(b + 1)
                    copy_x(b + 1)
                act.wait_ge(s_o.sem, s_o.at(b, -1))
                for g in range(G):
                    act.wait_ge(s_add2.sem, s_add2.at(b, g))
                    act.copy(heads[:, g, :], banks[g]).then_inc(s_heads.sem, 1)
                if more:
                    copy_queries(b + 1)
                else:
                    act.wait_ge(s_later, 16 * len(later))
                    next_ln.scale_and_round(act, 0, banks[2:4], lambda eng: None)

            over_batches(act, batch)

        @block.vector
        def _(dve):
            dve.sem_inc(s_x.sem, s_x.credit)
            dve.sem_inc(s_evac[1].sem, s_evac[1].credit)
            next_ln.start_vector(dve)
            for tile in (q1_diag, k_diag, k2_diag):
                dve.memset(tile[:], 0.0).then_inc(s_zero_diag, 1)
            dve.wait_ge(s_zero_diag, 3)
            dve.wait_ge(s_zero, 6)
            dve.wait_ge(s_in, 32)

            def pad_x(b):
                xb = x[:, bass.ds(b * QT, QT), :]
                dve.wait_ge(s_pv1.sem, s_pv1.at(b, -1))
                dve.sem_inc(s_noted_dve, 1)
                dve.tensor_copy(x_pad[:, :, :, 0:HD0].rearrange("p q h c -> p (q h) c"),
                                xb.rearrange("p q (h c) -> p (q h) c", h=H0)).then_inc(s_pad.sem, 1)

            def repeat_context(b):
                dve.wait_ge(s_ct.sem, s_ct.at(b, 0))
                dve.tensor_copy(c_rep[:], c_t[:, SE:SK].unsqueeze(1).broadcast_to([CTX, H0, NCA])).then_inc(s_crep.sem, 1)

            def place_context(b):
                dve.wait_ge(s_kp.sem, s_kp.at(b, 0))
                for j in range(HG):
                    rows = slice(j * HP, (j + 1) * HP)
                    dve.tensor_scalar(q1_diag[rows, j::HG, :], b_q1[rows, :].rearrange("p (g c) -> p g c", g=G),
                                      SCALE0, None, ALU.mult).then_inc(s_q1.sem, 1)
                for j in range(HG):
                    rows = slice(j * HP, (j + 1) * HP)
                    dve.tensor_copy(k_diag[rows, :, j, :], b_k[rows, 0:G * SE].rearrange("p (g k) -> p g k", g=G)).then_inc(s_kd.sem, 1)
                    dve.tensor_copy(k2_diag[rows, :, j, :], b_k[rows, G * SE:G * (SE + NCA)].rearrange("p (g k) -> p g k", g=G)).then_inc(s_kd.sem, 1)
                dve.wait_ge(s_vp.sem, s_vp.at(b, 0))
                dve.wait_ge(s_add2.sem, s_add2.at(b, -1))
                dve.wait_ge(s_w, 16 * N_W)
                dve.tensor_copy(v[:], banks[4][0:SE, 0:HC]).then_inc(s_vd.sem, 1)
                dve.tensor_tensor(v2[:], banks[4][0:H0 * NCA, HC:2 * HC], own[:], ALU.mult).then_inc(s_vd.sem, 1)

            pad_x(0)
            repeat_context(0)
            place_context(0)

            def batch(b, more):
                def max1(h):
                    dve.wait_ge(s_s1.sem, s_s1.at(b, h))
                    dve.tensor_reduce(negmax1[:, h % N1:h % N1 + 1], banks[h % 2][0:CTX, :], AX_X, ALU.max, negate=True).then_inc(s_max1.sem, 1)

                def inverses1(h):
                    dve.wait_ge(s_exp1.sem, s_exp1.at(b, h))
                    dve.reciprocal(inverse1[:, h % N1:h % N1 + 1], total1[:, h % N1:h % N1 + 1]).then_inc(s_inv1.sem, 1)

                heads_of = lambda q: probs[:, q, :, :, :].rearrange("p g h k -> p (g h) k")

                def shift(q):
                    s4 = banks.pair(5)[:, :, 0:HG * SE].rearrange("p g (h k) -> p g h k", h=HG)
                    m = top[:, q, :].rearrange("p (g h) -> p g h", g=G)
                    dve.wait_ge(s_s.sem, s_s.at(b, q))
                    dve.tensor_reduce(m, s4, AX_X, ALU.max).then_inc(s_max.sem, 1)
                    dve.wait_ge(s_max.sem, s_max.at(b, q))
                    if q == 0:
                        dve.wait_ge(s_turn.sem, s_turn.at(b, -1))
                    dve.tensor_tensor(probs[:, q, :, :, :], s4, m.unsqueeze(3).broadcast_to([P, G, HG, SE]), ALU.subtract).then_inc(s_sub.sem, 1)

                def inverses(q):
                    dve.wait_ge(s_exp.sem, s_exp.at(b, q))
                    dve.tensor_reduce(total[:, q, :], heads_of(q), AX_X, ALU.add).then_inc(s_sum.sem, 1)
                    dve.wait_ge(s_sum.sem, s_sum.at(b, q))
                    dve.reciprocal(inverse[:, q, :], total[:, q, :]).then_inc(s_inv.sem, 1)

                def copy_turned(h):
                    dve.wait_ge(s_turn.sem, s_turn.at(b, h))
                    dve.wait_ge(s_pv.sem, s_pv.at(b, h - 2))
                    dve.tensor_copy(turned[:, h % 2, :], banks[2 + h % 2][0:SE, :]).then_inc(s_evac[1].sem, 1)

                if not more:
                    next_ln.statistics(dve, 0)
                for i in range(H0 + 1):
                    if not more and i == H0 // 2:
                        next_ln.standardize(dve, 0)
                    if i < H0:
                        max1(i)
                    if i >= 1:
                        inverses1(i - 1)
                    if i in SCORES_AT:
                        shift(SCORES_AT.index(i))
                    if i in INVERSES_AT:
                        inverses(INVERSES_AT.index(i))
                s3 = banks[7][0:CTX, 0:H0 * NCA].rearrange("p (h k) -> p h k", h=H0)
                spread = lambda tile: tile[:].unsqueeze(2).broadcast_to([CTX, H0, NCA])
                copy_turned(1)
                dve.wait_ge(s_s2.sem, s_s2.at(b, 0))
                dve.tensor_reduce(top2[:], s3, AX_X, ALU.max).then_inc(s_soft2.sem, 1)
                dve.wait_ge(s_soft2.sem, s_soft2.at(b, 0))
                dve.tensor_tensor(probs2[:], s3, spread(top2), ALU.subtract).then_inc(s_soft2.sem, 1)
                copy_turned(3)
                dve.wait_ge(s_soft2.sem, s_soft2.at(b, 2))
                dve.tensor_reduce(total2[:], probs2[:], AX_X, ALU.add).then_inc(s_soft2.sem, 1)
                dve.wait_ge(s_soft2.sem, s_soft2.at(b, 3))
                dve.reciprocal(inverse2[:], total2[:]).then_inc(s_soft2.sem, 1)
                dve.wait_ge(s_soft2.sem, s_soft2.at(b, 4))
                dve.tensor_tensor(probs2[:], probs2[:], spread(inverse2), ALU.mult).then_inc(s_soft2.sem, 1)
                copy_turned(5)
                if more:
                    dve.wait_ge(s_xrest, 16)
                    pad_x(b + 1)
                copy_turned(7)
                if more:
                    repeat_context(b + 1)
                    place_context(b + 1)
                for i, ((_, parts), raw) in enumerate(zip(splits, raws)):
                    dve.wait_ge(s_rounded.sem, s_rounded.at(b, Split.ROUNDED * (i + 1) - 1))
                    parts.rest(dve, raw, columns(b), s_rest.sem)
                dve.wait_ge(s_bias.sem, s_bias.at(b, 0))
                for half in range(2):
                    dve.wait_ge(s_o.sem, s_o.at(b, half))
                    for i in range(2):
                        xt = x[:, bass.ds(b * QT + 2 * half + i, 1), :].rearrange("p a d -> p (a d)")
                        dve.tensor_tensor(xt, banks[5 + half][:, i * D:(i + 1) * D], xt, ALU.add).then_inc(s_x.sem, 1)
                if not more:
                    next_ln.remainder(dve, 0, lambda eng: None)

            over_batches(dve, batch)

        @block.gpsimd
        def _(pool):
            next_ln.start_gpsimd(pool)
            for tile in (wq_ca, wk, wk_ca, wv, wv_ca, x_pad, wq, wo):
                pool.memset(tile[:], 0.0).then_inc(s_zero, 1)
            pool.wait_ge(s_zero, 8)
            pool.wait_ge(s_in, 32)
            pool.wait_ge(s_wo, 16 * N_WO)

            def batch(b, more):
                if not more:
                    next_ln.deviations(pool, 0)
                xb = x[:, bass.ds(b * QT, QT), :]
                pool.wait_ge(s_pad.sem, s_pad.at(b, 0))
                pool.tensor_tensor(xb, xb, b_o[:].unsqueeze(1).broadcast_to([P, QT, D]), ALU.add).then_inc(s_bias.sem, 1)
                pool.wait_ge(s_ct.sem, s_ct.at(b, 0))
                pool.sem_inc(s_noted_pool, 1)
                pool.tensor_copy(ctx_t[:, bass.ds(b, 1), :].rearrange("p a k -> p (a k)"), c_t[:]).then_inc(s_ctall.sem, 1)
                for h in range(H0):
                    pool.wait_ge(s_inv1.sem, s_inv1.at(b, h))
                    pool.sem_inc(s_noted_pool, 1)
                    pool.tensor_scalar(probs1[:, h % N1, :], probs1[:, h % N1, :], inverse1[:, h % N1:h % N1 + 1], 1.0, ALU.mult, ALU.mult).then_inc(s_norm1.sem, 1)
                    if h in INVERSES_AT:
                        q = INVERSES_AT.index(h)
                        p = probs[:, q, :, :, :].rearrange("p g h k -> p (g h) k")
                        pool.wait_ge(s_inv.sem, s_inv.at(b, q))
                        pool.tensor_tensor(p, p, inverse[:, q, :].unsqueeze(2).broadcast_to([P, H0, SE]), ALU.mult).then_inc(s_norm.sem, 1)

            over_batches(pool, batch)


def crossattn(nc, x, ident, ln, next_ln, ctx_t, w_q, w_k, w_v, w_o, bias_o, banks, next_w, next_parts, raw, later):
    BUFS = 5
    LN_AT = 3
    SPLIT_AT = 7
    with ExitStack() as ctx:
        sb = lambda n, s, d=F32: ctx.enter_context(nc.sbuf_tensor("ca_" + n, s, d))
        sig = lambda n, per, credit=0, step=1: Signal(ctx, nc, "ca_" + n, per, credit, step)
        ctx_b = sb("ctx_b", [CTX, SK])
        q_sb = sb("q", [P, BUFS, S])
        k_diag = sb("k_diag", [P, BUFS, 2, SK])
        v_sb = sb("v", [SK, BUFS, P])
        probs = sb("probs", [P, BUFS, QT, 2, SK])
        turned = sb("turned", [SK, 2, S])
        att = sb("att", [P, NPAIR, S])
        top = sb("top", [P, BUFS, 2 * QT])
        total = sb("total", [P, BUFS, 2 * QT])
        inverse = sb("inverse", [P, BUFS, 2 * QT])

        b_proj, b_kv, b_turn, b_out = banks[0], banks[1], banks[2:4], banks[4:6]
        b_scores = banks.pair(6)
        used = 2 * 2 * SK
        scores_ap = b_scores[:, :, 0:used]
        b_ln = [b_proj, b_kv]

        s_zero = sig("diag_cleared", 1)
        s_ctx = sig("ctx_copied", 1)
        s_noted = ctx.enter_context(nc.semaphore("ca_use_noted"))
        s_q = sig("q_projected", NPAIR, 2)
        s_kv = sig("kv_projected", NPAIR, 2)
        s_qsb = sig("q_copied", NPAIR, 2)
        s_ksb = sig("k_copied", 3 * NPAIR, 6)
        s_scores = sig("scores_made", NPAIR, BUFS)
        s_max = sig("max_made", NPAIR)
        s_sub = sig("shifted", NPAIR, 2)
        s_exp = sig("exp_made", NPAIR)
        s_sum = sig("sum_made", NPAIR)
        s_inv = sig("inverse_made", NPAIR)
        s_norm = sig("probs_scaled", NPAIR)
        s_turn = sig("turned_made", 2 * NPAIR, 2 * BUFS)
        s_evac = sig("turned_copied", 2 * NPAIR, 2)
        s_pv = sig("pv_made", 2 * NPAIR, 2 * BUFS)
        s_att = sig("att_copied", NPAIR, 2)
        s_o = sig("out_projected", 2, 2)
        s_bias = sig("bias_added", 1)
        s_x = sig("x_updated", QT, QT)

        s_raw, s_later = (ctx.enter_context(nc.semaphore(f"ca_{n}_loaded")) for n in ("raw", "later"))
        s_rounded = sig("next_rounded", Split.ROUNDED)
        s_rest = sig("next_rest", Split.REST)
        columns = lambda b: bass.ds(b * (INNER // B), INNER // B)

        def following(b, more):
            return (ln, b + 1, b + 1) if more else (next_ln, b + 1, 0)

        def ahead(step, b, j, more):
            if j < NPAIR:
                step(b, j)
            elif more:
                step(b + 1, j - NPAIR)

        block = ctx.enter_context(nc.Block())

        @block.sync
        def _(sp):
            next_parts.load(sp, next_w, raw, s_raw)
            for tile, src in later:
                sp.dma_start(tile, src).then_inc(s_later, 16)
            sp.wait_ge(s_later, 16 * len(later))

        @block.tensor
        def _(pe):
            for s in (s_q, s_kv, s_scores, s_turn, s_pv, s_o):
                pe.sem_inc(s.sem, s.credit)

            def turn_norm(norm, b, nb):
                def bank_free(i):
                    if i == 0:
                        pe.wait_ge(s_qsb.sem, s_qsb.at(b, -1))
                    else:
                        pe.wait_ge(s_ksb.sem, s_ksb.at(b, -1))
                norm.turn(pe, nb, ident, b_ln, bank_free)

            def project(b, j):
                if j == 0:
                    ln.ready(pe, b)
                    pe.wait_ge(s_ctx.sem, s_ctx.at(b, 0))
                pe.wait_ge(s_qsb.sem, s_qsb.at(b, j - 1))
                ln.project(pe, b_proj, w_q, j * P).then_inc(s_q.sem, 1)
                pe.wait_ge(s_ksb.sem, s_ksb.at(b, 3 * j - 1))
                pe.matmul(b_kv[:, 0:SK], w_k[:, j * P:(j + 1) * P], ctx_b[:], start=True, stop=True)
                pe.matmul(b_kv[0:SK, P:2 * P], ctx_b[:], w_v[:, j * P:(j + 1) * P], start=True, stop=True).then_inc(s_kv.sem, 1)

            def scores(b, j):
                pe.wait_ge(s_qsb.sem, s_qsb.at(b, j))
                pe.wait_ge(s_ksb.sem, s_ksb.at(b, 3 * j + 2))
                pe.wait_ge(s_sub.sem, s_sub.at(b, j - 1))
                for q in range(QT):
                    last = pe.matmul(b_scores[:, q // 2, (q % 2) * 2 * SK:(q % 2 + 1) * 2 * SK], q_sb[:, j % BUFS, q * P:(q + 1) * P],
                                     k_diag[:, j % BUFS, :, :], start=True, stop=True)
                last.then_inc(s_scores.sem, 1)

            def turns(b, j):
                pe.wait_ge(s_norm.sem, s_norm.at(b, j))
                for e in range(2):
                    pe.wait_ge(s_evac.sem, s_evac.at(b, 2 * j + e - 2))
                    for q in range(QT):
                        last = pe.transpose(b_turn[e][0:SK, q * P:(q + 1) * P], probs[:, j % BUFS, q, e, :], ident[:])
                    last.then_inc(s_turn.sem, 1)

            def pv(b, j):
                if j >= 2:
                    pe.wait_ge(s_att.sem, s_att.at(b, j - 2))
                else:
                    pe.wait_ge(s_x.sem, s_x.at(b, 2 * j + 1 - QT))
                for e in range(2):
                    pe.wait_ge(s_evac.sem, s_evac.at(b, 2 * j + e))
                    pe.matmul(b_out[j % 2][e * HD:(e + 1) * HD, :], v_sb[:, j % BUFS, e * HD:(e + 1) * HD],
                              turned[:, e, :], start=True, stop=True).then_inc(s_pv.sem, 1)

            def project_out(b):
                for half in range(2):
                    for t in range(2):
                        q = 2 * half + t
                        for j in range(NPAIR):
                            if q == 0:
                                pe.wait_ge(s_att.sem, s_att.at(b, NPAIR - 2 if j < NPAIR - 1 else NPAIR - 1))
                            last = pe.matmul(b_out[half][:, t * D:(t + 1) * D], att[:, j, q * P:(q + 1) * P],
                                             w_o[:, j, :], start=(j == 0), stop=(j == NPAIR - 1))
                    last.then_inc(s_o.sem, 1)

            pe.wait_ge(s_zero.sem, 1)
            project(0, 0)
            project(0, 1)
            scores(0, 0)
            project(0, 2)
            scores(0, 1)

            def batch(b, more):
                for j in range(NPAIR):
                    ahead(scores, b, j + 2, more)
                    turns(b, j)
                    ahead(project, b, j + 3, more)
                    if j == NPAIR - 4:
                        turn_norm(*following(b, more))
                    pv(b, j)
                project_out(b)

            over_batches(pe, batch)

        @block.scalar
        def _(act):
            for s in (s_qsb, s_evac, s_att):
                act.sem_inc(s.sem, s.credit)

            def operands_free(b):
                def wait(eng):
                    eng.wait_ge(s_q.sem, s_q.at(b, -1))
                return wait

            def copy_q(b, j):
                act.wait_ge(s_q.sem, s_q.at(b, j))
                act.wait_ge(s_scores.sem, s_scores.at(b, j - BUFS))
                act.activation(q_sb[:, j % BUFS, :], b_proj, ACT.Copy, scale=SCALE1).then_inc(s_qsb.sem, 1)

            def exps(b, j):
                act.wait_ge(s_sub.sem, s_sub.at(b, j))
                p = probs[:, j % BUFS, :, :, :].rearrange("p a b c -> p (a b c)")
                act.activation(p, p, ACT.Exp).then_inc(s_exp.sem, 1)

            def copy_turned(b, j):
                for e in range(2):
                    act.wait_ge(s_turn.sem, s_turn.at(b, 2 * j + e))
                    act.wait_ge(s_pv.sem, s_pv.at(b, 2 * j + e - 2))
                    act.copy(turned[:, e, :], b_turn[e][0:SK, :]).then_inc(s_evac.sem, 1)

            def copy_att(b, j):
                act.wait_ge(s_pv.sem, s_pv.at(b, 2 * j + 1))
                act.wait_ge(s_o.sem, s_o.at(b, -1))
                act.copy(att[:, j, :], b_out[j % 2]).then_inc(s_att.sem, 1)

            copy_q(0, 0)
            copy_q(0, 1)
            exps(0, 0)
            copy_q(0, 2)
            exps(0, 1)

            def batch(b, more):
                for j in range(NPAIR):
                    if j >= 1:
                        copy_att(b, j - 1)
                    copy_turned(b, j)
                    ahead(copy_q, b, j + 3, more)
                    ahead(exps, b, j + 2, more)
                    if j == NPAIR - 4:
                        norm, _, nb = following(b, more)
                        norm.scale_and_round(act, nb, b_ln, operands_free(b + 1))
                    if j == SPLIT_AT:
                        act.wait_ge(s_raw, 16 * Split.LOADS)
                        next_parts.round(act, raw, columns(b), s_rounded.sem)
                copy_att(b, NPAIR - 1)

            over_batches(act, batch)

        @block.vector
        def _(dve):
            for s in (s_ksb, s_sub, s_x):
                dve.sem_inc(s.sem, s.credit)
            dve.memset(k_diag[:], 0.0).then_inc(s_zero.sem, 1)
            dve.wait_ge(s_zero.sem, 1)

            def operands_free(b):
                def wait(eng):
                    eng.wait_ge(s_q.sem, s_q.at(b, -1))
                return wait

            def copy_kv(b, j):
                dve.wait_ge(s_kv.sem, s_kv.at(b, j))
                dve.wait_ge(s_scores.sem, s_scores.at(b, j - BUFS))
                for e in range(2):
                    rows = slice(e * HD, (e + 1) * HD)
                    dve.tensor_copy(k_diag[rows, j % BUFS, e, :], b_kv[rows, 0:SK]).then_inc(s_ksb.sem, 1)
                dve.wait_ge(s_pv.sem, s_pv.at(b, 2 * (j - BUFS) + 1))
                dve.tensor_copy(v_sb[:, j % BUFS, :], b_kv[0:SK, P:2 * P]).then_inc(s_ksb.sem, 1)

            def shift(b, j):
                s4 = scores_ap.rearrange("p a (c k) -> p a c k", k=SK)
                p = probs[:, j % BUFS, :, :, :].rearrange("p (a q) e k -> p a (q e) k", a=2)
                m = top[:, j % BUFS, :]
                dve.wait_ge(s_scores.sem, s_scores.at(b, j))
                dve.tensor_reduce(m, s4, AX_X, ALU.max).then_inc(s_max.sem, 1)
                dve.wait_ge(s_max.sem, s_max.at(b, j))
                dve.wait_ge(s_turn.sem, s_turn.at(b, 2 * (j - BUFS) + 1))
                dve.tensor_tensor(p, s4, m.rearrange("p (a c) -> p a c", a=2).unsqueeze(3).broadcast_to([P, 2, QT, SK]),
                                  ALU.subtract).then_inc(s_sub.sem, 1)

            def invert(b, j):
                p = probs[:, j % BUFS, :, :, :].rearrange("p q e k -> p (q e) k")
                dve.wait_ge(s_exp.sem, s_exp.at(b, j))
                dve.tensor_reduce(total[:, j % BUFS, :], p, AX_X, ALU.add).then_inc(s_sum.sem, 1)
                dve.wait_ge(s_sum.sem, s_sum.at(b, j))
                dve.reciprocal(inverse[:, j % BUFS, :], total[:, j % BUFS, :]).then_inc(s_inv.sem, 1)

            def update(b):
                dve.wait_ge(s_bias.sem, s_bias.at(b, 0))
                for half in range(2):
                    dve.wait_ge(s_o.sem, s_o.at(b, half))
                    for t in range(2):
                        xt = x[:, bass.ds(b * QT + 2 * half + t, 1), :].rearrange("p a d -> p (a d)")
                        dve.tensor_tensor(xt, b_out[half][:, t * D:(t + 1) * D], xt, ALU.add).then_inc(s_x.sem, 1)

            copy_kv(0, 0)
            copy_kv(0, 1)
            shift(0, 0)
            copy_kv(0, 2)
            invert(0, 0)
            shift(0, 1)

            def batch(b, more):
                for j in range(NPAIR):
                    ahead(invert, b, j + 1, more)
                    ahead(shift, b, j + 2, more)
                    ahead(copy_kv, b, j + 3, more)
                    if j == SPLIT_AT + 1:
                        dve.wait_ge(s_rounded.sem, s_rounded.at(b, Split.ROUNDED - 1))
                        next_parts.rest(dve, raw, columns(b), s_rest.sem)
                    norm, _, nb = following(b, more)
                    if j == LN_AT:
                        norm.statistics(dve, nb)
                    if j == LN_AT + 1:
                        norm.standardize(dve, nb)
                    if j == NPAIR - 4:
                        norm.remainder(dve, nb, operands_free(b + 1))
                update(b)

            over_batches(dve, batch)

        @block.gpsimd
        def _(pool):
            def add_bias(b):
                pool.wait_ge(ln.s_hat.sem, ln.s_hat.at(ln.before + b, QT - 1))
                xt = x[:, bass.ds(b * QT, QT), :]
                pool.tensor_tensor(xt, xt, bias_o[:].unsqueeze(1).broadcast_to([P, QT, D]), ALU.add).then_inc(s_bias.sem, 1)

            def copy_context(b):
                pool.wait_ge(s_kv.sem, s_kv.at(b, -1))
                pool.sem_inc(s_noted, 1)
                pool.tensor_copy(ctx_b[:], ctx_t[:, bass.ds(b, 1), :].rearrange("p a k -> p (a k)")).then_inc(s_ctx.sem, 1)

            def scale(b, j):
                p = probs[:, j % BUFS, :, :, :].rearrange("p q e k -> p (q e) k")
                pool.wait_ge(s_inv.sem, s_inv.at(b, j))
                pool.tensor_tensor(p, p, inverse[:, j % BUFS, :].unsqueeze(2).broadcast_to([P, 2 * QT, SK]), ALU.mult).then_inc(s_norm.sem, 1)

            add_bias(0)
            copy_context(0)
            scale(0, 0)

            def batch(b, more):
                for j in range(NPAIR):
                    ahead(scale, b, j + 1, more)
                    if j == LN_AT + 1:
                        norm, _, nb = following(b, more)
                        norm.deviations(pool, nb)
                        if more:
                            add_bias(b + 1)
                    if more and j == NPAIR - 4:
                        copy_context(b + 1)

            over_batches(pool, batch)


def feedfwd(nc, x, ident, ln, w_1, b_1, w_2, bias_o, banks, out):
    with ExitStack() as ctx:
        sb = lambda n, s, d=F32: ctx.enter_context(nc.sbuf_tensor("ff_" + n, s, d))
        sig = lambda n, per, credit=0, step=1: Signal(ctx, nc, "ff_" + n, per, credit, step)
        gate = sb("gate", [P, 2, S])
        h = sb("h", [P, NF, S])

        b_gate, b_a, b_out, b_ln = banks[0:2], banks[2:4], banks[4:6], banks[6:8]

        s_g = sig("gate_projected", NF)
        s_a = sig("a_projected", NF, 1)
        s_gelu = sig("gelu_made", NF, 1)
        s_h = sig("h_made", NF, 2)
        s_o = sig("out_projected", 2, 1)
        s_bias = sig("bias_added", 1)
        s_x = sig("x_updated", QT, QT)
        s_out = sig("out_stored", 1, 0, 16)
        s_noted = ctx.enter_context(nc.semaphore("ff_x_noted"))

        block = ctx.enter_context(nc.Block())

        @block.tensor
        def _(pe):
            for s in (s_a, s_o):
                pe.sem_inc(s.sem, s.credit)

            def turn_norm(b):
                ln.turn(pe, b, ident, b_ln, lambda i: pe.wait_ge(ln.s_full.sem, ln.s_full.at(ln.before + b, i - 2)))

            def batch(b, more):
                ln.ready(pe, b)
                for m in range(NF):
                    before = max(m - 2, -1)
                    pe.wait_ge(s_gelu.sem, s_gelu.at(b, before))
                    ln.project(pe, b_gate[m % 2], w_1, DFF + m * P).then_inc(s_g.sem, 1)
                    pe.wait_ge(s_h.sem, s_h.at(b, before))
                    ln.project(pe, b_a[m % 2], w_1, m * P).then_inc(s_a.sem, 1)
                    if more and m == NF - 3:
                        turn_norm(b + 1)
                for half in range(2):
                    pe.wait_ge(s_x.sem, s_x.at(b, 2 * half + 1 - QT))
                    for t in range(2):
                        q = 2 * half + t
                        for m in range(NF):
                            if q == 0:
                                pe.wait_ge(s_h.sem, s_h.at(b, m))
                            last = pe.matmul(b_out[half][:, t * D:(t + 1) * D], h[:, m, q * P:(q + 1) * P],
                                             w_2[:, m, :], start=(m == 0), stop=(m == NF - 1))
                    last.then_inc(s_o.sem, 1)

            over_batches(pe, batch)

        @block.scalar
        def _(act):
            act.sem_inc(s_gelu.sem, 1)

            def operands_free(b):
                return lambda eng: eng.wait_ge(s_a.sem, s_a.at(b, -1))

            def batch(b, more):
                for m in range(NF):
                    act.wait_ge(s_g.sem, s_g.at(b, m))
                    act.wait_ge(s_h.sem, s_h.at(b, max(m - 2, -1)))
                    act.activation(gate[:, m % 2, :], b_gate[m % 2], ACT.Gelu_apprx_tanh, bias=b_1[:, NF + m:NF + m + 1]).then_inc(s_gelu.sem, 1)
                    if more and m == NF - 3:
                        ln.scale(act, b + 1, b_ln)
                if more:
                    ln.round(act, b + 1, operands_free(b + 1))

            over_batches(act, batch)

        @block.vector
        def _(dve):
            for s in (s_h, s_x):
                dve.sem_inc(s.sem, s.credit)

            def operands_free(b):
                return lambda eng: eng.wait_ge(s_a.sem, s_a.at(b, -1))

            def batch(b, more):
                if more:
                    ln.statistics(dve, b + 1)
                for m in range(NF):
                    dve.wait_ge(s_a.sem, s_a.at(b, m))
                    dve.wait_ge(s_gelu.sem, s_gelu.at(b, m))
                    dve.wait_ge(s_o.sem, s_o.at(b, -1))
                    dve.scalar_tensor_tensor(out=h[:, m, :], in0=b_a[m % 2], scalar=b_1[:, m:m + 1], in1=gate[:, m % 2, :],
                                             op0=ALU.add, op1=ALU.mult).then_inc(s_h.sem, 1)
                    if more and m == 0:
                        ln.standardize(dve, b + 1)
                if more:
                    ln.remainder(dve, b + 1, operands_free(b + 1))
                dve.wait_ge(s_bias.sem, s_bias.at(b, 0))
                for half in range(2):
                    dve.wait_ge(s_o.sem, s_o.at(b, half))
                    for t in range(2):
                        xt = x[:, bass.ds(b * QT + 2 * half + t, 1), :].rearrange("p a d -> p (a d)")
                        dve.tensor_tensor(xt, b_out[half][:, t * D:(t + 1) * D], xt, ALU.add).then_inc(s_x.sem, 1)

            over_batches(dve, batch)

        @block.gpsimd
        def _(pool):
            def batch(b, more):
                if more:
                    ln.deviations(pool, b + 1)
                pool.wait_ge(ln.s_hat.sem, ln.s_hat.at(ln.before + b, QT - 1))
                xt = x[:, bass.ds(b * QT, QT), :]
                pool.tensor_tensor(xt, xt, bias_o[:].unsqueeze(1).broadcast_to([P, QT, D]), ALU.add).then_inc(s_bias.sem, 1)

            over_batches(pool, batch)

        @block.sync
        def _(sp):
            tiles = out.rearrange("b (q p) d -> p (b q) d", p=P)
            with sp.Fori(0, B) as b:
                sp.wait_ge(s_x.sem, s_x.at(b, QT - 1))
                sp.sem_inc(s_noted, 1)
                sp.dma_start(tiles[:, bass.ds(b * QT, QT), :], x[:, bass.ds(b * QT, QT), :]).then_inc(s_out.sem, 16)
            sp.wait_ge(s_out.sem, s_out.at(B - 1, 0))


class Banks:

    def __init__(self, psum):
        self.psum = psum

    def __getitem__(self, i):
        if isinstance(i, slice):
            return [self.psum[:, k, :] for k in range(*i.indices(8))]
        return self.psum[:, i, :]

    def pair(self, i):
        return self.psum[:, i:i + 2, :]


def build(nc, t, out):
    w = lambda n: t["L1_xattn_" + n]
    with ExitStack() as ctx:
        psum = ctx.enter_context(nc.psum_tensor("banks", [P, 8, 512], F32))
        banks = Banks(psum)
        keep = lambda n, s, d=F32: ctx.enter_context(nc.sbuf_tensor(n, s, d))
        x = keep("x", [P, B * QT, D])
        ident = keep("ident", [P, P])
        ctx_t = keep("ctx_t", [CTX, B, SK])
        bias = {n: keep(n, [P, D]) for n in ("bo1", "bo2")}
        gains = {n: keep(n, [P, 2]) for n in ("g1", "be1", "g2", "be2", "g3", "be3")}
        b_1 = keep("b_1", [P, 2 * NF])
        wa, wb, wc = (Split(ctx, nc, f"w{c}_") for c in "abc")
        raw = Raw(ctx, nc, "raw_")
        w_o1, w_o2 = keep("w_o1", [P, NPAIR, D]), keep("w_o2", [P, NPAIR, D])
        w_k2, w_v2 = keep("w_k2", [CTX, INNER]), keep("w_v2", [CTX, INNER])

        pairs = lambda ap: ap.rearrange("(j p) d -> p j d", p=P)
        later = [(b_1[:, m:m + 1], w("b_ff1")[m * P:(m + 1) * P].unsqueeze(1)) for m in range(2 * NF)]
        later += [(to[:], w(name).unsqueeze(0).broadcast_to([P, D])) for name, to in bias.items()]
        for name, to in gains.items():
            later += [(to[:, 0:1], w(name)[0:P].unsqueeze(1)), (to[0:DT, 1:2], w(name)[P:D].unsqueeze(1))]
        later += [(w_o1[:], pairs(w("wo1"))), (w_o2[:], pairs(w("wo2"))), (w_k2[:], w("wk2")), (w_v2[:], w("wv2"))]

        store = NormStore(ctx, nc, x)
        ln1, ln2, ln3 = (Norm(store, i, gains[f"g{i + 1}"], gains[f"be{i + 1}"]) for i in range(3))

        adapter(nc, t, x, ident, ctx_t, banks, [(w("wq1"), wa), (w("wk1"), wb), (w("wv1"), wc)], later, ln1)
        selfattn(nc, x, ident, ln1, ln2, wa, wb, wc, w_o1, bias["bo1"], banks, w("wq2"), raw)
        w_2, b_2 = keep("w_2", [P, NF, D]), keep("b_2", [P, D])
        crossattn(nc, x, ident, ln2, ln3, ctx_t, wa, w_k2, w_v2, w_o2, bias["bo2"], banks, w("w_ff1"), wb, raw,
                  [(w_2[:], pairs(w("w_ff2"))), (b_2[:], w("b_ff2").unsqueeze(0).broadcast_to([P, D]))])
        feedfwd(nc, x, ident, ln3, wb, b_1, w_2, b_2, banks, out)


def kernel(**inputs):
    import concourse.bacc as bacc
    from concourse.bass_utils import run_bass_kernel_spmd

    nc = bacc.Bacc("TRN2", target_bir_lowering=False, num_devices=1)
    arrays = {"in_" + n: np.ascontiguousarray(a) for n, a in inputs.items()}
    arrays["in_ident"] = np.eye(P, dtype=np.float32)
    repeated = np.linspace(0, CTX - 1, S).astype(np.int64)
    arrays["in_expand"] = (np.arange(CTX)[:, None] == repeated[None, :]).astype(np.float32)
    arrays["in_own"] = (np.arange(H0 * NCA)[:, None] // NCA == np.arange(H0 * HP)[None, :] // HP).astype(np.float32)
    t = {n[3:]: nc.dram_tensor(n, a.shape, F32, kind="ExternalInput").ap() for n, a in arrays.items()}
    out = nc.dram_tensor("out", (B, S, D), F32, kind="ExternalOutput").ap()
    build(nc, t, out)
    r = run_bass_kernel_spmd(nc, [arrays], core_ids=[0])
    return r.results[0]["out"]
```
